# Optimizing a Trainium2 kernel written in Bass

```python
import numpy as np
import jax
import jax.numpy as jnp

def _softmax(x, axis=-1):
    return jax.nn.softmax(x, axis=axis)

def _gelu(x):
    return jax.nn.gelu(x, approximate=True)

def _silu(x):
    return jax.nn.silu(x)

def _sigmoid(x):
    return jax.nn.sigmoid(x)

def _layernorm(x, axis=-1, eps=1e-05):
    m = jnp.mean(x, axis=axis, keepdims=True)
    v = jnp.var(x, axis=axis, keepdims=True)
    return (x - m) / jnp.sqrt(v + eps)

def _scatter_add(tgt, idx, src, axis=0):
    return tgt.at[idx].add(src)

def _segment_sum(src, seg, n):
    return jax.ops.segment_sum(src, seg, n)
kernel_name = 'mk_xattn_ffn_d1_seqx_r4_8020da'

def setup_inputs(seed: int=0):
    np.random.seed(seed)
    _w = jnp.asarray

    def _rec_inputs():
        import jax
        import jax.numpy as jnp
        _rk = jax.random.key(seed)
        x = -0.0002928 + 1 * jax.random.normal(jax.random.fold_in(_rk, 1), (2, 1024, 256), jnp.float32)
        _lenS = 1024 - jax.random.randint(jax.random.fold_in(_rk, 7), (2,), 0, max(1, 1024 // 4) + 1, jnp.int32)
        _lenS2 = 154 - jax.random.randint(jax.random.fold_in(_rk, 8), (2,), 0, max(1, 154 // 4) + 1, jnp.int32)
        _ctx_1024P = jax.random.normal(jax.random.fold_in(_rk, 11), (2, 16, 256), jnp.float32)
        _ctx_1024c = jax.random.dirichlet(jax.random.fold_in(_rk, 511), 0.3 * jnp.ones((16,), jnp.float32), (2, 154))
        _ctx_1024t = jnp.einsum('bsk,bkd->bsd', _ctx_1024c, _ctx_1024P)
        _ctx_1024t = _ctx_1024t * jax.lax.rsqrt(jnp.mean(jnp.square(_ctx_1024t)) + 1e-12) * 0.953939
        ctx_1024 = -1.39393e-06 + 0.999914 * (_ctx_1024t + 0.3 * jax.random.normal(jax.random.fold_in(_rk, 611), (2, 154, 256), jnp.float32))
        _validS = jnp.arange(1024)[None, :] < _lenS[:, None]
        _validS2 = jnp.arange(154)[None, :] < _lenS2[:, None]
        _causal = jnp.tril(jnp.ones((1024, 1024), dtype=bool))
        mask_1x1xSxS2_bk1 = jnp.broadcast_to(_validS2[0:1, None, None, :], (1, 1, 1024, 154))
        return (x, ctx_1024, mask_1x1xSxS2_bk1)
    x, ctx_1024, mask_1x1xSxS2_bk1 = _rec_inputs()

    def _L0_xattn_setup():
        import jax, jax.numpy as jnp
        import numpy as np
        import math
        B, S, D_EMB = (2, 512, 256)
        H, D_HEAD, D_OUT = (16, 64, 256)
        D_MID = H * D_HEAD
        NEG = jnp.float32(-1e+30)
        key = jax.random.key(seed)
        ks = jax.random.split(key, 11)
        sc = 0.02
        inp = {'x_q': jax.random.normal(ks[0], (B, S, D_EMB), jnp.float32), 'x_k': jax.random.normal(ks[1], (B, S, D_EMB), jnp.float32), 'x_v': jax.random.normal(ks[2], (B, S, D_EMB), jnp.float32), 'mask_mat': jnp.triu(jnp.ones((S, S), jnp.bool_), k=1)[None, None], 'Wq': jax.random.normal(ks[3], (D_EMB, D_MID), jnp.float32) * sc, 'bq': jnp.zeros((D_MID,), jnp.float32), 'Wk': jax.random.normal(ks[4], (D_EMB, D_MID), jnp.float32) * sc, 'bk': jnp.zeros((D_MID,), jnp.float32), 'Wv': jax.random.normal(ks[5], (D_EMB, D_MID), jnp.float32) * sc, 'bv': jnp.zeros((D_MID,), jnp.float32), 'Wo': jax.random.normal(ks[6], (D_MID, D_OUT), jnp.float32) * sc, 'bo': jnp.zeros((D_OUT,), jnp.float32)}
        return inp
    _L0_xattn_all = _L0_xattn_setup()
    _L0_xattn_in = {k: v for k, v in _L0_xattn_all.items() if k in ('Wq', 'bq', 'Wk', 'bk', 'Wv', 'bv', 'Wo', 'bo')}
    del _L0_xattn_all

    def _L0_ffn_setup():
        import jax, jax.numpy as jnp
        import numpy as np
        B, N, D = (4, 1024, 256)
        E, S, F = (16, 64, 512)
        DO = 256
        EPS = 1e-05

        def _layernorm(x, g, b):
            mu = jnp.mean(x, axis=-1, keepdims=True)
            var = jnp.mean(jnp.square(x - mu), axis=-1, keepdims=True)
            return (x - mu) * jax.lax.rsqrt(var + EPS) * g + b
        key = jax.random.key(seed)
        ks = jax.random.split(key, 8)
        d = {'x': jax.random.normal(ks[0], (B, N, D), dtype=jnp.float32), 'norm_g': jnp.ones((D,), jnp.float32), 'norm_b': jnp.zeros((D,), jnp.float32), 'slot_g': jnp.ones((D,), jnp.float32), 'slot_b': jnp.zeros((D,), jnp.float32), 'scale': jnp.ones((1,), jnp.float32), 'slot_embeds': jax.random.normal(ks[1], (E, S, D), jnp.float32) / np.sqrt(D), 'Wg': jax.random.normal(ks[2], (E, D, F), jnp.float32) * np.sqrt(2.0 / (D + F)), 'bg': jnp.zeros((E, F), jnp.float32), 'Wu': jax.random.normal(ks[3], (E, D, F), jnp.float32) * np.sqrt(2.0 / (D + F)), 'bu': jnp.zeros((E, F), jnp.float32), 'Wd': jax.random.normal(ks[4], (E, F, DO), jnp.float32) * np.sqrt(2.0 / (F + DO)), 'bd': jnp.zeros((E, DO), jnp.float32)}
        return d
    _L0_ffn_all = _L0_ffn_setup()
    _L0_ffn_in = {k: v for k, v in _L0_ffn_all.items() if k in ('norm_g', 'norm_b', 'slot_g', 'slot_b', 'scale', 'slot_embeds', 'Wg', 'bg', 'Wu', 'bu', 'Wd', 'bd')}
    del _L0_ffn_all
    return {'x': x, 'ctx_1024': ctx_1024, 'mask_1x1xSxS2_bk1': mask_1x1xSxS2_bk1, 'L0_xattn_Wq': _L0_xattn_in['Wq'], 'L0_xattn_bq': _L0_xattn_in['bq'], 'L0_xattn_Wk': _L0_xattn_in['Wk'], 'L0_xattn_bk': _L0_xattn_in['bk'], 'L0_xattn_Wv': _L0_xattn_in['Wv'], 'L0_xattn_bv': _L0_xattn_in['bv'], 'L0_xattn_Wo': _L0_xattn_in['Wo'], 'L0_xattn_bo': _L0_xattn_in['bo'], 'L0_ffn_norm_g': _L0_ffn_in['norm_g'], 'L0_ffn_norm_b': _L0_ffn_in['norm_b'], 'L0_ffn_slot_g': _L0_ffn_in['slot_g'], 'L0_ffn_slot_b': _L0_ffn_in['slot_b'], 'L0_ffn_scale': _L0_ffn_in['scale'], 'L0_ffn_slot_embeds': _L0_ffn_in['slot_embeds'], 'L0_ffn_Wg': _L0_ffn_in['Wg'], 'L0_ffn_bg': _L0_ffn_in['bg'], 'L0_ffn_Wu': _L0_ffn_in['Wu'], 'L0_ffn_bu': _L0_ffn_in['bu'], 'L0_ffn_Wd': _L0_ffn_in['Wd'], 'L0_ffn_bd': _L0_ffn_in['bd']}

def reference(x, ctx_1024, mask_1x1xSxS2_bk1, L0_xattn_Wq, L0_xattn_bq, L0_xattn_Wk, L0_xattn_bk, L0_xattn_Wv, L0_xattn_bv, L0_xattn_Wo, L0_xattn_bo, L0_ffn_norm_g, L0_ffn_norm_b, L0_ffn_slot_g, L0_ffn_slot_b, L0_ffn_scale, L0_ffn_slot_embeds, L0_ffn_Wg, L0_ffn_bg, L0_ffn_Wu, L0_ffn_bu, L0_ffn_Wd, L0_ffn_bd):
    import jax
    import jax.numpy as jnp

    def _L0_xattn_ref(x_q, x_k, x_v, mask_mat, Wq, bq, Wk, bk, Wv, bv, Wo, bo):
        import jax, jax.numpy as jnp
        import numpy as np
        import math
        B, S, D_EMB = (2, 512, 256)
        H, D_HEAD, D_OUT = (16, 64, 256)
        D_MID = H * D_HEAD
        NEG = jnp.float32(-1e+30)
        b, sq, _ = x_q.shape
        sk = x_k.shape[1]
        q = (x_q @ Wq + bq).reshape(b, sq, H, D_HEAD).transpose(0, 2, 1, 3)
        k = (x_k @ Wk + bk).reshape(b, sk, H, D_HEAD).transpose(0, 2, 1, 3)
        v = (x_v @ Wv + bv).reshape(b, sk, H, D_HEAD).transpose(0, 2, 1, 3)
        s0 = jnp.einsum('bhqd,bhkd->bhqk', q, k) / math.sqrt(D_HEAD)
        s0 = jnp.where(mask_mat, NEG, s0)
        p = jax.nn.softmax(s0, axis=-1)
        s1 = jnp.einsum('bhqk,bhkd->bhqd', p, v)
        s1 = s1.transpose(0, 2, 1, 3).reshape(b, sq, D_MID)
        return s1 @ Wo + bo

    def _L0_ffn_ref(x, norm_g, norm_b, slot_g, slot_b, scale, slot_embeds, Wg, bg, Wu, bu, Wd, bd):
        import jax, jax.numpy as jnp
        import numpy as np
        B, N, D = (4, 1024, 256)
        E, S, F = (16, 64, 512)
        DO = 256
        EPS = 1e-05

        def _layernorm(x, g, b):
            mu = jnp.mean(x, axis=-1, keepdims=True)
            var = jnp.mean(jnp.square(x - mu), axis=-1, keepdims=True)
            return (x - mu) * jax.lax.rsqrt(var + EPS) * g + b
        x = _layernorm(x, norm_g, norm_b)
        se = _layernorm(slot_embeds, slot_g, slot_b) * scale
        logits = jnp.einsum('bnd,esd->bnes', x, se)
        dispatch = jax.nn.softmax(logits, axis=1)
        combine = jax.nn.softmax(logits.reshape(x.shape[0], x.shape[1], -1), axis=-1)
        slots = jnp.einsum('bnd,bnes->besd', x, dispatch)
        gate = jax.nn.gelu(jnp.einsum('besd,edf->besf', slots, Wg) + bg[None, :, None, :], approximate=False)
        up = jnp.einsum('besd,edf->besf', slots, Wu) + bu[None, :, None, :]
        eout = jnp.einsum('besf,efo->beso', gate * up, Wd) + bd[None, :, None, :]
        eout = eout.reshape(eout.shape[0], -1, eout.shape[-1])
        return jnp.einsum('bns,bso->bno', combine, eout)
    x = x + _L0_xattn_ref(_layernorm(x, axis=-1), ctx_1024, ctx_1024, mask_1x1xSxS2_bk1, L0_xattn_Wq, L0_xattn_bq, L0_xattn_Wk, L0_xattn_bk, L0_xattn_Wv, L0_xattn_bv, L0_xattn_Wo, L0_xattn_bo)
    x = x + _L0_ffn_ref(_layernorm(x, axis=-1), L0_ffn_norm_g, L0_ffn_norm_b, L0_ffn_slot_g, L0_ffn_slot_b, L0_ffn_scale, L0_ffn_slot_embeds, L0_ffn_Wg, L0_ffn_bg, L0_ffn_Wu, L0_ffn_bu, L0_ffn_Wd, L0_ffn_bd)
    return x

_drawn_inputs = setup_inputs


def setup_inputs(seed=0):
    import zlib

    import numpy as np

    out = dict(_drawn_inputs(seed))
    spreads = {'L0_xattn_bq': (0.0, 0.8),
     'L0_xattn_bk': (0.0, 0.8),
     'L0_xattn_bv': (0.0, 0.1),
     'L0_xattn_bo': (0.0, 0.1),
     'L0_ffn_norm_g': (1.0, 0.2),
     'L0_ffn_norm_b': (0.0, 0.1),
     'L0_ffn_slot_g': (1.0, 0.2),
     'L0_ffn_slot_b': (0.0, 0.1),
     'L0_ffn_bg': (0.0, 0.1),
     'L0_ffn_bu': (0.0, 0.1),
     'L0_ffn_bd': (0.0, 0.1)}
    factors = {'L0_xattn_Wq': 6.072, 'L0_xattn_Wk': 5.753}
    for name, (base, spread) in spreads.items():
        noise = np.random.default_rng([zlib.crc32(name.encode()), seed]).standard_normal(out[name].shape)
        drawn = base * np.exp(spread * noise) if base else spread * noise
        out[name] = jnp.asarray(drawn.astype(out[name].dtype))
    for name, factor in factors.items():
        out[name] = (out[name] * factor).astype(out[name].dtype)
    return out
```

```python
from contextlib import ExitStack

import concourse.bass as bass
from concourse import mybir

P = 128
F32 = mybir.dt.float32
F32R = mybir.dt.float32r
BF16 = mybir.dt.bfloat16
U8 = mybir.dt.uint8
ALU = mybir.AluOpType
ACT = mybir.ActivationFunctionType
AX = mybir.AxisListType.X
EPS = 1e-5
MASKED = -1e30

PASSES = ((0, 0), (0, 1), (1, 0))


def attention_schedule(groups, quads):
    steps = groups * quads
    order = [("LN", 0), ("XN", 0), ("xT", 0, 0), ("xT", 0, 1), ("Q", 0, 0), ("Q", 0, 1)]
    for n in range(steps + 1):
        g, q = divmod(n, quads)
        now, nxt, before = n < steps, n + 1 < steps, n >= 1
        order += [("Q", n + 1, 0)] * nxt
        order += [("R", n - 1, 1)] * before
        order += [("S", n, 0, 0)] * now
        order += [("T", n - 1, 0)] * before
        order += [("S", n, 0, 1)] * now
        order += [("Q", n + 1, 1)] * nxt
        order += [("T", n - 1, 1)] * before
        order += [("R", n, 0)] * now
        order += [("S", n, 1, 0)] * now
        order += [("T", n - 1, 2), ("PV", n - 1, 0)] * before
        if q == 1 and g + 1 < groups:
            order += [("LN", g + 1)]
        order += [("S", n, 1, 1)] * now
        order += [("PV", n - 1, 1)] * before
        if q == 0 and g >= 1:
            order += [("Y", g - 1, 0), ("Y", g - 1, 1)]
        if q == 1 and g + 1 < groups:
            order += [("XN", g + 1)]
        if q == quads - 2 and g + 1 < groups and now:
            order += [("xT", g + 1, 0), ("xT", g + 1, 1)]
    return order


def program(nc, io):
    x, ctx, mask = io["x"], io["ctx_1024"], io["mask_1x1xSxS2_bk1"]
    Wq, bq, Wk, bk = (io["L0_xattn_" + n] for n in ("Wq", "bq", "Wk", "bk"))
    Wv, bv, Wo, bo = (io["L0_xattn_" + n] for n in ("Wv", "bv", "Wo", "bo"))
    norm_g, norm_b, slot_g, slot_b = (io["L0_ffn_" + n] for n in ("norm_g", "norm_b", "slot_g", "slot_b"))
    scale, slot_embeds = io["L0_ffn_scale"], io["L0_ffn_slot_embeds"]
    Wg, bg, Wu, bu, Wd, bd = (io["L0_ffn_" + n] for n in ("Wg", "bg", "Wu", "bu", "Wd", "bd"))
    out, logits_dram = io["out"], io["logits"]

    B, N, D = x.shape
    SK = ctx.shape[1]
    DM = Wq.shape[1]
    DH = 64
    E, SLOTS, _ = slot_embeds.shape
    F = Wg.shape[2]
    KD = D // P
    TILES = B * N // P
    TB = N // P
    GROUPS = TILES // 2
    PAIRS = DM // P
    QUADS = PAIRS // 2
    TAIL = SK - P
    PK = 2 * SK
    T4 = 4 * TAIL
    ES = E * SLOTS
    ST = ES // P
    FT = F // P
    DN = D + 2
    assert D == 2 * P and DM == 1024 and ES == 1024 and F == 512 and B == 2 and T4 <= P

    prologue = [("cT", k) for k in range(KD)] + [("K", p) for p in range(PAIRS)] \
        + [("V", b, c, t) for b in range(B) for c in range(2) for t in range(2)]
    attention = attention_schedule(GROUPS, QUADS)
    logits = [("seT", t) for t in range(ST)] + [("N2", 0), ("N2", 1), ("x2T", 0)]
    for i in range(TILES):
        logits += [("N2", i + 2)] * (i + 2 < TILES) + [("x2T", i + 1)] * (i + 1 < TILES) + [("L", i)]
    slots = []
    for b in range(B):
        slots += [("CM", b), ("D", b, 0)]
        for t in range(ST):
            slots += [("D", b, t + 1)] * (t + 1 < ST) + [("sT", b, t)]
    experts = [("GU", 0)]
    for e in range(E):
        experts += [("GU", e + 1)] * (e + 1 < E) + [("HT", e), ("EO", e)]
    pieces = [(e, w) for e in range(2) for w in range(3)]
    for kind, e in experts:
        if e + 2 < E and kind == "GU":
            pieces += [(e + 2, 0), (e + 2, 1)]
        elif e + 2 < E and kind == "EO":
            pieces += [(e + 2, 2)]
    piece_no = {piece: i for i, piece in enumerate(pieces)}
    combine = [("C", 0), ("CT", 0, 0), ("CT", 0, 1)]
    for i in range(TILES):
        combine += [("C", i + 1), ("CT", i + 1, 0), ("CT", i + 1, 1)] * (i + 1 < TILES) + [("CO", i)]

    acc_no, t_no, s_no, high_no = {}, {}, {}, {}
    for ev in prologue + attention + logits + slots + experts + combine:
        if ev[0] in ("cT", "K", "V", "xT", "Q", "PV", "Y", "seT", "x2T", "D", "sT", "HT", "EO", "CO"):
            acc_no[ev] = len(acc_no)
        if ev[0] == "T":
            t_no[ev] = len(t_no)
        if ev[0] == "S":
            s_no[ev] = len(s_no)
        if ev[0] in ("cT", "xT", "Q", "PV", "seT", "x2T", "sT", "HT", "EO"):
            high_no[ev] = len(high_no)

    top = ExitStack()
    top.enter_context(nc.allow_non_contiguous_dma(reason="three bias vectors, one value a partition"))

    def sb(stack, name, shape, dt=F32):
        return stack.enter_context(nc.sbuf_tensor(name, shape, dt))

    def halves(stack, name, shape):
        return [sb(stack, name + "_high", shape, F32R), sb(stack, name + "_low", shape, F32R)]

    def sem(name):
        return top.enter_context(nc.semaphore(name))

    ident = sb(top, "ident", [P, P])
    ident16 = sb(top, "ident16", [P, P], BF16)
    ones = sb(top, "ones", [P, P])
    ones_row = sb(top, "ones_row", [P, P], F32R)
    x1 = sb(top, "x1", [P, TILES, D])
    gain = sb(top, "gain", [P, D])
    shift = sb(top, "shift", [P, D])
    eps = sb(top, "eps", [P, 2])
    mhalf = sb(top, "mhalf", [P, ST])
    mv2 = sb(top, "mv2", [P, TILES, 2])
    rstd2 = sb(top, "rstd2", [P, TILES])
    neg_amax = sb(top, "neg_amax", [P, TILES])
    csum = sb(top, "csum", [P, TILES])
    crec = sb(top, "crec", [P, TILES])

    att = ExitStack()
    bo_b = sb(att, "bo_b", [P, D])
    bq_c = sb(att, "bq_c", [P, PAIRS])
    bk_c = sb(att, "bk_c", [P, PAIRS])
    bv_c = sb(att, "bv_c", [P, PAIRS])
    maskb = sb(att, "maskb", [P, TB, SK], BF16)
    wkq = halves(att, "wkq", [P, KD, DM])
    wvo = halves(att, "wvo", [P, 2 * DM])
    wv = [w[:, :].rearrange("p (k n) -> p k n", k=KD) for w in wvo]
    wo = [w[:, :].rearrange("p (k n) -> p k n", k=PAIRS) for w in wvo]
    kbd = halves(att, "kbd", [P, B, PAIRS, PK])
    vm = halves(att, "vm", [P, B, PAIRS, 3 * DH])
    vt = halves(att, "vt", [T4, B, QUADS, 4 * DH])
    xn = sb(att, "xn", [P, 2, D])
    bst = sb(att, "bst", [P, 2, 6])
    bmv = sb(att, "bmv", [P, 2, 2])
    rstd = sb(att, "rstd", [P, 2, 2])
    bst2 = sb(att, "bst2", [P, 6])
    norm2 = sb(att, "norm2", [P, 6, 2])
    nmax = sb(att, "nmax", [P, 2, 2])
    psums = sb(att, "psums", [P, 2, 2, 2])
    prec = sb(att, "prec", [P, 2, 2, 2])
    xT = halves(att, "xT", [P, KD, 2 * P])
    pro = ExitStack()
    wraw = sb(pro, "wraw", [P, 2, 2 * DM])
    mask_u8 = sb(pro, "mask_u8", [P, TB, SK], U8)
    ctx_main = sb(pro, "ctx_main", [P, B, D])
    ctx_tail = sb(pro, "ctx_tail", [TAIL, B, D])
    cT = halves(pro, "cT", [P, KD, B, SK])
    cT4 = halves(pro, "cT4", [P, KD, B, 4, TAIL])
    k_f = sb(pro, "k_f", [P, 2, B, SK])
    v_f = sb(pro, "v_f", [T4, 2, 4 * DH])
    quad_mask = sb(pro, "quad_mask", [T4, 4, DH])
    pro.close()
    loop = ExitStack()
    qT = halves(loop, "qT", [P, 2, 2, 2 * P])
    pT = halves(loop, "pT", [P, 2, 5, 2 * P])
    oT = halves(loop, "oT", [P, PAIRS, 2 * P])
    expo = sb(loop, "expo", [P, 2, 2, 2, SK])
    prob = sb(loop, "prob", [P, 2, 2, 4, P])
    prob_t = sb(loop, "prob_t", [P, 2, 2, 4, TAIL])
    loop.close()
    att.close()

    ffn = ExitStack()
    sT = halves(ffn, "sT", [P, KD, E, B, SLOTS])
    lg = ExitStack()
    lsb = sb(lg, "lsb", [P, TILES, ES])
    x2 = halves(lg, "x2", [P, TILES, DN])
    colmax = sb(lg, "colmax", [P, B, ES])
    den = sb(lg, "den", [P, 2])
    la = ExitStack()
    seT = halves(la, "seT", [P, KD, ES])
    se = sb(la, "se", [P, ST, D])
    sg_b = sb(la, "sg_b", [P, D])
    sb_b = sb(la, "sb_b", [P, D])
    sc_b = sb(la, "sc_b", [P, 1])
    sst = sb(la, "sst", [P, ST, 6])
    smv = sb(la, "smv", [P, ST, 2])
    srs = sb(la, "srs", [P, 2, ST])
    x2f = sb(la, "x2f", [P, 2, D])
    x2T = halves(la, "x2T", [P, 2, KD, P])
    la.close()
    lb = ExitStack()
    nb = sb(lb, "nb", [P, ST])
    nb_b = sb(lb, "nb_b", [P, ES])
    disp_f = sb(lb, "disp_f", [P, 2, TB, P])
    disp = halves(lb, "disp", [P, 2, TB, P])
    slot_f = sb(lb, "slot_f", [P, 2, D])
    lb.close()
    lg.close()
    ex = ExitStack()
    eo = halves(ex, "eo", [P, B, ST, D])
    lraw = sb(ex, "lraw", [P, 3, ES])
    outb = sb(ex, "outb", [P, 2, D])
    exw = ExitStack()
    RAW = 4
    w_raw = sb(exw, "w_raw", [P, RAW, 1024])
    w_gu = halves(exw, "w_gu", [P, 2, 2, KD, F])
    w_d = halves(exw, "w_d", [P, 2, FT, D])
    BW = 2 * F + D
    b_raw = sb(exw, "b_raw", [1, 2, BW])
    b_row = sb(exw, "b_row", [33, 4, BW], F32R)
    gate = sb(exw, "gate", [P, F])
    hid = sb(exw, "hid", [P, 2, F])
    hT = halves(exw, "hT", [P, 2, FT, P])
    exw.close()
    cb = ExitStack()
    comb = sb(cb, "comb", [P, 2, ES])
    combT = halves(cb, "combT", [P, 2, ST, P])
    cb.close()
    ex.close()
    ffn.close()

    ps = top.enter_context(nc.psum_tensor("ps", [P, 8, 512], F32))

    def acc(no):
        return ps[:, 4 + no % 4, :]

    d_ctx, d_bk, d_x, d_small, d_mask, d_gain, d_se = (sem(s) for s in (
        "d_ctx", "d_bk", "d_x", "d_small", "d_mask", "d_gain", "d_se"))
    d_w = [sem(f"d_w{i}") for i in range(4)]
    d_raw = [sem(f"d_raw{i}") for i in range(RAW)]
    d_bias = [sem(f"d_bias{i}") for i in range(2)]
    d_lst = sem("d_lst")
    d_lld = [sem(f"d_lld{i}") for i in range(3)]
    d_out = [sem(f"d_out{i}") for i in range(2)]
    const_pool, const_dve, mask_ready = sem("const_pool"), sem("const_dve"), sem("mask_ready")
    acc_full, acc_high, acc_free = sem("acc_full"), sem("acc_high"), sem("acc_free")
    split_high, split_low = sem("split_high"), sem("split_low")
    k_ready, k_high, k_low = sem("k_ready"), sem("k_high"), sem("k_low")
    v_ready, v_high, v_low = sem("v_ready"), sem("v_high"), sem("v_low")
    cT4_ready = sem("cT4_ready")
    var_ready, rstd_ready, xn_ready, xbo_ready = sem("var_ready"), sem("rstd_ready"), sem("xn_ready"), sem("xbo_ready")
    s_full, s_max, s_exp = sem("s_full"), sem("s_max"), sem("s_exp")
    recip_ready, norm_ready = sem("recip_ready"), sem("norm_ready")
    t_full, t_high, t_free = sem("t_full"), sem("t_high"), sem("t_free")
    mv2_ready, rstd2_ready = sem("mv2_ready"), sem("rstd2_ready")
    dve_step, pool_step = sem("dve_step"), sem("pool_step")
    se_var, se_rstd, se_ready = sem("se_var"), sem("se_rstd"), sem("se_ready")
    x2_centered, x2_ready, x2_high, x2_low = sem("x2_centered"), sem("x2_ready"), sem("x2_high"), sem("x2_low")
    l_full, l_ready, amax_ready, colmax_ready = sem("l_full"), sem("l_ready"), sem("amax_ready"), sem("colmax_ready")
    cm_full, cm_max, cm_diag, cm_bcast, cm_ready = (sem(s) for s in (
        "cm_full", "cm_max", "cm_diag", "cm_bcast", "cm_ready"))
    d_shift, d_exp, d_high, d_low, slot_ready = (sem(s) for s in (
        "d_shift", "d_exp", "d_high", "d_low", "slot_ready"))
    w_high, gu_low, down_low, b_high, b_low = (sem(s) for s in ("w_high", "gu_low", "down_low", "b_high", "b_low"))
    gu_full, gate_ready, hid_ready = sem("gu_full"), sem("gate_ready"), sem("hid_ready")
    c_ready, ct_full, ct_high, ct_low, out_ready = (sem(s) for s in (
        "c_ready", "ct_full", "ct_high", "ct_low", "out_ready"))

    ATT_END = acc_no[("Y", GROUPS - 1, 1)] + 1
    SLOTS_END = acc_no[("sT", B - 1, ST - 1)] + 1
    EXPERTS_END = acc_no[("EO", E - 1)] + 1

    def wait_used(eng, ev):
        eng.wait_ge(acc_free, acc_no[ev] + 1)

    def wait_done(eng, ev):
        eng.wait_ge(acc_full, acc_no[ev] + 1)

    def weight_piece(e, w):
        return [(w_gu[s][:, e % 2, w] if w < 2 else w_d[s][:, e % 2]) for s in range(2)]

    block = top.enter_context(nc.Block())

    @block.sync
    def _(sp):
        sp.dma_start(ctx_main[:], ctx[:, 0:P].rearrange("b p d -> p b d")).then_inc(d_ctx, 16)
        sp.dma_start(ctx_tail[:], ctx[:, P:SK].rearrange("b p d -> p b d")).then_inc(d_ctx, 16)
        weights = [w.rearrange("(k p) n -> p k n", p=P) for w in (Wk, Wv, Wq, Wo)]

        def load_weights(i):
            if i >= 2:
                sp.wait_ge(split_high, i - 1)
                sp.wait_ge(split_low, i - 1)
            k = weights[i].shape[1]
            sp.dma_start(wraw[:, i % 2].rearrange("p (k n) -> p k n", k=k), weights[i]).then_inc(d_w[i], 16)

        load_weights(0)
        sp.dma_start(bk_c[:], bk.rearrange("(m p) -> p m", p=P)).then_inc(d_bk, 16)
        x_t = x.rearrange("b (t p) d -> p (b t) d", p=P)
        sp.dma_start(x1[:, 0:2], x_t[:, 0:2]).then_inc(d_x, 16)
        load_weights(1)
        load_weights(2)
        sp.dma_start(bq_c[:], bq.rearrange("(m p) -> p m", p=P)).then_inc(d_small, 16)
        sp.dma_start(bv_c[:], bv.rearrange("(m p) -> p m", p=P)).then_inc(d_small, 16)
        sp.dma_start(bo_b[:], bo.unsqueeze(0).to_broadcast([P, D])).then_inc(d_small, 16)
        sp.dma_start(mask_u8[:], mask.rearrange("a b (t p) k -> p (a b t) k", p=P)).then_inc(d_mask, 16)
        sp.dma_start(x1[:, 2:TILES], x_t[:, 2:TILES]).then_inc(d_x, 16)
        load_weights(3)
        sp.dma_start(gain[:], norm_g.unsqueeze(0).to_broadcast([P, D])).then_inc(d_gain, 16)
        sp.dma_start(shift[:], norm_b.unsqueeze(0).to_broadcast([P, D])).then_inc(d_gain, 16)
        sp.wait_ge(acc_free, ATT_END)
        sp.dma_start(se[:], slot_embeds.rearrange("(t e) s d -> (e s) t d", e=P // SLOTS)).then_inc(d_se, 16)
        sp.dma_start(sg_b[:], slot_g.unsqueeze(0).to_broadcast([P, D])).then_inc(d_se, 16)
        sp.dma_start(sb_b[:], slot_b.unsqueeze(0).to_broadcast([P, D])).then_inc(d_se, 16)
        sp.dma_start(sc_b[:], scale.unsqueeze(0).to_broadcast([P, 1])).then_inc(d_se, 16)
        l_t = logits_dram.rearrange("(t p) s -> p t s", p=P)
        for i in range(TILES):
            sp.wait_ge(l_ready, i + 1)
            sp.dma_start(l_t[:, i], lsb[:, i]).then_inc(d_lst, 16)
        sp.wait_ge(acc_free, SLOTS_END)
        sp.wait_ge(d_lst, 16 * TILES)
        for i, (e, w) in enumerate(pieces):
            if w == 0:
                if e >= 2:
                    sp.wait_ge(b_low, e - 1)
                for bias, at in ((bg, 0), (bu, F), (bd, 2 * F)):
                    sp.dma_start(b_raw[:, e % 2, at:at + bias.shape[1]], bias[e:e + 1]).then_inc(d_bias[e % 2], 16)
            if i >= RAW:
                sp.wait_ge(w_high, i - RAW + 1)
                e0, w0 = pieces[i - RAW]
                if w0 < 2:
                    sp.wait_ge(gu_low, 2 * e0 + w0 + 1)
                else:
                    sp.wait_ge(down_low, e0 + 1)
            view = (Wg, Wu, Wd)[w][e].rearrange("(k p) n -> p k n", p=P)
            sp.dma_start(w_raw[:, i % RAW].rearrange("p (k n) -> p k n", k=view.shape[1]), view)\
                .then_inc(d_raw[i % RAW], 16)
        out_t = out.rearrange("b (t p) d -> p (b t) d", p=P)
        for i in range(TILES + 2):
            if i < TILES:
                if i >= 3:
                    sp.wait_ge(c_ready, i - 2)
                sp.dma_start(lraw[:, i % 3], l_t[:, i]).then_inc(d_lld[i % 3], 16)
            if i >= 2:
                sp.wait_ge(out_ready, i - 1)
                sp.dma_start(out_t[:, i - 2], outb[:, i % 2]).then_inc(d_out[i % 2], 16)
        for s in d_out:
            sp.wait_ge(s, 16 * TILES // 2)

    @block.gpsimd
    def _(pool):
        steps = [0]

        def link(ins):
            steps[0] += 1
            ins.then_inc(pool_step, 1)
            pool.wait_ge(pool_step, steps[0])

        link(pool.memset(ident[:], 0.0))
        link(pool.affine_select(out=ident[:], in_=ident[:], compare_op=ALU.not_equal, fill=1.0, base=0,
                                pattern=[[-1, P]], channel_multiplier=1))
        pool.tensor_copy(ident16[:], ident[:]).then_inc(const_pool, 1)
        link(pool.memset(quad_mask[:], 1.0))
        link(pool.affine_select(out=quad_mask[:], in_=quad_mask[:], compare_op=ALU.is_ge, fill=0.0, base=0,
                                pattern=[[-TAIL, 4], [0, DH]], channel_multiplier=1))
        pool.affine_select(out=quad_mask[:], in_=quad_mask[:], compare_op=ALU.is_ge, fill=0.0, base=TAIL - 1,
                           pattern=[[TAIL, 4], [0, DH]], channel_multiplier=-1).then_inc(const_pool, 1)
        pool.wait_ge(const_dve, 1)
        pool.wait_ge(d_small, 48)
        for ev in attention:
            if ev[0] == "LN":
                g = ev[1]
                pool.wait_ge(var_ready, g + 1)
                link(pool.tensor_tensor(rstd[:, 0], bmv[:, :, 1], eps[:], ALU.add))
                pool.tensor_tensor(rstd[:, 1], rstd[:, 0], mhalf[:, 0:2], ALU.pow).then_inc(rstd_ready, 1)
            elif ev[0] == "XN":
                g = ev[1]
                pool.wait_ge(xn_ready, g + 1)
                pool.tensor_tensor(x1[:, 2 * g:2 * g + 2], x1[:, 2 * g:2 * g + 2],
                                   bo_b[:].unsqueeze(1).to_broadcast([P, 2, D]), ALU.add).then_inc(xbo_ready, 1)
            elif ev[0] == "R":
                _, n, pp = ev
                pool.wait_ge(recip_ready, 2 * n + pp + 1)
                if n >= 2:
                    pool.wait_ge(t_full, 3 * (n - 2) + 3)
                heads = slice(2 * pp, 2 * pp + 2)
                pool.tensor_tensor(prob[:, n % 2, :, heads, :], expo[:, pp, :, :, 0:P],
                                   prec[:, pp].unsqueeze(3).to_broadcast([P, 2, 2, P]), ALU.mult)
                pool.tensor_tensor(prob_t[:, n % 2, :, heads, :], expo[:, pp, :, :, P:SK],
                                   prec[:, pp].unsqueeze(3).to_broadcast([P, 2, 2, TAIL]), ALU.mult)\
                    .then_inc(norm_ready, 1)
            elif ev[0] == "Y" and ev[2] == 1:
                g = ev[1]
                pool.wait_ge(mv2_ready, 2 * g + 2)
                v = mv2[:, 2 * g:2 * g + 2, 1]
                link(pool.tensor_tensor(norm2[:, 0], v, eps[:], ALU.add))
                link(pool.tensor_tensor(norm2[:, 1], norm2[:, 0], mhalf[:, 0:2], ALU.pow))
                link(pool.tensor_tensor(norm2[:, 2], v, norm2[:, 1], ALU.mult))
                link(pool.tensor_tensor(norm2[:, 3], norm2[:, 2], norm2[:, 1], ALU.mult))
                link(pool.tensor_tensor(norm2[:, 4], norm2[:, 3], eps[:], ALU.add))
                link(pool.tensor_tensor(norm2[:, 5], norm2[:, 4], mhalf[:, 0:2], ALU.pow))
                pool.tensor_tensor(rstd2[:, 2 * g:2 * g + 2], norm2[:, 5], norm2[:, 1], ALU.mult)\
                    .then_inc(rstd2_ready, 1)
        pool.wait_ge(acc_free, ATT_END)
        pool.wait_ge(d_gain, 32)
        pool.wait_ge(se_var, 1)
        link(pool.tensor_tensor(srs[:, 0], smv[:, :, 1], eps[:, 0:1].to_broadcast([P, ST]), ALU.add))
        pool.tensor_tensor(srs[:, 1], srs[:, 0], mhalf[:], ALU.pow).then_inc(se_rstd, 1)
        for ev in logits:
            if ev[0] == "N2":
                i = ev[1]
                pool.wait_ge(x2_centered, i + 1)
                link(pool.tensor_tensor(x2f[:, i % 2], x2f[:, i % 2], gain[:], ALU.mult))
                pool.tensor_tensor(x2f[:, i % 2], x2f[:, i % 2], shift[:], ALU.add).then_inc(x2_ready, 1)
            elif ev[0] == "x2T":
                i = ev[1]
                pool.wait_ge(x2_high, i + 1)
                pool.tensor_tensor(x2[1][:, i, 0:D], x2f[:, i % 2], x2[0][:, i, 0:D], ALU.subtract).then_inc(x2_low, 1)
        for ev in slots:
            if ev[0] == "D":
                _, b, t = ev
                n = b * ST + t
                pool.wait_ge(cm_ready, b + 1)
                if n >= 2:
                    pool.wait_ge(d_low, n - 1)
                pool.tensor_tensor(disp_f[:, n % 2], lsb[:, b * TB:(b + 1) * TB, t * P:(t + 1) * P],
                                   nb_b[:, t * P:(t + 1) * P].unsqueeze(1).to_broadcast([P, TB, P]), ALU.add)\
                    .then_inc(d_shift, 1)
        pool.wait_ge(acc_free, SLOTS_END)
        for e in range(E):
            i = piece_no[e, 2]
            pool.wait_ge(w_high, i + 1)
            high, low = weight_piece(e, 2)
            pool.tensor_tensor(low, w_raw[:, i % RAW].rearrange("p (k n) -> p k n", k=FT), high, ALU.subtract)\
                .then_inc(down_low, 1)

    @block.scalar
    def _(act):
        def high_half(ev, dst, src, bias=0.0):
            wait_done(act, ev)
            act.activation(dst, src, ACT.Identity, bias=bias).then_inc(acc_high, 1)

        def split_weights(i, dst):
            act.wait_ge(d_w[i], 16)
            act.copy(dst, wraw[:, i % 2]).then_inc(split_high, 1)

        split_weights(0, wkq[0][:].rearrange("p k n -> p (k n)"))
        act.wait_ge(d_bk, 16)
        for ev in prologue:
            no = acc_no[ev]
            if ev[0] == "cT":
                high_half(ev, cT[0][:, ev[1]], acc(no)[:, 0:B * SK].rearrange("p (b s) -> p b s", b=B))
                if ev[1] == KD - 1:
                    split_weights(1, wvo[0][:])
            elif ev[0] == "K":
                p = ev[1]
                act.wait_ge(k_ready, p + 1)
                act.copy(kbd[0][0:DH, :, p, 0:SK], k_f[0:DH, p % 2])
                act.copy(kbd[0][DH:P, :, p, SK:PK], k_f[DH:P, p % 2]).then_inc(k_high, 1)
            else:
                _, b, c, t = ev
                if t == 0:
                    wait_done(act, ev)
                    act.copy(vm[0][:, b, 4 * c:4 * c + 4, :].rearrange("p q (a d) -> p q a d", a=3)[:, :, 0:3:2],
                             acc(no).rearrange("p (q a d) -> p q a d", q=4, a=2)).then_inc(v_high, 1)
                else:
                    act.wait_ge(v_ready, b * 2 + c + 1)
                    act.copy(vt[0][:, b, 2 * c:2 * c + 2, :], v_f[:]).then_inc(v_high, 1)
        wait_done(act, ("K", PAIRS - 1))
        split_weights(2, wkq[0][:].rearrange("p k n -> p (k n)"))
        wait_done(act, prologue[-1])
        split_weights(3, wvo[0][:])
        act.wait_ge(split_low, 4)
        act.wait_ge(v_low, 2 * B)
        act.wait_ge(mask_ready, 1)
        act.wait_ge(d_small, 48)
        for ev in attention:
            no = acc_no.get(ev)
            if ev[0] == "xT":
                high_half(ev, xT[0][:, ev[2]], acc(no)[:, 0:2 * P])
            elif ev[0] == "Q":
                _, n, pp = ev
                p = 2 * (n % QUADS) + pp
                high_half(ev, qT[0][:, n % 2, pp], acc(no)[:, 0:2 * P], bq_c[:, p:p + 1])
            elif ev[0] == "S":
                _, n, pp, j = ev
                s = s_no[ev]
                act.wait_ge(s_max, s + 1)
                if n >= 1:
                    act.wait_ge(norm_ready, 2 * (n - 1) + pp + 1)
                for h in range(2):
                    ins = act.activation(expo[:, pp, j, h, :], ps[:, s % 2, h * SK:(h + 1) * SK], ACT.Exp,
                                         bias=nmax[:, s % 2, h:h + 1],
                                         accum_out=psums[:, pp, j, h:h + 1])
                ins.then_inc(s_exp, 1)
            elif ev[0] == "T":
                _, n, t = ev
                k = t_no[ev]
                act.wait_ge(t_full, k + 1)
                if n >= 2:
                    wait_done(act, ("PV", n - 2, 1))
                rows, tiles = (P, 2) if t < 2 else (T4, 1)
                act.copy(pT[0][0:rows, n % 2, 2 * t:2 * t + tiles],
                         ps[0:rows, 2 + k % 2, 0:tiles * 2 * P].rearrange("p (t n) -> p t n", t=tiles))\
                    .then_inc(t_high, 1)
            elif ev[0] == "PV":
                _, n, pp = ev
                p = 2 * (n % QUADS) + pp
                high_half(ev, oT[0][:, p], acc(no)[:, 0:2 * P], bv_c[:, p:p + 1])
        act.wait_ge(acc_free, ATT_END)
        for ev in logits:
            no = acc_no.get(ev)
            if ev[0] == "seT":
                t = ev[1]
                high_half(ev, seT[0][:, :, t * P:(t + 1) * P], acc(no)[:, 0:2 * P].rearrange("p (k s) -> p k s", k=KD))
            elif ev[0] == "x2T":
                i = ev[1]
                high_half(ev, x2T[0][:, i % 2], acc(no)[:, 0:2 * P].rearrange("p (k s) -> p k s", k=KD))
                act.copy(x2[0][:, i, 0:D], x2f[:, i % 2]).then_inc(x2_high, 1)
            elif ev[0] == "L":
                i = ev[1]
                act.wait_ge(l_full, i + 1)
                act.copy(lsb[:, i].rearrange("p (c n) -> p c n", c=2), ps[:, 2 * (i % 2):2 * (i % 2) + 2, :])\
                    .then_inc(l_ready, 1)
        for ev in slots:
            no = acc_no.get(ev)
            if ev[0] == "CM":
                b = ev[1]
                act.wait_ge(cm_bcast, b + 1)
                if b:
                    act.wait_ge(d_shift, b * ST)
                act.copy(nb_b[:].rearrange("p (c n) -> p c n", c=2), ps[:, 0:2, :]).then_inc(cm_ready, 1)
            elif ev[0] == "D":
                _, b, t = ev
                n = b * ST + t
                act.wait_ge(d_shift, n + 1)
                act.activation(disp_f[:, n % 2], disp_f[:, n % 2], ACT.Exp).then_inc(d_exp, 1)
                if n >= 2:
                    wait_done(act, ("D",) + divmod(n - 2, ST))
                act.wait_ge(d_exp, n + 1)
                act.copy(disp[0][:, n % 2], disp_f[:, n % 2]).then_inc(d_high, 1)
            elif ev[0] == "sT":
                _, b, t = ev
                wait_done(act, ev)
                for k in range(KD):
                    ins = act.copy(sT[0][:, k, 2 * t:2 * t + 2, b, :],
                                   acc(no)[:, k * P:(k + 1) * P].rearrange("p (e s) -> p e s", e=2))
                ins.then_inc(acc_high, 1)
        act.wait_ge(acc_free, SLOTS_END)
        act.wait_ge(d_lst, 16 * TILES)

        def weights_high(e, w):
            i = piece_no[e, w]
            act.wait_ge(d_raw[i % RAW], 16 * (i // RAW + 1))
            if e >= 2:
                act.wait_ge(gu_full, e - 1) if w < 2 else wait_done(act, ("EO", e - 2))
            act.copy(weight_piece(e, w)[0],
                     w_raw[:, i % RAW].rearrange("p (k n) -> p k n", k=KD if w < 2 else FT)).then_inc(w_high, 1)
            if w == 0:
                act.wait_ge(d_bias[e % 2], 48 * (e // 2 + 1))
                if e >= 4:
                    wait_done(act, ("EO", e - 4))
                act.copy(b_row[0:1, e % 4], b_raw[:, e % 2]).then_inc(b_high, 1)

        act.wait_ge(const_dve, 3)
        for e, w in pieces[:6]:
            weights_high(e, w)
        for ev in experts:
            no = acc_no.get(ev)
            if ev[0] == "GU":
                e = ev[1]
                act.wait_ge(gu_full, e + 1)
                if e >= 1:
                    act.wait_ge(hid_ready, e)
                act.activation(gate[:], ps[:, 2 * (e % 2), :], ACT.Gelu).then_inc(gate_ready, 1)
                if e + 2 < E:
                    weights_high(e + 2, 0)
                    weights_high(e + 2, 1)
            elif ev[0] == "HT":
                e = ev[1]
                high_half(ev, hT[0][:, e % 2].rearrange("p f s -> p (f s)"), acc(no))
            else:
                e = ev[1]
                wait_done(act, ev)
                for b in range(B):
                    ins = act.copy(eo[0][64 * (e % 2):64 * (e % 2) + 64, b, e // 2, :],
                                   acc(no)[64 * b:64 * b + 64, 0:D])
                ins.then_inc(acc_high, 1)
                if e + 2 < E:
                    weights_high(e + 2, 2)
        act.wait_ge(acc_free, EXPERTS_END)
        for ev in combine:
            if ev[0] == "C":
                i = ev[1]
                act.wait_ge(d_lld[i % 3], 16 * (i // 3 + 1))
                if i >= 2:
                    act.wait_ge(ct_full, 2 * (i - 1))
                act.activation(comb[:, i % 2], lraw[:, i % 3], ACT.Exp, bias=neg_amax[:, i:i + 1],
                               accum_out=csum[:, i:i + 1]).then_inc(c_ready, 1)
            elif ev[0] == "CT":
                _, i, c = ev
                k = 2 * i + c
                act.wait_ge(ct_full, k + 1)
                if i >= 2:
                    wait_done(act, ("CO", i - 2))
                act.copy(combT[0][:, i % 2, 4 * c:4 * c + 4].rearrange("p t n -> p (t n)"), ps[:, k % 4, :])\
                    .then_inc(ct_high, 1)

    @block.vector
    def _(dve):
        steps = [0]

        def link(ins):
            steps[0] += 1
            ins.then_inc(dve_step, 1)
            dve.wait_ge(dve_step, steps[0])

        def low_half(ev, dst, src, high, bias=None):
            dve.wait_ge(acc_high, high_no[ev] + 1)
            if bias is None:
                dve.tensor_tensor(dst, src, high, ALU.subtract).then_inc(acc_free, 1)
            else:
                dve.scalar_tensor_tensor(out=dst, in0=src, scalar=bias, in1=high, op0=ALU.add, op1=ALU.subtract)\
                    .then_inc(acc_free, 1)

        dve.memset(eps[:], EPS)
        dve.memset(mhalf[:], -0.5)
        dve.memset(ones[:], 1.0)
        dve.memset(kbd[0][:].bitcast(F32), 0.0)
        dve.memset(kbd[1][:].bitcast(F32), 0.0)
        dve.memset(vm[0][:].bitcast(F32), 0.0)
        link(dve.memset(vm[1][:].bitcast(F32), 0.0))
        dve.tensor_copy(ones_row[:], ones[:]).then_inc(const_dve, 1)

        def split_weights(i, high, low):
            dve.wait_ge(split_high, i + 1)
            dve.tensor_tensor(low, wraw[:, i % 2], high, ALU.subtract).then_inc(split_low, 1)

        flat = [w[:].rearrange("p k n -> p (k n)") for w in wkq]
        split_weights(0, flat[0], flat[1])
        dve.wait_ge(d_bk, 16)
        dve.wait_ge(const_pool, 2)
        for ev in prologue:
            no = acc_no[ev]
            if ev[0] == "cT":
                k = ev[1]
                low_half(ev, cT[1][:, k], acc(no)[:, 0:B * SK].rearrange("p (b s) -> p b s", b=B), cT[0][:, k])
                if k == KD - 1:
                    wait_used(dve, ev)
                    for s in range(2):
                        for kk in range(KD):
                            ins = dve.tensor_copy(cT4[s][:, kk],
                                                  cT[s][:, kk, :, P:SK].unsqueeze(2).to_broadcast([P, B, 4, TAIL]))
                    ins.then_inc(cT4_ready, 1)
                    split_weights(1, wvo[0][:], wvo[1][:])
            elif ev[0] == "K":
                p = ev[1]
                wait_done(dve, ev)
                if p >= 2:
                    dve.wait_ge(k_low, p - 1)
                dve.tensor_scalar(k_f[:, p % 2], acc(no)[:, 0:B * SK].rearrange("p (b s) -> p b s", b=B),
                                  bk_c[:, p:p + 1], DH ** -0.5, ALU.add, ALU.mult).then_inc(k_ready, 1)
                dve.wait_ge(k_high, p + 1)
                dve.tensor_tensor(kbd[1][0:DH, :, p, 0:SK], k_f[0:DH, p % 2], kbd[0][0:DH, :, p, 0:SK], ALU.subtract)\
                    .then_inc(acc_free, 1)
                dve.tensor_tensor(kbd[1][DH:P, :, p, SK:PK], k_f[DH:P, p % 2], kbd[0][DH:P, :, p, SK:PK], ALU.subtract)\
                    .then_inc(k_low, 1)
            else:
                _, b, c, t = ev
                m = 4 * b + 2 * c + t
                if t == 0:
                    src = acc(no).rearrange("p (q a d) -> p q a d", q=4, a=2)
                    view = [v[:, b, 4 * c:4 * c + 4, :].rearrange("p q (a d) -> p q a d", a=3)[:, :, 0:3:2] for v in vm]
                    dve.wait_ge(v_high, m + 1)
                    dve.tensor_tensor(view[1], src, view[0], ALU.subtract).then_inc(acc_free, 1)
                else:
                    wait_done(dve, ev)
                    if m >= 2:
                        dve.wait_ge(v_low, m // 2)
                    dve.tensor_tensor(v_f[:], acc(no)[0:T4, :].rearrange("p (q n) -> p q n", q=2),
                                      quad_mask[:].rearrange("p a d -> p (a d)").unsqueeze(1).to_broadcast([T4, 2, 4 * DH]),
                                      ALU.mult).then_inc(v_ready, 1)
                    dve.wait_ge(v_high, m + 1)
                    dve.tensor_tensor(vt[1][:, b, 2 * c:2 * c + 2, :], v_f[:], vt[0][:, b, 2 * c:2 * c + 2, :],
                                      ALU.subtract).then_inc(v_low, 1)
                    dve.wait_ge(v_low, m // 2 + 1)
                    dve.engine_nop().then_inc(acc_free, 1)
        dve.wait_ge(d_mask, 16)
        dve.tensor_scalar(maskb[:], mask_u8[:], MASKED, None, ALU.mult).then_inc(mask_ready, 1)
        split_weights(2, flat[0], flat[1])
        split_weights(3, wvo[0][:], wvo[1][:])
        dve.wait_ge(split_low, 4)
        dve.wait_ge(mask_ready, 1)
        dve.wait_ge(d_small, 48)
        for ev in attention:
            no = acc_no.get(ev)
            if ev[0] == "LN":
                g = ev[1]
                dve.wait_ge(d_x, 16 if g == 0 else 32)
                for j in range(2):
                    ins = dve.bn_stats(bst[:, j], x1[:, 2 * g + j])
                link(ins)
                for j in range(2):
                    ins = dve.bn_aggr(bmv[:, j], bst[:, j])
                ins.then_inc(var_ready, 1)
            elif ev[0] == "XN":
                g = ev[1]
                dve.wait_ge(rstd_ready, g + 1)
                dve.wait_ge(var_ready, g + 1)
                if g:
                    wait_done(dve, ("xT", g - 1, 1))
                for j in range(2):
                    ins = dve.tensor_scalar(xn[:, j], x1[:, 2 * g + j], bmv[:, j, 0:1], rstd[:, 1, j:j + 1],
                                            ALU.subtract, ALU.mult)
                ins.then_inc(xn_ready, 1)
            elif ev[0] == "xT":
                low_half(ev, xT[1][:, ev[2]], acc(no)[:, 0:2 * P], xT[0][:, ev[2]])
            elif ev[0] == "Q":
                _, n, pp = ev
                p = 2 * (n % QUADS) + pp
                low_half(ev, qT[1][:, n % 2, pp], acc(no)[:, 0:2 * P], qT[0][:, n % 2, pp], bq_c[:, p:p + 1])
            elif ev[0] == "S":
                s = s_no[ev]
                dve.wait_ge(s_full, s + 1)
                dve.tensor_reduce(nmax[:, s % 2], ps[:, s % 2, 0:PK].rearrange("p (h k) -> p h k", h=2), AX, ALU.max,
                                  negate=True).then_inc(s_max, 1)
            elif ev[0] == "R":
                _, n, pp = ev
                dve.wait_ge(s_exp, s_no[("S", n, pp, 1)] + 1)
                if n >= 1:
                    dve.wait_ge(norm_ready, 2 * (n - 1) + pp + 1)
                dve.reciprocal(prec[:, pp], psums[:, pp]).then_inc(recip_ready, 1)
            elif ev[0] == "T":
                _, n, t = ev
                k = t_no[ev]
                dve.wait_ge(t_high, k + 1)
                rows, tiles = (P, 2) if t < 2 else (T4, 1)
                dve.tensor_tensor(pT[1][0:rows, n % 2, 2 * t:2 * t + tiles],
                                  ps[0:rows, 2 + k % 2, 0:tiles * 2 * P].rearrange("p (t n) -> p t n", t=tiles),
                                  pT[0][0:rows, n % 2, 2 * t:2 * t + tiles], ALU.subtract).then_inc(t_free, 1)
            elif ev[0] == "PV":
                _, n, pp = ev
                p = 2 * (n % QUADS) + pp
                low_half(ev, oT[1][:, p], acc(no)[:, 0:2 * P], oT[0][:, p], bv_c[:, p:p + 1])
            elif ev[0] == "Y":
                _, g, j = ev
                i = 2 * g + j
                wait_done(dve, ev)
                dve.wait_ge(xbo_ready, g + 1)
                dve.tensor_tensor(x1[:, i], acc(no)[:, 0:D], x1[:, i], ALU.add).then_inc(acc_free, 1)
                wait_used(dve, ev)
                link(dve.bn_stats(bst2[:], x1[:, i]))
                dve.bn_aggr(mv2[:, i], bst2[:]).then_inc(mv2_ready, 1)
        dve.wait_ge(acc_free, ATT_END)
        dve.wait_ge(mv2_ready, TILES)
        dve.memset(x2[0][:, :, D:D + 1].bitcast(F32), 1.0)
        dve.memset(x2[0][:, :, D + 1:DN].bitcast(F32), 0.0)
        dve.memset(x2[1][:, :, D:DN].bitcast(F32), 0.0).then_inc(const_dve, 1)
        dve.wait_ge(d_se, 64)
        for t in range(ST):
            ins = dve.bn_stats(sst[:, t], se[:, t])
        link(ins)
        for t in range(ST):
            ins = dve.bn_aggr(smv[:, t], sst[:, t])
        ins.then_inc(se_var, 1)
        dve.wait_ge(se_rstd, 1)
        dve.wait_ge(se_var, 1)
        for t in range(ST):
            ins = dve.tensor_scalar(se[:, t], se[:, t], smv[:, t, 0:1], srs[:, 1, t:t + 1], ALU.subtract, ALU.mult)
        link(ins)
        link(dve.tensor_tensor(se[:], se[:], sg_b[:].unsqueeze(1).to_broadcast([P, ST, D]), ALU.mult))
        link(dve.tensor_tensor(se[:], se[:], sb_b[:].unsqueeze(1).to_broadcast([P, ST, D]), ALU.add))
        dve.tensor_scalar(se[:], se[:], sc_b[:, 0:1], None, ALU.mult).then_inc(se_ready, 1)
        for ev in logits:
            no = acc_no.get(ev)
            if ev[0] == "seT":
                t = ev[1]
                cols = slice(t * P, (t + 1) * P)
                low_half(ev, seT[1][:, :, cols], acc(no)[:, 0:2 * P].rearrange("p (k s) -> p k s", k=KD),
                         seT[0][:, :, cols])
            elif ev[0] == "N2":
                i = ev[1]
                dve.wait_ge(rstd2_ready, i // 2 + 1)
                if i >= 2:
                    wait_done(dve, ("x2T", i - 2))
                    dve.wait_ge(x2_high, i - 1)
                    dve.wait_ge(x2_low, i - 1)
                dve.tensor_scalar(x2f[:, i % 2], x1[:, i], mv2[:, i, 0:1], rstd2[:, i:i + 1],
                                  ALU.subtract, ALU.mult).then_inc(x2_centered, 1)
            elif ev[0] == "x2T":
                i = ev[1]
                low_half(ev, x2T[1][:, i % 2], acc(no)[:, 0:2 * P].rearrange("p (k s) -> p k s", k=KD), x2T[0][:, i % 2])
            elif ev[0] == "L":
                i = ev[1]
                dve.wait_ge(l_ready, i + 1)
                dve.tensor_reduce(neg_amax[:, i:i + 1], lsb[:, i], AX, ALU.max, negate=True).then_inc(amax_ready, 1)
                b = i // TB
                if i % TB:
                    dve.wait_ge(colmax_ready, i)
                first = lsb[:, i] if i % TB == 0 else colmax[:, b]
                dve.tensor_tensor(colmax[:, b], first, lsb[:, i], ALU.max).then_inc(colmax_ready, 1)
        for ev in slots:
            no = acc_no.get(ev)
            if ev[0] == "CM":
                b = ev[1]
                dve.wait_ge(cm_full, b + 1)
                link(dve.tensor_reduce(nb[:].rearrange("p (c t) -> p c t", c=2),
                                       ps[:, 2:4, :].rearrange("p c (t n) -> p c t n", t=4), AX, ALU.max, negate=True))
                dve.tensor_tensor(disp_f[:, 1], ident[:].unsqueeze(1).to_broadcast([P, ST, P]),
                                  nb[:].unsqueeze(2).to_broadcast([P, ST, P]), ALU.mult).then_inc(cm_diag, 1)
            elif ev[0] == "D":
                _, b, t = ev
                n = b * ST + t
                dve.wait_ge(d_high, n + 1)
                dve.tensor_tensor(disp[1][:, n % 2], disp_f[:, n % 2], disp[0][:, n % 2], ALU.subtract).then_inc(d_low, 1)
                wait_done(dve, ev)
                if n >= 2:
                    wait_done(dve, ("sT",) + divmod(n - 2, ST))
                link(dve.reciprocal(den[:, n % 2:n % 2 + 1], acc(no)[:, D:D + 1]))
                dve.tensor_scalar(slot_f[:, n % 2], acc(no)[:, 0:D], den[:, n % 2:n % 2 + 1], None, ALU.mult)\
                    .then_inc(acc_free, 1)
            elif ev[0] == "sT":
                _, b, t = ev
                dve.wait_ge(acc_high, high_no[ev] + 1)
                for k in range(KD):
                    at = (slice(None), k, slice(2 * t, 2 * t + 2), b)
                    ins = dve.tensor_tensor(sT[1][at], acc(no)[:, k * P:(k + 1) * P].rearrange("p (e s) -> p e s", e=2),
                                            sT[0][at], ALU.subtract)
                ins.then_inc(acc_free, 1)
        dve.wait_ge(acc_free, SLOTS_END)
        dve.wait_ge(d_lst, 16 * TILES)
        dve.memset(b_row[:].bitcast(F32), 0.0).then_inc(const_dve, 1)
        dve.wait_ge(const_dve, 3)

        def weights_low(e):
            for w in range(2):
                i = piece_no[e, w]
                high, low = weight_piece(e, w)
                dve.wait_ge(w_high, i + 1)
                dve.tensor_tensor(low, w_raw[:, i % RAW].rearrange("p (k n) -> p k n", k=KD), high, ALU.subtract)\
                    .then_inc(gu_low, 1)
            dve.wait_ge(b_high, e + 1)
            dve.tensor_tensor(b_row[32:33, e % 4], b_raw[:, e % 2], b_row[0:1, e % 4], ALU.subtract).then_inc(b_low, 1)

        weights_low(0)
        weights_low(1)
        for ev in experts:
            no = acc_no.get(ev)
            e = ev[1]
            if ev[0] == "GU":
                dve.wait_ge(gate_ready, e + 1)
                if e >= 2:
                    wait_done(dve, ("HT", e - 2))
                dve.tensor_tensor(hid[:, e % 2], ps[:, 2 * (e % 2) + 1, :], gate[:], ALU.mult)\
                    .then_inc(hid_ready, 1)
                if e + 2 < E:
                    weights_low(e + 2)
            elif ev[0] == "HT":
                low_half(ev, hT[1][:, e % 2].rearrange("p f s -> p (f s)"), acc(no),
                         hT[0][:, e % 2].rearrange("p f s -> p (f s)"))
            else:
                dve.wait_ge(acc_high, high_no[ev] + 1)
                for b in range(B):
                    at = (slice(64 * (e % 2), 64 * (e % 2) + 64), b, e // 2)
                    ins = dve.tensor_tensor(eo[1][at], acc(no)[64 * b:64 * b + 64, 0:D], eo[0][at], ALU.subtract)
                ins.then_inc(acc_free, 1)
        for ev in combine:
            if ev[0] == "C":
                i = ev[1]
                dve.wait_ge(c_ready, i + 1)
                dve.reciprocal(crec[:, i:i + 1], csum[:, i:i + 1]).then_inc(dve_step, 1)
                steps[0] += 1
            elif ev[0] == "CT":
                _, i, c = ev
                k = 2 * i + c
                dve.wait_ge(ct_high, k + 1)
                at = (slice(None), i % 2, slice(4 * c, 4 * c + 4))
                dve.tensor_tensor(combT[1][at].rearrange("p t n -> p (t n)"), ps[:, k % 4, :],
                                  combT[0][at].rearrange("p t n -> p (t n)"), ALU.subtract).then_inc(ct_low, 1)
            elif ev[0] == "CO":
                i = ev[1]
                no = acc_no[ev]
                wait_done(dve, ev)
                if i >= 2:
                    dve.wait_ge(d_out[i % 2], 16 * (i // 2))
                dve.wait_ge(dve_step, steps[0])
                dve.scalar_tensor_tensor(out=outb[:, i % 2], in0=acc(no)[:, 0:D], scalar=crec[:, i:i + 1],
                                         in1=x1[:, i], op0=ALU.mult, op1=ALU.add).then_inc(out_ready, 1)
                dve.wait_ge(out_ready, i + 1)
                dve.engine_nop().then_inc(acc_free, 1)

    @block.tensor
    def _(pe):
        def bank(ev):
            no = acc_no[ev]
            if no >= 4:
                pe.wait_ge(acc_free, no - 3)
            return acc(no)

        pe.wait_ge(const_pool, 2)
        pe.wait_ge(const_dve, 1)
        pe.wait_ge(d_ctx, 32)
        for ev in prologue:
            dst = bank(ev)
            if ev[0] == "cT":
                k = ev[1]
                for b in range(B):
                    pe.transpose(dst[:, b * SK:b * SK + P], ctx_main[:, b, k * P:(k + 1) * P], ident[:])
                    ins = pe.transpose(dst[:, b * SK + P:(b + 1) * SK], ctx_tail[:, b, k * P:(k + 1) * P],
                                       ident[0:TAIL, 0:TAIL])
            elif ev[0] == "K":
                p = ev[1]
                if p == 0:
                    pe.wait_ge(split_low, 1)
                    wait_used(pe, ("cT", KD - 1))
                for n, (s, m) in enumerate(PASSES):
                    for k in range(KD):
                        ins = pe.matmul(dst[:, 0:B * SK], wkq[s][:, k, p * P:(p + 1) * P],
                                        cT[m][:, k].rearrange("p b s -> p (b s)"),
                                        start=(n == 0 and k == 0), stop=(n == 2 and k == KD - 1))
            else:
                _, b, c, t = ev
                if (b, c, t) == (0, 0, 0):
                    pe.wait_ge(split_low, 2)
                    pe.wait_ge(cT4_ready, 1)
                rows = P if t == 0 else T4
                for n, (s, m) in enumerate(PASSES):
                    for k in range(KD):
                        lhs = cT[s][:, k, b, 0:P] if t == 0 else cT4[s][:, k, b].rearrange("p a t -> p (a t)")
                        ins = pe.matmul(dst[0:rows, :], lhs, wv[m][:, k, c * F:(c + 1) * F],
                                        start=(n == 0 and k == 0), stop=(n == 2 and k == KD - 1))
            ins.then_inc(acc_full, 1)

        for ev in attention:
            if ev[0] == "xT":
                _, g, k = ev
                dst = bank(ev)
                pe.wait_ge(xn_ready, g + 1)
                for j in range(2):
                    ins = pe.transpose(dst[:, j * P:(j + 1) * P], xn[:, j, k * P:(k + 1) * P], ident[:])
                ins.then_inc(acc_full, 1)
            elif ev[0] == "Q":
                _, n, pp = ev
                g, q = divmod(n, QUADS)
                p = 2 * q + pp
                dst = bank(ev)
                wait_used(pe, ("xT", g, 1))
                if n == 0:
                    pe.wait_ge(split_low, 3)
                for r, (s, m) in enumerate(PASSES):
                    for k in range(KD):
                        ins = pe.matmul(dst[:, 0:2 * P], wkq[s][:, k, p * P:(p + 1) * P], xT[m][:, k],
                                        start=(r == 0 and k == 0), stop=(r == 2 and k == KD - 1))
                ins.then_inc(acc_full, 1)
            elif ev[0] == "S":
                _, n, pp, j = ev
                g, q = divmod(n, QUADS)
                s_i, tile = s_no[ev], 2 * g + j
                b, p = tile // TB, 2 * q + pp
                if s_i == 0:
                    pe.wait_ge(mask_ready, 1)
                    pe.wait_ge(k_low, PAIRS)
                if s_i >= 2:
                    pe.wait_ge(s_exp, s_i - 1)
                wait_used(pe, ("Q", n, pp))
                dst = ps[:, s_i % 2, 0:PK]
                pe.matmul(dst.rearrange("p (h k) -> p h k", h=2), ident16[:],
                          maskb[:, tile % TB].unsqueeze(1).to_broadcast([P, 2, SK]), start=True, stop=False)
                for r, (s, m) in enumerate(PASSES):
                    ins = pe.matmul(dst, qT[s][:, n % 2, pp, j * P:(j + 1) * P], kbd[m][:, b, p],
                                    start=False, stop=(r == 2))
                ins.then_inc(s_full, 1)
            elif ev[0] == "T":
                _, n, t = ev
                k = t_no[ev]
                if k >= 2:
                    pe.wait_ge(t_free, k - 1)
                pe.wait_ge(norm_ready, 2 * n + 1 + (t > 0))
                for j in range(2):
                    if t < 2:
                        for h in range(2):
                            ins = pe.transpose(ps[:, 2 + k % 2, (2 * h + j) * P:(2 * h + j + 1) * P],
                                               prob[:, n % 2, j, 2 * t + h, 0:P], ident[:])
                    else:
                        ins = pe.transpose(ps[0:T4, 2 + k % 2, j * P:(j + 1) * P],
                                           prob_t[:, n % 2, j].rearrange("p h k -> p (h k)"), ident[:])
                ins.then_inc(t_full, 1)
            elif ev[0] == "PV":
                _, n, pp = ev
                g, q = divmod(n, QUADS)
                b, p = 2 * g // TB, 2 * q + pp
                dst = bank(ev)
                pe.wait_ge(t_free, t_no[("T", n, 2)] + 1)
                if n == 0:
                    pe.wait_ge(v_low, 2 * B)
                for r, (s, m) in enumerate(PASSES):
                    for h in range(2):
                        pe.matmul(dst[:, 0:2 * P], vm[s][:, b, p, h * DH:h * DH + P], pT[m][:, n % 2, 2 * pp + h],
                                  start=(r == 0 and h == 0), stop=False)
                    ins = pe.matmul(dst[:, 0:2 * P], vt[s][:, b, q, pp * P:(pp + 1) * P], pT[m][0:T4, n % 2, 4],
                                    start=False, stop=(r == 2))
                ins.then_inc(acc_full, 1)
            elif ev[0] == "Y":
                _, g, j = ev
                dst = bank(ev)
                for p in range(PAIRS):
                    if p >= PAIRS - 2:
                        wait_used(pe, ("PV", QUADS * g + QUADS - 1, p - PAIRS + 2))
                    if g == 0 and p == 0:
                        pe.wait_ge(split_low, 4)
                    for r, (s, m) in enumerate(PASSES):
                        ins = pe.matmul(dst[:, 0:D], oT[s][:, p, j * P:(j + 1) * P], wo[m][:, p],
                                        start=(p == 0 and r == 0), stop=(p == PAIRS - 1 and r == 2))
                ins.then_inc(acc_full, 1)

        pe.wait_ge(acc_free, ATT_END)
        for ev in logits:
            if ev[0] == "seT":
                t = ev[1]
                dst = bank(ev)
                pe.wait_ge(se_ready, 1)
                for k in range(KD):
                    ins = pe.transpose(dst[:, k * P:(k + 1) * P], se[:, t, k * P:(k + 1) * P], ident[:])
                ins.then_inc(acc_full, 1)
            elif ev[0] == "x2T":
                i = ev[1]
                dst = bank(ev)
                pe.wait_ge(x2_ready, i + 1)
                for k in range(KD):
                    ins = pe.transpose(dst[:, k * P:(k + 1) * P], x2f[:, i % 2, k * P:(k + 1) * P], ident[:])
                ins.then_inc(acc_full, 1)
            elif ev[0] == "L":
                i = ev[1]
                wait_used(pe, ("x2T", i))
                if i >= 2:
                    pe.wait_ge(l_ready, i - 1)
                for c in range(2):
                    for r, (s, m) in enumerate(PASSES):
                        for k in range(KD):
                            ins = pe.matmul(ps[:, 2 * (i % 2) + c, :], x2T[s][:, i % 2, k],
                                            seT[m][:, k, c * 512:(c + 1) * 512],
                                            start=(r == 0 and k == 0), stop=(r == 2 and k == KD - 1))
                ins.then_inc(l_full, 1)
        pe.wait_ge(l_ready, TILES)
        for ev in slots:
            if ev[0] == "CM":
                b = ev[1]
                pe.wait_ge(colmax_ready, TB * (b + 1))
                for t in range(ST):
                    ins = pe.transpose(ps[:, 2 + t // 4, t % 4 * P:(t % 4 + 1) * P], colmax[:, b, t * P:(t + 1) * P],
                                       ident[:])
                ins.then_inc(cm_full, 1)
                pe.wait_ge(cm_diag, b + 1)
                for t in range(ST):
                    ins = pe.matmul(ps[:, t // 4, t % 4 * P:(t % 4 + 1) * P], ones[:], disp_f[:, 1, t],
                                    start=True, stop=True)
                ins.then_inc(cm_bcast, 1)
            elif ev[0] == "D":
                _, b, t = ev
                n = b * ST + t
                dst = bank(ev)
                pe.wait_ge(d_low, n + 1)
                if n == 0:
                    pe.wait_ge(x2_low, TILES)
                    pe.wait_ge(const_dve, 2)
                for r, (s, m) in enumerate(PASSES):
                    for i in range(TB):
                        ins = pe.matmul(dst[:, 0:DN], disp[s][:, n % 2, i], x2[m][:, b * TB + i],
                                        start=(r == 0 and i == 0), stop=(r == 2 and i == TB - 1))
                ins.then_inc(acc_full, 1)
            else:
                _, b, t = ev
                n = b * ST + t
                dst = bank(ev)
                wait_used(pe, ("D", b, t))
                for k in range(KD):
                    ins = pe.transpose(dst[:, k * P:(k + 1) * P], slot_f[:, n % 2, k * P:(k + 1) * P], ident[:])
                ins.then_inc(acc_full, 1)
        pe.wait_ge(acc_free, SLOTS_END)
        for ev in experts:
            e = ev[1]
            if ev[0] == "GU":
                if e >= 2:
                    pe.wait_ge(hid_ready, e - 1)
                pe.wait_ge(b_low, e + 1)
                pe.wait_ge(gu_low, 2 * e + 2)
                for w in range(2):
                    dst = ps[:, 2 * (e % 2) + w, :]
                    pe.matmul(dst, ones_row[0:33, :], b_row[:, e % 4, w * F:(w + 1) * F], start=True, stop=False)
                    for r, (s, m) in enumerate(PASSES):
                        for k in range(KD):
                            ins = pe.matmul(dst, sT[s][:, k, e].rearrange("p b s -> p (b s)"), w_gu[m][:, e % 2, w, k],
                                            start=False, stop=(r == 2 and k == KD - 1))
                ins.then_inc(gu_full, 1)
            elif ev[0] == "HT":
                dst = bank(ev)
                pe.wait_ge(hid_ready, e + 1)
                for f in range(FT):
                    ins = pe.transpose(dst[:, f * P:(f + 1) * P], hid[:, e % 2, f * P:(f + 1) * P], ident[:])
                ins.then_inc(acc_full, 1)
            else:
                dst = bank(ev)
                wait_used(pe, ("HT", e))
                pe.wait_ge(down_low, e + 1)
                pe.matmul(dst[:, 0:D], ones_row[0:33, :], b_row[:, e % 4, 2 * F:BW], start=True, stop=False)
                for r, (s, m) in enumerate(PASSES):
                    for f in range(FT):
                        ins = pe.matmul(dst[:, 0:D], hT[s][:, e % 2, f], w_d[m][:, e % 2, f],
                                        start=False, stop=(r == 2 and f == FT - 1))
                ins.then_inc(acc_full, 1)
        for ev in combine:
            if ev[0] == "CT":
                _, i, c = ev
                k = 2 * i + c
                pe.wait_ge(c_ready, i + 1)
                if k >= 4:
                    pe.wait_ge(ct_low, k - 3)
                else:
                    pe.wait_ge(hid_ready, E)
                for t in range(4):
                    ins = pe.transpose(ps[:, k % 4, t * P:(t + 1) * P], comb[:, i % 2, (4 * c + t) * P:(4 * c + t + 1) * P],
                                       ident[:])
                ins.then_inc(ct_full, 1)
            elif ev[0] == "CO":
                i = ev[1]
                b = i // TB
                dst = bank(ev)
                pe.wait_ge(ct_low, 2 * i + 2)
                wait_used(pe, ("EO", E - 1))
                for r, (s, m) in enumerate(PASSES):
                    for t in range(ST):
                        ins = pe.matmul(dst[:, 0:D], combT[s][:, i % 2, t], eo[m][:, b, t],
                                        start=(r == 0 and t == 0), stop=(r == 2 and t == ST - 1))
                ins.then_inc(acc_full, 1)

    top.close()


_INS = ['x', 'ctx_1024', 'mask_1x1xSxS2_bk1', 'L0_xattn_Wq', 'L0_xattn_bq', 'L0_xattn_Wk', 'L0_xattn_bk',
        'L0_xattn_Wv', 'L0_xattn_bv', 'L0_xattn_Wo', 'L0_xattn_bo', 'L0_ffn_norm_g', 'L0_ffn_norm_b',
        'L0_ffn_slot_g', 'L0_ffn_slot_b', 'L0_ffn_scale', 'L0_ffn_slot_embeds', 'L0_ffn_Wg', 'L0_ffn_bg',
        'L0_ffn_Wu', 'L0_ffn_bu', 'L0_ffn_Wd', 'L0_ffn_bd']


def kernel(**inputs):
    import numpy as _np
    import concourse.bacc as _bacc
    from concourse import mybir as _mybir
    from concourse.bass_utils import run_bass_kernel_spmd as _run

    nc = _bacc.Bacc("TRN2", target_bir_lowering=False, num_devices=1)
    arrays, io = {}, {}
    for name in _INS:
        a = _np.ascontiguousarray(inputs[name])
        arrays[f"in_{name}_dram"] = a
        io[name] = nc.dram_tensor(f"in_{name}_dram", a.shape, _mybir.dt.from_np(a.dtype), kind="ExternalInput").ap()
    shape = inputs["x"].shape
    slots = inputs["L0_ffn_slot_embeds"].shape
    io["out"] = nc.dram_tensor("out_0_dram", shape, _mybir.dt.float32, kind="ExternalOutput").ap()
    io["logits"] = nc.dram_tensor("logits_dram", (shape[0] * shape[1], slots[0] * slots[1]),
                                  _mybir.dt.float32, kind="Internal").ap()
    program(nc, io)
    r = _run(nc, [arrays], core_ids=[0])
    return r.results[0]["out_0_dram"]
```

```python
from contextlib import ExitStack

import concourse.bass as bass
from concourse import mybir

P = 128
F32 = mybir.dt.float32
F32R = mybir.dt.float32r
BF16 = mybir.dt.bfloat16
U8 = mybir.dt.uint8
ALU = mybir.AluOpType
ACT = mybir.ActivationFunctionType
AX = mybir.AxisListType.X
EPS = 1e-5
MASKED = -1e30
STORE_LAG = 3
LATER_DVE = {"R": 3.5, "T": 0.5}
LATER_ACT = {"S": 2.5, "Q": 0.5}
STEP = "R1 LN S00 PV0 S01 T0 Q0 R0 PV1 Q1 S10 T1 T2 Y0 XN Y1 S11 xT0 xT1"

PASSES = ((0, 0), (0, 1), (1, 0))


def attention_schedule(groups, quads):
    steps = groups * quads
    order = [("LN", 0), ("XN", 0), ("xT", 0, 0), ("xT", 0, 1), ("Q", 0, 0), ("Q", 0, 1)]
    for n in range(steps + 2):
        g, q = divmod(n, quads)
        now, nxt, last, before = n < steps, n + 1 < steps, 1 <= n <= steps, n >= 2
        norm, result = q == 1 and g + 1 < groups, q == 1 and g >= 1
        parts = {"Q0": [("Q", n + 1, 0)] * nxt, "Q1": [("Q", n + 1, 1)] * nxt,
                 "S00": [("S", n, 0, 0)] * now, "S01": [("S", n, 0, 1)] * now,
                 "S10": [("S", n, 1, 0)] * now, "S11": [("S", n, 1, 1)] * now,
                 "R0": [("R", n, 0)] * now, "R1": [("R", n - 1, 1)] * last,
                 "T0": [("T", n - 1, 0)] * last, "T1": [("T", n - 1, 1)] * last, "T2": [("T", n - 1, 2)] * last,
                 "PV0": [("PV", n - 2, 0)] * before, "PV1": [("PV", n - 2, 1)] * before,
                 "LN": [("LN", g + 1)] * norm, "XN": [("XN", g + 1)] * norm,
                 "Y0": [("Y", g - 1, 0)] * result, "Y1": [("Y", g - 1, 1)] * result,
                 "xT0": [("xT", g + 1, 0)] * (q == quads - 2 and g + 1 < groups and now),
                 "xT1": [("xT", g + 1, 1)] * (q == quads - 2 and g + 1 < groups and now)}
        for part in STEP.split():
            order += parts[part]
    return order


def later(order, by):
    at = [i + by.get(ev[0], 0) for i, ev in enumerate(order)]
    return [order[i] for i in sorted(range(len(order)), key=lambda i: (at[i], i))]


def program(nc, io):
    x, ctx, mask = io["x"], io["ctx_1024"], io["mask_1x1xSxS2_bk1"]
    Wq, bq, Wk, bk = (io["L0_xattn_" + n] for n in ("Wq", "bq", "Wk", "bk"))
    Wv, bv, Wo, bo = (io["L0_xattn_" + n] for n in ("Wv", "bv", "Wo", "bo"))
    norm_g, norm_b, slot_g, slot_b = (io["L0_ffn_" + n] for n in ("norm_g", "norm_b", "slot_g", "slot_b"))
    scale, slot_embeds = io["L0_ffn_scale"], io["L0_ffn_slot_embeds"]
    Wg, bg, Wu, bu, Wd, bd = (io["L0_ffn_" + n] for n in ("Wg", "bg", "Wu", "bu", "Wd", "bd"))
    out, logits_dram = io["out"], io["logits"]

    B, N, D = x.shape
    SK = ctx.shape[1]
    DM = Wq.shape[1]
    DH = 64
    E, SLOTS, _ = slot_embeds.shape
    F = Wg.shape[2]
    KD = D // P
    TILES = B * N // P
    TB = N // P
    GROUPS = TILES // 2
    PAIRS = DM // P
    QUADS = PAIRS // 2
    TAIL = SK - P
    PK = 2 * SK
    T4 = 4 * TAIL
    ES = E * SLOTS
    ST = ES // P
    FT = F // P
    DN = D + 2
    assert D == 2 * P and DM == 1024 and ES == 1024 and F == 512 and B == 2 and T4 <= P

    prologue = [("cT", k) for k in range(KD)] + [("K", p) for p in range(PAIRS)] \
        + [("V", b, c, t) for b in range(B) for c in range(2) for t in range(2)]
    attention = attention_schedule(GROUPS, QUADS)
    attention_dve = later(attention, LATER_DVE)
    attention_act = later(attention, LATER_ACT)
    logits = [("seT", t) for t in range(ST)] + [("N2", 0), ("N2", 1), ("N2", 2), ("x2T", 0)]
    for i in range(TILES):
        logits += [("x2T", i + 1)] * (i + 1 < TILES) + [("N2", i + 3)] * (i + 3 < TILES) + [("L", i)]
    slots = [("CM", b) for b in range(B)] + [("E", 0), ("E", 1), ("D", 0)]
    for n in range(B * ST):
        slots += [("E", n + 2)] * (n + 2 < B * ST) + [("D", n + 1)] * (n + 1 < B * ST) + [("sT", n)]
    experts = [("GU", 0)]
    for e in range(E):
        experts += [("GU", e + 1)] * (e + 1 < E) + [("HT", e)] + [("EO", e - 1)] * (e >= 1)
    experts += [("EO", E - 1)]
    pieces = [(e, w) for e in range(2) for w in range(3)]
    for kind, e in experts:
        if e + 2 < E and kind == "GU":
            pieces += [(e + 2, 0), (e + 2, 1)]
        elif e + 2 < E and kind == "EO":
            pieces += [(e + 2, 2)]
    piece_no = {piece: i for i, piece in enumerate(pieces)}
    combine = [("C", 0), ("C", 1), ("CT", 0, 0), ("CT", 0, 1)]
    for i in range(TILES):
        combine += [("CT", i + 1, 0), ("CT", i + 1, 1)] * (i + 1 < TILES) + [("C", i + 2)] * (i + 2 < TILES)
        combine += [("CO", i)]

    acc_no, t_no, s_no, high_no = {}, {}, {}, {}
    for ev in prologue + attention + logits + slots + experts + combine:
        if ev[0] in ("cT", "K", "V", "xT", "Q", "PV", "Y", "seT", "x2T", "D", "sT", "HT", "EO", "CO"):
            acc_no[ev] = len(acc_no)
        if ev[0] == "T":
            t_no[ev] = len(t_no)
        if ev[0] == "S":
            s_no[ev] = len(s_no)
        if ev[0] in ("cT", "xT", "Q", "PV", "seT", "x2T", "sT", "HT"):
            high_no[ev] = len(high_no)

    top = ExitStack()
    top.enter_context(nc.allow_non_contiguous_dma(reason="three bias vectors, one value a partition"))

    def sb(stack, name, shape, dt=F32):
        return stack.enter_context(nc.sbuf_tensor(name, shape, dt))

    def halves(stack, name, shape):
        return [sb(stack, name + "_high", shape, F32R), sb(stack, name + "_low", shape, F32R)]

    def sem(name):
        return top.enter_context(nc.semaphore(name))

    ident = sb(top, "ident", [P, P])
    ident16 = sb(top, "ident16", [P, P], BF16)
    ones = sb(top, "ones", [P, P])
    x1 = sb(top, "x1", [P, TILES, D])
    gain = sb(top, "gain", [P, D])
    shift = sb(top, "shift", [P, D])
    eps = sb(top, "eps", [P, 2])
    mhalf = sb(top, "mhalf", [P, ST])
    mv2 = sb(top, "mv2", [P, TILES, 2])
    rstd2 = sb(top, "rstd2", [P, TILES])
    neg_amax = sb(top, "neg_amax", [P, TILES])
    csum = sb(top, "csum", [P, TILES])
    crec = sb(top, "crec", [P, TILES])

    att = ExitStack()
    bo_b = sb(att, "bo_b", [P, D])
    bq_c = sb(att, "bq_c", [P, PAIRS])
    bk_c = sb(att, "bk_c", [P, PAIRS])
    bv_c = sb(att, "bv_c", [P, PAIRS])
    maskb = sb(att, "maskb", [P, TB, SK], BF16)
    wkq = halves(att, "wkq", [P, KD, DM])
    wvo = halves(att, "wvo", [P, 2 * DM])
    wv = [w[:, :].rearrange("p (k n) -> p k n", k=KD) for w in wvo]
    wo = [w[:, :].rearrange("p (k n) -> p k n", k=PAIRS) for w in wvo]
    kbd = halves(att, "kbd", [P, B, PAIRS, PK])
    vm = halves(att, "vm", [P, B, PAIRS, 3 * DH])
    vt = halves(att, "vt", [T4, B, QUADS, 4 * DH])
    xn = sb(att, "xn", [P, 2, D])
    bst = sb(att, "bst", [P, 2, 6])
    bmv = sb(att, "bmv", [P, 2, 2])
    rstd = sb(att, "rstd", [P, 2, 2])
    bst2 = sb(att, "bst2", [P, 6])
    norm2 = sb(att, "norm2", [P, 6, 2])
    nmax = sb(att, "nmax", [P, 2, 2])
    psums = sb(att, "psums", [P, 2, 2, 2])
    prec = sb(att, "prec", [P, 2, 2, 2])
    xT = halves(att, "xT", [P, KD, 2 * P])
    pro = ExitStack()
    wraw = sb(pro, "wraw", [P, 2, 2 * DM])
    mask_u8 = sb(pro, "mask_u8", [P, TB, SK], U8)
    ctx_main = sb(pro, "ctx_main", [P, B, D])
    ctx_tail = sb(pro, "ctx_tail", [TAIL, B, D])
    cT = halves(pro, "cT", [P, KD, B, SK])
    cT4 = halves(pro, "cT4", [P, KD, B, 4, TAIL])
    k_f = sb(pro, "k_f", [P, 2, B, SK])
    v_f = sb(pro, "v_f", [T4, 2, 4 * DH])
    quad_mask = sb(pro, "quad_mask", [T4, 4, DH])
    pro.close()
    loop = ExitStack()
    qT = halves(loop, "qT", [P, 2, 2, 2 * P])
    pT = halves(loop, "pT", [P, 2, 5, 2 * P])
    oT = halves(loop, "oT", [P, PAIRS, 2 * P])
    expo = sb(loop, "expo", [P, 2, 2, 2, SK])
    prob = sb(loop, "prob", [P, 2, 2, 4, P])
    prob_t = sb(loop, "prob_t", [P, 2, 2, 4, TAIL])
    loop.close()
    att.close()

    ffn = ExitStack()
    sT = halves(ffn, "sT", [P, KD, E, B, SLOTS])
    lg = ExitStack()
    lsb = sb(lg, "lsb", [P, TILES, ES])
    x2 = halves(lg, "x2", [P, TILES, DN])
    colmax = sb(lg, "colmax", [P, B, ES])
    den = sb(lg, "den", [P, 2])
    la = ExitStack()
    seT = halves(la, "seT", [P, KD, ES])
    se = sb(la, "se", [P, ST, D])
    sg_b = sb(la, "sg_b", [P, D])
    sb_b = sb(la, "sb_b", [P, D])
    sc_b = sb(la, "sc_b", [P, 1])
    sst = sb(la, "sst", [P, ST, 6])
    smv = sb(la, "smv", [P, ST, 2])
    srs = sb(la, "srs", [P, 2, ST])
    x2f = sb(la, "x2f", [P, 3, D])
    x2T = halves(la, "x2T", [P, 2, KD, P])
    la.close()
    lb = ExitStack()
    nb = sb(lb, "nb", [P, ST])
    nb_b = sb(lb, "nb_b", [P, B, ES])
    disp_f = sb(lb, "disp_f", [P, 2, TB, P])
    disp = halves(lb, "disp", [P, 3, TB, P])
    slot_f = sb(lb, "slot_f", [P, 2, D])
    lb.close()
    lg.close()
    ex = ExitStack()
    eo = halves(ex, "eo", [P, B, ST, D])
    lraw = sb(ex, "lraw", [P, 3, ES])
    outb = sb(ex, "outb", [P, 2, D])
    exw = ExitStack()
    RAW = 6
    w_raw = sb(exw, "w_raw", [P, RAW, 1024])
    w_gu = halves(exw, "w_gu", [P, 2, 2, KD, F])
    w_d = halves(exw, "w_d", [P, 2, FT, D])
    BW = 2 * F + D
    b_raw = sb(exw, "b_raw", [E, BW])
    b_row = sb(exw, "b_row", [32 + E, BW], F32R)
    b_pick = sb(exw, "b_pick", [32 + E, E, P], F32R)
    gate = sb(exw, "gate", [P, F])
    hid = sb(exw, "hid", [P, 2, F])
    hT = halves(exw, "hT", [P, 2, FT, P])
    exw.close()
    cb = ExitStack()
    comb = sb(cb, "comb", [P, 2, ES])
    combT = halves(cb, "combT", [P, 2, ST, P])
    cb.close()
    ex.close()
    ffn.close()

    ps = top.enter_context(nc.psum_tensor("ps", [P, 8, 512], F32))

    def acc(no):
        return ps[:, 4 + no % 4, :]

    d_ctx, d_bk, d_x, d_small, d_mask, d_gain, d_se = (sem(s) for s in (
        "d_ctx", "d_bk", "d_x", "d_small", "d_mask", "d_gain", "d_se"))
    d_w = [sem(f"d_w{i}") for i in range(4)]
    d_raw = [sem(f"d_raw{i}") for i in range(RAW)]
    d_bias = sem("d_bias")
    d_lst = sem("d_lst")
    d_lld = [sem(f"d_lld{i}") for i in range(3)]
    d_out = [sem(f"d_out{i}") for i in range(2)]
    const_pool, const_dve, mask_ready = sem("const_pool"), sem("const_dve"), sem("mask_ready")
    acc_full, acc_high, acc_free = sem("acc_full"), sem("acc_high"), sem("acc_free")
    split_high, split_low = sem("split_high"), sem("split_low")
    k_ready, k_high, k_low = sem("k_ready"), sem("k_high"), sem("k_low")
    v_ready, v_high, v_low = sem("v_ready"), sem("v_high"), sem("v_low")
    cT4_ready = sem("cT4_ready")
    var_ready, rstd_ready, xn_ready, xbo_ready = sem("var_ready"), sem("rstd_ready"), sem("xn_ready"), sem("xbo_ready")
    s_full, s_max, s_exp = sem("s_full"), sem("s_max"), sem("s_exp")
    recip_ready, norm_ready = sem("recip_ready"), sem("norm_ready")
    t_full, t_high, t_free = sem("t_full"), sem("t_high"), sem("t_free")
    mv2_ready, rstd2_ready = sem("mv2_ready"), sem("rstd2_ready")
    dve_step, pool_step = sem("dve_step"), sem("pool_step")
    se_var, se_rstd, se_ready = sem("se_var"), sem("se_rstd"), sem("se_ready")
    x2_centered, x2_ready, x2_high, x2_low = sem("x2_centered"), sem("x2_ready"), sem("x2_high"), sem("x2_low")
    l_full, l_ready, amax_ready, colmax_ready = sem("l_full"), sem("l_ready"), sem("amax_ready"), sem("colmax_ready")
    cm_full, cm_max, cm_diag, cm_bcast, cm_ready = (sem(s) for s in (
        "cm_full", "cm_max", "cm_diag", "cm_bcast", "cm_ready"))
    d_shift, d_exp, d_high, d_low, slot_ready = (sem(s) for s in (
        "d_shift", "d_exp", "d_high", "d_low", "slot_ready"))
    w_high, gate_low, up_low, down_low, b_high, b_low = (sem(s) for s in (
        "w_high", "gate_low", "up_low", "down_low", "b_high", "b_low"))
    gu_full, gate_ready, hid_ready = sem("gu_full"), sem("gate_ready"), sem("hid_ready")
    c_ready, ct_full, ct_high, ct_low, out_ready = (sem(s) for s in (
        "c_ready", "ct_full", "ct_high", "ct_low", "out_ready"))

    ATT_END = acc_no[("Y", GROUPS - 1, 1)] + 1
    SLOTS_END = acc_no[("sT", B * ST - 1)] + 1
    EXPERTS_END = acc_no[("EO", E - 1)] + 1

    def wait_used(eng, ev):
        eng.wait_ge(acc_free, acc_no[ev] + 1)

    def wait_done(eng, ev):
        eng.wait_ge(acc_full, acc_no[ev] + 1)

    def weight_piece(e, w):
        return [(w_gu[s][:, e % 2, w] if w < 2 else w_d[s][:, e % 2]) for s in range(2)]

    block = top.enter_context(nc.Block())

    @block.sync
    def _(sp):
        sp.dma_start(ctx_main[:], ctx[:, 0:P].rearrange("b p d -> p b d")).then_inc(d_ctx, 16)
        sp.dma_start(ctx_tail[:], ctx[:, P:SK].rearrange("b p d -> p b d")).then_inc(d_ctx, 16)
        weights = [w.rearrange("(k p) n -> p k n", p=P) for w in (Wk, Wv, Wq, Wo)]

        def load_weights(i):
            if i >= 2:
                sp.wait_ge(split_high, i - 1)
                sp.wait_ge(split_low, i - 1)
            k = weights[i].shape[1]
            sp.dma_start(wraw[:, i % 2].rearrange("p (k n) -> p k n", k=k), weights[i]).then_inc(d_w[i], 16)

        load_weights(0)
        sp.dma_start(bk_c[:], bk.rearrange("(m p) -> p m", p=P)).then_inc(d_bk, 16)
        x_t = x.rearrange("b (t p) d -> p (b t) d", p=P)
        sp.dma_start(x1[:, 0:2], x_t[:, 0:2]).then_inc(d_x, 16)
        load_weights(1)
        load_weights(2)
        sp.dma_start(bq_c[:], bq.rearrange("(m p) -> p m", p=P)).then_inc(d_small, 16)
        sp.dma_start(bv_c[:], bv.rearrange("(m p) -> p m", p=P)).then_inc(d_small, 16)
        sp.dma_start(bo_b[:], bo.unsqueeze(0).to_broadcast([P, D])).then_inc(d_small, 16)
        sp.dma_start(mask_u8[:], mask.rearrange("a b (t p) k -> p (a b t) k", p=P)).then_inc(d_mask, 16)
        sp.dma_start(x1[:, 2:TILES], x_t[:, 2:TILES]).then_inc(d_x, 16)
        load_weights(3)
        sp.dma_start(gain[:], norm_g.unsqueeze(0).to_broadcast([P, D])).then_inc(d_gain, 16)
        sp.dma_start(shift[:], norm_b.unsqueeze(0).to_broadcast([P, D])).then_inc(d_gain, 16)
        sp.wait_ge(acc_free, ATT_END)
        sp.dma_start(se[:], slot_embeds.rearrange("(t e) s d -> (e s) t d", e=P // SLOTS)).then_inc(d_se, 16)
        sp.dma_start(sg_b[:], slot_g.unsqueeze(0).to_broadcast([P, D])).then_inc(d_se, 16)
        sp.dma_start(sb_b[:], slot_b.unsqueeze(0).to_broadcast([P, D])).then_inc(d_se, 16)
        sp.dma_start(sc_b[:], scale.unsqueeze(0).to_broadcast([P, 1])).then_inc(d_se, 16)
        l_t = logits_dram.rearrange("(t p) s -> p t s", p=P)
        for i in range(TILES):
            sp.wait_ge(l_ready, i + 1)
            sp.dma_start(l_t[:, i], lsb[:, i]).then_inc(d_lst, 16)
        sp.wait_ge(acc_free, SLOTS_END)
        sp.wait_ge(d_lst, 16 * TILES)
        for bias, at in ((bg, 0), (bu, F), (bd, 2 * F)):
            sp.dma_start(b_raw[:, at:at + bias.shape[1]], bias).then_inc(d_bias, 16)
        for i, (e, w) in enumerate(pieces):
            if i >= RAW:
                sp.wait_ge(w_high, i - RAW + 1)
                e0, w0 = pieces[i - RAW]
                sp.wait_ge((gate_low, up_low, down_low)[w0], e0 + 1)
            view = (Wg, Wu, Wd)[w][e].rearrange("(k p) n -> p k n", p=P)
            sp.dma_start(w_raw[:, i % RAW].rearrange("p (k n) -> p k n", k=view.shape[1]), view)\
                .then_inc(d_raw[i % RAW], 16)
        out_t = out.rearrange("b (t p) d -> p (b t) d", p=P)
        for i in range(TILES + STORE_LAG):
            if i < TILES:
                if i >= 3:
                    sp.wait_ge(c_ready, i - 2)
                sp.dma_start(lraw[:, i % 3], l_t[:, i]).then_inc(d_lld[i % 3], 16)
            if i >= STORE_LAG:
                o = i - STORE_LAG
                sp.wait_ge(out_ready, o + 1)
                sp.dma_start(out_t[:, o], outb[:, o % 2]).then_inc(d_out[o % 2], 16)
        for s in d_out:
            sp.wait_ge(s, 16 * TILES // 2)

    @block.gpsimd
    def _(pool):
        steps = [0]

        def link(ins):
            steps[0] += 1
            ins.then_inc(pool_step, 1)
            pool.wait_ge(pool_step, steps[0])

        link(pool.memset(ident[:], 0.0))
        link(pool.affine_select(out=ident[:], in_=ident[:], compare_op=ALU.not_equal, fill=1.0, base=0,
                                pattern=[[-1, P]], channel_multiplier=1))
        pool.tensor_copy(ident16[:], ident[:]).then_inc(const_pool, 1)
        link(pool.memset(quad_mask[:], 1.0))
        link(pool.affine_select(out=quad_mask[:], in_=quad_mask[:], compare_op=ALU.is_ge, fill=0.0, base=0,
                                pattern=[[-TAIL, 4], [0, DH]], channel_multiplier=1))
        pool.affine_select(out=quad_mask[:], in_=quad_mask[:], compare_op=ALU.is_ge, fill=0.0, base=TAIL - 1,
                           pattern=[[TAIL, 4], [0, DH]], channel_multiplier=-1).then_inc(const_pool, 1)
        pool.wait_ge(const_dve, 1)
        pool.wait_ge(d_small, 48)
        for ev in attention:
            if ev[0] == "LN":
                g = ev[1]
                pool.wait_ge(var_ready, g + 1)
                link(pool.tensor_tensor(rstd[:, 0], bmv[:, :, 1], eps[:], ALU.add))
                pool.tensor_tensor(rstd[:, 1], rstd[:, 0], mhalf[:, 0:2], ALU.pow).then_inc(rstd_ready, 1)
            elif ev[0] == "XN":
                g = ev[1]
                pool.wait_ge(xn_ready, g + 1)
                pool.tensor_tensor(x1[:, 2 * g:2 * g + 2], x1[:, 2 * g:2 * g + 2],
                                   bo_b[:].unsqueeze(1).to_broadcast([P, 2, D]), ALU.add).then_inc(xbo_ready, 1)
            elif ev[0] == "R":
                _, n, pp = ev
                pool.wait_ge(recip_ready, 2 * n + pp + 1)
                if n >= 2:
                    pool.wait_ge(t_full, 3 * (n - 2) + 3)
                heads = slice(2 * pp, 2 * pp + 2)
                pool.tensor_tensor(prob[:, n % 2, :, heads, :], expo[:, pp, :, :, 0:P],
                                   prec[:, pp].unsqueeze(3).to_broadcast([P, 2, 2, P]), ALU.mult)
                pool.tensor_tensor(prob_t[:, n % 2, :, heads, :], expo[:, pp, :, :, P:SK],
                                   prec[:, pp].unsqueeze(3).to_broadcast([P, 2, 2, TAIL]), ALU.mult)\
                    .then_inc(norm_ready, 1)
            elif ev[0] == "Y" and ev[2] == 1:
                g = ev[1]
                pool.wait_ge(mv2_ready, 2 * g + 2)
                v = mv2[:, 2 * g:2 * g + 2, 1]
                link(pool.tensor_tensor(norm2[:, 0], v, eps[:], ALU.add))
                link(pool.tensor_tensor(norm2[:, 1], norm2[:, 0], mhalf[:, 0:2], ALU.pow))
                link(pool.tensor_tensor(norm2[:, 2], v, norm2[:, 1], ALU.mult))
                link(pool.tensor_tensor(norm2[:, 3], norm2[:, 2], norm2[:, 1], ALU.mult))
                link(pool.tensor_tensor(norm2[:, 4], norm2[:, 3], eps[:], ALU.add))
                link(pool.tensor_tensor(norm2[:, 5], norm2[:, 4], mhalf[:, 0:2], ALU.pow))
                pool.tensor_tensor(rstd2[:, 2 * g:2 * g + 2], norm2[:, 5], norm2[:, 1], ALU.mult)\
                    .then_inc(rstd2_ready, 1)
        pool.wait_ge(acc_free, ATT_END)
        pool.wait_ge(d_gain, 32)
        pool.wait_ge(se_var, 1)
        link(pool.tensor_tensor(srs[:, 0], smv[:, :, 1], eps[:, 0:1].to_broadcast([P, ST]), ALU.add))
        pool.tensor_tensor(srs[:, 1], srs[:, 0], mhalf[:], ALU.pow).then_inc(se_rstd, 1)
        for ev in logits:
            if ev[0] == "N2":
                i = ev[1]
                pool.wait_ge(x2_centered, i + 1)
                link(pool.tensor_tensor(x2f[:, i % 3], x2f[:, i % 3], gain[:], ALU.mult))
                pool.tensor_tensor(x2f[:, i % 3], x2f[:, i % 3], shift[:], ALU.add).then_inc(x2_ready, 1)
            elif ev[0] == "x2T":
                i = ev[1]
                pool.wait_ge(x2_high, i + 1)
                pool.tensor_tensor(x2[1][:, i, 0:D], x2f[:, i % 3], x2[0][:, i, 0:D], ALU.subtract).then_inc(x2_low, 1)
        for ev in slots:
            if ev[0] == "E":
                n = ev[1]
                b, t = divmod(n, ST)
                pool.wait_ge(cm_ready, B)
                if n >= 2:
                    pool.wait_ge(d_low, n - 1)
                pool.tensor_tensor(disp_f[:, n % 2], lsb[:, b * TB:(b + 1) * TB, t * P:(t + 1) * P],
                                   nb_b[:, b, t * P:(t + 1) * P].unsqueeze(1).to_broadcast([P, TB, P]), ALU.add)\
                    .then_inc(d_shift, 1)
        pool.wait_ge(acc_free, SLOTS_END)
        for e, w in pieces:
            if w == 1:
                continue
            i = piece_no[e, w]
            pool.wait_ge(w_high, i + 1)
            high, low = weight_piece(e, w)
            pool.tensor_tensor(low, w_raw[:, i % RAW].rearrange("p (k n) -> p k n", k=KD if w == 0 else FT), high,
                               ALU.subtract).then_inc(gate_low if w == 0 else down_low, 1)

    @block.scalar
    def _(act):
        def high_half(ev, dst, src, bias=0.0):
            wait_done(act, ev)
            act.activation(dst, src, ACT.Identity, bias=bias).then_inc(acc_high, 1)

        def split_weights(i, dst):
            act.wait_ge(d_w[i], 16)
            act.copy(dst, wraw[:, i % 2]).then_inc(split_high, 1)

        split_weights(0, wkq[0][:].rearrange("p k n -> p (k n)"))
        act.wait_ge(d_bk, 16)
        for ev in prologue:
            no = acc_no[ev]
            if ev[0] == "cT":
                high_half(ev, cT[0][:, ev[1]], acc(no)[:, 0:B * SK].rearrange("p (b s) -> p b s", b=B))
                if ev[1] == KD - 1:
                    split_weights(1, wvo[0][:])
            elif ev[0] == "K":
                p = ev[1]
                act.wait_ge(k_ready, p + 1)
                act.copy(kbd[0][0:DH, :, p, 0:SK], k_f[0:DH, p % 2])
                act.copy(kbd[0][DH:P, :, p, SK:PK], k_f[DH:P, p % 2]).then_inc(k_high, 1)
            else:
                _, b, c, t = ev
                if t == 0:
                    wait_done(act, ev)
                    act.copy(vm[0][:, b, 4 * c:4 * c + 4, :].rearrange("p q (a d) -> p q a d", a=3)[:, :, 0:3:2],
                             acc(no).rearrange("p (q a d) -> p q a d", q=4, a=2)).then_inc(v_high, 1)
                else:
                    act.wait_ge(v_ready, b * 2 + c + 1)
                    act.copy(vt[0][:, b, 2 * c:2 * c + 2, :], v_f[:]).then_inc(v_high, 1)
        wait_done(act, ("K", PAIRS - 1))
        split_weights(2, wkq[0][:].rearrange("p k n -> p (k n)"))
        wait_done(act, prologue[-1])
        split_weights(3, wvo[0][:])
        act.wait_ge(split_low, 4)
        act.wait_ge(v_low, 2 * B)
        act.wait_ge(mask_ready, 1)
        act.wait_ge(d_small, 48)
        for ev in attention_act:
            no = acc_no.get(ev)
            if ev[0] == "xT":
                high_half(ev, xT[0][:, ev[2]], acc(no)[:, 0:2 * P])
            elif ev[0] == "Q":
                _, n, pp = ev
                p = 2 * (n % QUADS) + pp
                high_half(ev, qT[0][:, n % 2, pp], acc(no)[:, 0:2 * P], bq_c[:, p:p + 1])
            elif ev[0] == "S":
                _, n, pp, j = ev
                s = s_no[ev]
                act.wait_ge(s_max, s + 1)
                if n >= 1:
                    act.wait_ge(norm_ready, 2 * (n - 1) + pp + 1)
                for h in range(2):
                    ins = act.activation(expo[:, pp, j, h, :], ps[:, s % 2, h * SK:(h + 1) * SK], ACT.Exp,
                                         bias=nmax[:, s % 2, h:h + 1],
                                         accum_out=psums[:, pp, j, h:h + 1])
                ins.then_inc(s_exp, 1)
            elif ev[0] == "T":
                _, n, t = ev
                k = t_no[ev]
                act.wait_ge(t_full, k + 1)
                if n >= 2:
                    wait_done(act, ("PV", n - 2, 1))
                rows, tiles = (P, 2) if t < 2 else (T4, 1)
                act.copy(pT[0][0:rows, n % 2, 2 * t:2 * t + tiles],
                         ps[0:rows, 2 + k % 2, 0:tiles * 2 * P].rearrange("p (t n) -> p t n", t=tiles))\
                    .then_inc(t_high, 1)
            elif ev[0] == "PV":
                _, n, pp = ev
                p = 2 * (n % QUADS) + pp
                high_half(ev, oT[0][:, p], acc(no)[:, 0:2 * P], bv_c[:, p:p + 1])
        act.wait_ge(acc_free, ATT_END)
        for ev in logits:
            no = acc_no.get(ev)
            if ev[0] == "seT":
                t = ev[1]
                high_half(ev, seT[0][:, :, t * P:(t + 1) * P], acc(no)[:, 0:2 * P].rearrange("p (k s) -> p k s", k=KD))
            elif ev[0] == "x2T":
                i = ev[1]
                high_half(ev, x2T[0][:, i % 2], acc(no)[:, 0:2 * P].rearrange("p (k s) -> p k s", k=KD))
                act.copy(x2[0][:, i, 0:D], x2f[:, i % 3]).then_inc(x2_high, 1)
            elif ev[0] == "L":
                i = ev[1]
                act.wait_ge(l_full, i + 1)
                act.copy(lsb[:, i].rearrange("p (c n) -> p c n", c=2), ps[:, 2 * (i % 2):2 * (i % 2) + 2, :])\
                    .then_inc(l_ready, 1)
        for ev in slots:
            no = acc_no.get(ev)
            if ev[0] == "CM":
                b = ev[1]
                act.wait_ge(cm_bcast, b + 1)
                act.copy(nb_b[:, b].rearrange("p (c n) -> p c n", c=2), ps[:, 0:2, :]).then_inc(cm_ready, 1)
            elif ev[0] == "E":
                n = ev[1]
                act.wait_ge(d_shift, n + 1)
                act.activation(disp_f[:, n % 2], disp_f[:, n % 2], ACT.Exp).then_inc(d_exp, 1)
                if n >= 3:
                    wait_done(act, ("D", n - 3))
                act.wait_ge(d_exp, n + 1)
                act.copy(disp[0][:, n % 3], disp_f[:, n % 2]).then_inc(d_high, 1)
            elif ev[0] == "sT":
                b, t = divmod(ev[1], ST)
                wait_done(act, ev)
                for k in range(KD):
                    ins = act.copy(sT[0][:, k, 2 * t:2 * t + 2, b, :],
                                   acc(no)[:, k * P:(k + 1) * P].rearrange("p (e s) -> p e s", e=2))
                ins.then_inc(acc_high, 1)
        act.wait_ge(acc_free, SLOTS_END)
        act.wait_ge(d_lst, 16 * TILES)

        def weights_high(e, w):
            i = piece_no[e, w]
            act.wait_ge(d_raw[i % RAW], 16 * (i // RAW + 1))
            if e >= 2:
                act.wait_ge(gu_full, e - 1) if w < 2 else wait_done(act, ("EO", e - 2))
            act.copy(weight_piece(e, w)[0],
                     w_raw[:, i % RAW].rearrange("p (k n) -> p k n", k=KD if w < 2 else FT)).then_inc(w_high, 1)

        act.wait_ge(const_dve, 3)
        act.wait_ge(d_bias, 48)
        act.copy(b_row[0:E], b_raw[:]).then_inc(b_high, 1)
        for e, w in pieces[:6]:
            weights_high(e, w)
        for ev in experts:
            no = acc_no.get(ev)
            if ev[0] == "GU":
                e = ev[1]
                act.wait_ge(gu_full, e + 1)
                if e >= 1:
                    act.wait_ge(hid_ready, e)
                act.activation(gate[:], ps[:, 2 * (e % 2), :], ACT.Gelu).then_inc(gate_ready, 1)
                if e + 2 < E:
                    weights_high(e + 2, 0)
                    weights_high(e + 2, 1)
            elif ev[0] == "HT":
                e = ev[1]
                high_half(ev, hT[0][:, e % 2].rearrange("p f s -> p (f s)"), acc(no))
            elif ev[1] + 2 < E:
                weights_high(ev[1] + 2, 2)
        act.wait_ge(acc_free, EXPERTS_END)
        for ev in combine:
            if ev[0] == "C":
                i = ev[1]
                act.wait_ge(d_lld[i % 3], 16 * (i // 3 + 1))
                if i >= 2:
                    act.wait_ge(ct_full, 2 * (i - 1))
                act.activation(comb[:, i % 2], lraw[:, i % 3], ACT.Exp, bias=neg_amax[:, i:i + 1],
                               accum_out=csum[:, i:i + 1]).then_inc(c_ready, 1)
            elif ev[0] == "CT":
                _, i, c = ev
                k = 2 * i + c
                act.wait_ge(ct_full, k + 1)
                if i >= 2:
                    wait_done(act, ("CO", i - 2))
                act.copy(combT[0][:, i % 2, 4 * c:4 * c + 4].rearrange("p t n -> p (t n)"), ps[:, k % 4, :])\
                    .then_inc(ct_high, 1)

    @block.vector
    def _(dve):
        steps = [0]

        def link(ins):
            steps[0] += 1
            ins.then_inc(dve_step, 1)
            dve.wait_ge(dve_step, steps[0])

        def low_half(ev, dst, src, high, bias=None):
            dve.wait_ge(acc_high, high_no[ev] + 1)
            if bias is None:
                dve.tensor_tensor(dst, src, high, ALU.subtract).then_inc(acc_free, 1)
            else:
                dve.scalar_tensor_tensor(out=dst, in0=src, scalar=bias, in1=high, op0=ALU.add, op1=ALU.subtract)\
                    .then_inc(acc_free, 1)

        dve.memset(eps[:], EPS)
        dve.memset(mhalf[:], -0.5)
        dve.memset(ones[:], 1.0)
        dve.memset(kbd[0][:].bitcast(F32), 0.0)
        dve.memset(kbd[1][:].bitcast(F32), 0.0)
        dve.memset(vm[0][:].bitcast(F32), 0.0)
        dve.memset(vm[1][:].bitcast(F32), 0.0).then_inc(const_dve, 1)

        def split_weights(i, high, low):
            dve.wait_ge(split_high, i + 1)
            dve.tensor_tensor(low, wraw[:, i % 2], high, ALU.subtract).then_inc(split_low, 1)

        flat = [w[:].rearrange("p k n -> p (k n)") for w in wkq]
        split_weights(0, flat[0], flat[1])
        dve.wait_ge(d_bk, 16)
        dve.wait_ge(const_pool, 2)
        for ev in prologue:
            no = acc_no[ev]
            if ev[0] == "cT":
                k = ev[1]
                low_half(ev, cT[1][:, k], acc(no)[:, 0:B * SK].rearrange("p (b s) -> p b s", b=B), cT[0][:, k])
                if k == KD - 1:
                    wait_used(dve, ev)
                    for s in range(2):
                        for kk in range(KD):
                            ins = dve.tensor_copy(cT4[s][:, kk],
                                                  cT[s][:, kk, :, P:SK].unsqueeze(2).to_broadcast([P, B, 4, TAIL]))
                    ins.then_inc(cT4_ready, 1)
                    split_weights(1, wvo[0][:], wvo[1][:])
            elif ev[0] == "K":
                p = ev[1]
                wait_done(dve, ev)
                if p >= 2:
                    dve.wait_ge(k_low, p - 1)
                dve.tensor_scalar(k_f[:, p % 2], acc(no)[:, 0:B * SK].rearrange("p (b s) -> p b s", b=B),
                                  bk_c[:, p:p + 1], DH ** -0.5, ALU.add, ALU.mult).then_inc(k_ready, 1)
                dve.wait_ge(k_high, p + 1)
                dve.tensor_tensor(kbd[1][0:DH, :, p, 0:SK], k_f[0:DH, p % 2], kbd[0][0:DH, :, p, 0:SK], ALU.subtract)\
                    .then_inc(acc_free, 1)
                dve.tensor_tensor(kbd[1][DH:P, :, p, SK:PK], k_f[DH:P, p % 2], kbd[0][DH:P, :, p, SK:PK], ALU.subtract)\
                    .then_inc(k_low, 1)
            else:
                _, b, c, t = ev
                m = 4 * b + 2 * c + t
                if t == 0:
                    src = acc(no).rearrange("p (q a d) -> p q a d", q=4, a=2)
                    view = [v[:, b, 4 * c:4 * c + 4, :].rearrange("p q (a d) -> p q a d", a=3)[:, :, 0:3:2] for v in vm]
                    dve.wait_ge(v_high, m + 1)
                    dve.tensor_tensor(view[1], src, view[0], ALU.subtract).then_inc(acc_free, 1)
                else:
                    wait_done(dve, ev)
                    if m >= 2:
                        dve.wait_ge(v_low, m // 2)
                    dve.tensor_tensor(v_f[:], acc(no)[0:T4, :].rearrange("p (q n) -> p q n", q=2),
                                      quad_mask[:].rearrange("p a d -> p (a d)").unsqueeze(1).to_broadcast([T4, 2, 4 * DH]),
                                      ALU.mult).then_inc(v_ready, 1)
                    dve.wait_ge(v_high, m + 1)
                    dve.tensor_tensor(vt[1][:, b, 2 * c:2 * c + 2, :], v_f[:], vt[0][:, b, 2 * c:2 * c + 2, :],
                                      ALU.subtract).then_inc(v_low, 1)
                    dve.wait_ge(v_low, m // 2 + 1)
                    dve.engine_nop().then_inc(acc_free, 1)
        dve.wait_ge(d_mask, 16)
        dve.tensor_scalar(maskb[:], mask_u8[:], MASKED, None, ALU.mult).then_inc(mask_ready, 1)
        split_weights(2, flat[0], flat[1])
        split_weights(3, wvo[0][:], wvo[1][:])
        dve.wait_ge(split_low, 4)
        dve.wait_ge(mask_ready, 1)
        dve.wait_ge(d_small, 48)
        for ev in attention_dve:
            no = acc_no.get(ev)
            if ev[0] == "LN":
                g = ev[1]
                dve.wait_ge(d_x, 16 if g == 0 else 32)
                for j in range(2):
                    ins = dve.bn_stats(bst[:, j], x1[:, 2 * g + j])
                link(ins)
                for j in range(2):
                    ins = dve.bn_aggr(bmv[:, j], bst[:, j])
                ins.then_inc(var_ready, 1)
            elif ev[0] == "XN":
                g = ev[1]
                dve.wait_ge(rstd_ready, g + 1)
                dve.wait_ge(var_ready, g + 1)
                if g:
                    wait_done(dve, ("xT", g - 1, 1))
                for j in range(2):
                    ins = dve.tensor_scalar(xn[:, j], x1[:, 2 * g + j], bmv[:, j, 0:1], rstd[:, 1, j:j + 1],
                                            ALU.subtract, ALU.mult)
                ins.then_inc(xn_ready, 1)
            elif ev[0] == "xT":
                low_half(ev, xT[1][:, ev[2]], acc(no)[:, 0:2 * P], xT[0][:, ev[2]])
            elif ev[0] == "Q":
                _, n, pp = ev
                p = 2 * (n % QUADS) + pp
                low_half(ev, qT[1][:, n % 2, pp], acc(no)[:, 0:2 * P], qT[0][:, n % 2, pp], bq_c[:, p:p + 1])
            elif ev[0] == "S":
                s = s_no[ev]
                dve.wait_ge(s_full, s + 1)
                dve.tensor_reduce(nmax[:, s % 2], ps[:, s % 2, 0:PK].rearrange("p (h k) -> p h k", h=2), AX, ALU.max,
                                  negate=True).then_inc(s_max, 1)
            elif ev[0] == "R":
                _, n, pp = ev
                dve.wait_ge(s_exp, s_no[("S", n, pp, 1)] + 1)
                if n >= 1:
                    dve.wait_ge(norm_ready, 2 * (n - 1) + pp + 1)
                dve.reciprocal(prec[:, pp], psums[:, pp]).then_inc(recip_ready, 1)
            elif ev[0] == "T":
                _, n, t = ev
                k = t_no[ev]
                dve.wait_ge(t_high, k + 1)
                rows, tiles = (P, 2) if t < 2 else (T4, 1)
                dve.tensor_tensor(pT[1][0:rows, n % 2, 2 * t:2 * t + tiles],
                                  ps[0:rows, 2 + k % 2, 0:tiles * 2 * P].rearrange("p (t n) -> p t n", t=tiles),
                                  pT[0][0:rows, n % 2, 2 * t:2 * t + tiles], ALU.subtract).then_inc(t_free, 1)
            elif ev[0] == "PV":
                _, n, pp = ev
                p = 2 * (n % QUADS) + pp
                low_half(ev, oT[1][:, p], acc(no)[:, 0:2 * P], oT[0][:, p], bv_c[:, p:p + 1])
            elif ev[0] == "Y":
                _, g, j = ev
                i = 2 * g + j
                wait_done(dve, ev)
                dve.wait_ge(xbo_ready, g + 1)
                dve.tensor_tensor(x1[:, i], acc(no)[:, 0:D], x1[:, i], ALU.add).then_inc(acc_free, 1)
                wait_used(dve, ev)
                link(dve.bn_stats(bst2[:], x1[:, i]))
                dve.bn_aggr(mv2[:, i], bst2[:]).then_inc(mv2_ready, 1)
        dve.wait_ge(acc_free, ATT_END)
        dve.wait_ge(mv2_ready, TILES)
        dve.memset(x2[0][:, :, D:D + 1].bitcast(F32), 1.0)
        dve.memset(x2[0][:, :, D + 1:DN].bitcast(F32), 0.0)
        dve.memset(x2[1][:, :, D:DN].bitcast(F32), 0.0).then_inc(const_dve, 1)
        dve.wait_ge(d_se, 64)
        for t in range(ST):
            ins = dve.bn_stats(sst[:, t], se[:, t])
        link(ins)
        for t in range(ST):
            ins = dve.bn_aggr(smv[:, t], sst[:, t])
        ins.then_inc(se_var, 1)
        dve.wait_ge(se_rstd, 1)
        dve.wait_ge(se_var, 1)
        for t in range(ST):
            ins = dve.tensor_scalar(se[:, t], se[:, t], smv[:, t, 0:1], srs[:, 1, t:t + 1], ALU.subtract, ALU.mult)
        link(ins)
        link(dve.tensor_tensor(se[:], se[:], sg_b[:].unsqueeze(1).to_broadcast([P, ST, D]), ALU.mult))
        link(dve.tensor_tensor(se[:], se[:], sb_b[:].unsqueeze(1).to_broadcast([P, ST, D]), ALU.add))
        dve.tensor_scalar(se[:], se[:], sc_b[:, 0:1], None, ALU.mult).then_inc(se_ready, 1)
        for ev in logits:
            no = acc_no.get(ev)
            if ev[0] == "seT":
                t = ev[1]
                cols = slice(t * P, (t + 1) * P)
                low_half(ev, seT[1][:, :, cols], acc(no)[:, 0:2 * P].rearrange("p (k s) -> p k s", k=KD),
                         seT[0][:, :, cols])
            elif ev[0] == "N2":
                i = ev[1]
                dve.wait_ge(rstd2_ready, i // 2 + 1)
                if i >= 3:
                    wait_done(dve, ("x2T", i - 3))
                    dve.wait_ge(x2_high, i - 2)
                    dve.wait_ge(x2_low, i - 2)
                dve.tensor_scalar(x2f[:, i % 3], x1[:, i], mv2[:, i, 0:1], rstd2[:, i:i + 1],
                                  ALU.subtract, ALU.mult).then_inc(x2_centered, 1)
            elif ev[0] == "x2T":
                i = ev[1]
                low_half(ev, x2T[1][:, i % 2], acc(no)[:, 0:2 * P].rearrange("p (k s) -> p k s", k=KD), x2T[0][:, i % 2])
            elif ev[0] == "L":
                i = ev[1]
                dve.wait_ge(l_ready, i + 1)
                dve.tensor_reduce(neg_amax[:, i:i + 1], lsb[:, i], AX, ALU.max, negate=True).then_inc(amax_ready, 1)
                b = i // TB
                if i % TB:
                    dve.wait_ge(colmax_ready, i)
                first = lsb[:, i] if i % TB == 0 else colmax[:, b]
                dve.tensor_tensor(colmax[:, b], first, lsb[:, i], ALU.max).then_inc(colmax_ready, 1)
        for ev in slots:
            no = acc_no.get(ev)
            if ev[0] == "CM":
                b = ev[1]
                if b:
                    dve.wait_ge(cm_bcast, b)
                dve.wait_ge(cm_full, b + 1)
                link(dve.tensor_reduce(nb[:].rearrange("p (c t) -> p c t", c=2),
                                       ps[:, 2:4, :].rearrange("p c (t n) -> p c t n", t=4), AX, ALU.max, negate=True))
                dve.tensor_tensor(disp_f[:, 1], ident[:].unsqueeze(1).to_broadcast([P, ST, P]),
                                  nb[:].unsqueeze(2).to_broadcast([P, ST, P]), ALU.mult).then_inc(cm_diag, 1)
            elif ev[0] == "E":
                n = ev[1]
                dve.wait_ge(d_high, n + 1)
                dve.tensor_tensor(disp[1][:, n % 3], disp_f[:, n % 2], disp[0][:, n % 3], ALU.subtract).then_inc(d_low, 1)
            elif ev[0] == "D":
                n = ev[1]
                wait_done(dve, ev)
                if n >= 2:
                    wait_done(dve, ("sT", n - 2))
                link(dve.reciprocal(den[:, n % 2:n % 2 + 1], acc(no)[:, D:D + 1]))
                dve.tensor_scalar(slot_f[:, n % 2], acc(no)[:, 0:D], den[:, n % 2:n % 2 + 1], None, ALU.mult)\
                    .then_inc(acc_free, 1)
            elif ev[0] == "sT":
                b, t = divmod(ev[1], ST)
                dve.wait_ge(acc_high, high_no[ev] + 1)
                for k in range(KD):
                    at = (slice(None), k, slice(2 * t, 2 * t + 2), b)
                    ins = dve.tensor_tensor(sT[1][at], acc(no)[:, k * P:(k + 1) * P].rearrange("p (e s) -> p e s", e=2),
                                            sT[0][at], ALU.subtract)
                ins.then_inc(acc_free, 1)
        dve.wait_ge(acc_free, SLOTS_END)
        dve.wait_ge(d_lst, 16 * TILES)
        dve.memset(b_row[:].bitcast(F32), 0.0)
        rows = slice(0, 32 + E)
        dve.tensor_tensor(b_pick[:], ident[rows, 0:E].unsqueeze(2).to_broadcast([32 + E, E, P]),
                          ident[rows, 32:32 + E].unsqueeze(2).to_broadcast([32 + E, E, P]), ALU.add)\
            .then_inc(const_dve, 1)
        dve.wait_ge(const_dve, 3)

        def weights_low(e):
            i = piece_no[e, 1]
            high, low = weight_piece(e, 1)
            dve.wait_ge(w_high, i + 1)
            dve.tensor_tensor(low, w_raw[:, i % RAW].rearrange("p (k n) -> p k n", k=KD), high, ALU.subtract)\
                .then_inc(up_low, 1)

        dve.wait_ge(b_high, 1)
        dve.tensor_tensor(b_row[32:32 + E], b_raw[:], b_row[0:E], ALU.subtract).then_inc(b_low, 1)
        weights_low(0)
        weights_low(1)
        for ev in experts:
            no = acc_no.get(ev)
            e = ev[1]
            if ev[0] == "GU":
                dve.wait_ge(gate_ready, e + 1)
                if e >= 2:
                    wait_done(dve, ("HT", e - 2))
                dve.tensor_tensor(hid[:, e % 2], ps[:, 2 * (e % 2) + 1, :], gate[:], ALU.mult)\
                    .then_inc(hid_ready, 1)
                if e + 2 < E:
                    weights_low(e + 2)
            elif ev[0] == "HT":
                low_half(ev, hT[1][:, e % 2].rearrange("p f s -> p (f s)"), acc(no),
                         hT[0][:, e % 2].rearrange("p f s -> p (f s)"))
            else:
                wait_done(dve, ev)
                places = [(slice(64 * (e % 2), 64 * (e % 2) + 64), b, e // 2) for b in range(B)]
                for b, at in enumerate(places):
                    ins = dve.tensor_copy(eo[0][at], acc(no)[64 * b:64 * b + 64, 0:D])
                link(ins)
                for b, at in enumerate(places):
                    ins = dve.tensor_tensor(eo[1][at], acc(no)[64 * b:64 * b + 64, 0:D], eo[0][at], ALU.subtract)
                ins.then_inc(acc_free, 1)
        for ev in combine:
            if ev[0] == "C":
                i = ev[1]
                dve.wait_ge(c_ready, i + 1)
                dve.reciprocal(crec[:, i:i + 1], csum[:, i:i + 1]).then_inc(dve_step, 1)
                steps[0] += 1
            elif ev[0] == "CT":
                _, i, c = ev
                k = 2 * i + c
                dve.wait_ge(ct_high, k + 1)
                at = (slice(None), i % 2, slice(4 * c, 4 * c + 4))
                dve.tensor_tensor(combT[1][at].rearrange("p t n -> p (t n)"), ps[:, k % 4, :],
                                  combT[0][at].rearrange("p t n -> p (t n)"), ALU.subtract).then_inc(ct_low, 1)
            elif ev[0] == "CO":
                i = ev[1]
                no = acc_no[ev]
                wait_done(dve, ev)
                if i >= 2:
                    dve.wait_ge(d_out[i % 2], 16 * (i // 2))
                dve.wait_ge(dve_step, steps[0])
                dve.scalar_tensor_tensor(out=outb[:, i % 2], in0=acc(no)[:, 0:D], scalar=crec[:, i:i + 1],
                                         in1=x1[:, i], op0=ALU.mult, op1=ALU.add).then_inc(out_ready, 1)
                dve.wait_ge(out_ready, i + 1)
                dve.engine_nop().then_inc(acc_free, 1)

    @block.tensor
    def _(pe):
        def bank(ev):
            no = acc_no[ev]
            if no >= 4:
                pe.wait_ge(acc_free, no - 3)
            return acc(no)

        pe.wait_ge(const_pool, 2)
        pe.wait_ge(const_dve, 1)
        pe.wait_ge(d_ctx, 32)
        for ev in prologue:
            dst = bank(ev)
            if ev[0] == "cT":
                k = ev[1]
                for b in range(B):
                    pe.transpose(dst[:, b * SK:b * SK + P], ctx_main[:, b, k * P:(k + 1) * P], ident[:])
                    ins = pe.transpose(dst[:, b * SK + P:(b + 1) * SK], ctx_tail[:, b, k * P:(k + 1) * P],
                                       ident[0:TAIL, 0:TAIL])
            elif ev[0] == "K":
                p = ev[1]
                if p == 0:
                    pe.wait_ge(split_low, 1)
                    wait_used(pe, ("cT", KD - 1))
                for n, (s, m) in enumerate(PASSES):
                    for k in range(KD):
                        ins = pe.matmul(dst[:, 0:B * SK], wkq[s][:, k, p * P:(p + 1) * P],
                                        cT[m][:, k].rearrange("p b s -> p (b s)"),
                                        start=(n == 0 and k == 0), stop=(n == 2 and k == KD - 1))
            else:
                _, b, c, t = ev
                if (b, c, t) == (0, 0, 0):
                    pe.wait_ge(split_low, 2)
                    pe.wait_ge(cT4_ready, 1)
                rows = P if t == 0 else T4
                for n, (s, m) in enumerate(PASSES):
                    for k in range(KD):
                        lhs = cT[s][:, k, b, 0:P] if t == 0 else cT4[s][:, k, b].rearrange("p a t -> p (a t)")
                        ins = pe.matmul(dst[0:rows, :], lhs, wv[m][:, k, c * F:(c + 1) * F],
                                        start=(n == 0 and k == 0), stop=(n == 2 and k == KD - 1))
            ins.then_inc(acc_full, 1)

        for ev in attention:
            if ev[0] == "xT":
                _, g, k = ev
                dst = bank(ev)
                pe.wait_ge(xn_ready, g + 1)
                for j in range(2):
                    ins = pe.transpose(dst[:, j * P:(j + 1) * P], xn[:, j, k * P:(k + 1) * P], ident[:])
                ins.then_inc(acc_full, 1)
            elif ev[0] == "Q":
                _, n, pp = ev
                g, q = divmod(n, QUADS)
                p = 2 * q + pp
                dst = bank(ev)
                wait_used(pe, ("xT", g, 1))
                if n == 0:
                    pe.wait_ge(split_low, 3)
                for r, (s, m) in enumerate(PASSES):
                    for k in range(KD):
                        ins = pe.matmul(dst[:, 0:2 * P], wkq[s][:, k, p * P:(p + 1) * P], xT[m][:, k],
                                        start=(r == 0 and k == 0), stop=(r == 2 and k == KD - 1))
                ins.then_inc(acc_full, 1)
            elif ev[0] == "S":
                _, n, pp, j = ev
                g, q = divmod(n, QUADS)
                s_i, tile = s_no[ev], 2 * g + j
                b, p = tile // TB, 2 * q + pp
                if s_i == 0:
                    pe.wait_ge(mask_ready, 1)
                    pe.wait_ge(k_low, PAIRS)
                if s_i >= 2:
                    pe.wait_ge(s_exp, s_i - 1)
                wait_used(pe, ("Q", n, pp))
                dst = ps[:, s_i % 2, 0:PK]
                pe.matmul(dst.rearrange("p (h k) -> p h k", h=2), ident16[:],
                          maskb[:, tile % TB].unsqueeze(1).to_broadcast([P, 2, SK]), start=True, stop=False)
                for r, (s, m) in enumerate(PASSES):
                    ins = pe.matmul(dst, qT[s][:, n % 2, pp, j * P:(j + 1) * P], kbd[m][:, b, p],
                                    start=False, stop=(r == 2))
                ins.then_inc(s_full, 1)
            elif ev[0] == "T":
                _, n, t = ev
                k = t_no[ev]
                if k >= 2:
                    pe.wait_ge(t_free, k - 1)
                pe.wait_ge(norm_ready, 2 * n + 1 + (t > 0))
                for j in range(2):
                    if t < 2:
                        for h in range(2):
                            ins = pe.transpose(ps[:, 2 + k % 2, (2 * h + j) * P:(2 * h + j + 1) * P],
                                               prob[:, n % 2, j, 2 * t + h, 0:P], ident[:])
                    else:
                        ins = pe.transpose(ps[0:T4, 2 + k % 2, j * P:(j + 1) * P],
                                           prob_t[:, n % 2, j].rearrange("p h k -> p (h k)"), ident[:])
                ins.then_inc(t_full, 1)
            elif ev[0] == "PV":
                _, n, pp = ev
                g, q = divmod(n, QUADS)
                b, p = 2 * g // TB, 2 * q + pp
                dst = bank(ev)
                pe.wait_ge(t_free, t_no[("T", n, 2)] + 1)
                if n == 0:
                    pe.wait_ge(v_low, 2 * B)
                for r, (s, m) in enumerate(PASSES):
                    for h in range(2):
                        pe.matmul(dst[:, 0:2 * P], vm[s][:, b, p, h * DH:h * DH + P], pT[m][:, n % 2, 2 * pp + h],
                                  start=(r == 0 and h == 0), stop=False)
                    ins = pe.matmul(dst[:, 0:2 * P], vt[s][:, b, q, pp * P:(pp + 1) * P], pT[m][0:T4, n % 2, 4],
                                    start=False, stop=(r == 2))
                ins.then_inc(acc_full, 1)
            elif ev[0] == "Y":
                _, g, j = ev
                dst = bank(ev)
                for p in range(PAIRS):
                    if p >= PAIRS - 2:
                        wait_used(pe, ("PV", QUADS * g + QUADS - 1, p - PAIRS + 2))
                    if g == 0 and p == 0:
                        pe.wait_ge(split_low, 4)
                    for r, (s, m) in enumerate(PASSES):
                        ins = pe.matmul(dst[:, 0:D], oT[s][:, p, j * P:(j + 1) * P], wo[m][:, p],
                                        start=(p == 0 and r == 0), stop=(p == PAIRS - 1 and r == 2))
                ins.then_inc(acc_full, 1)

        pe.wait_ge(acc_free, ATT_END)
        for ev in logits:
            if ev[0] == "seT":
                t = ev[1]
                dst = bank(ev)
                pe.wait_ge(se_ready, 1)
                for k in range(KD):
                    ins = pe.transpose(dst[:, k * P:(k + 1) * P], se[:, t, k * P:(k + 1) * P], ident[:])
                ins.then_inc(acc_full, 1)
            elif ev[0] == "x2T":
                i = ev[1]
                dst = bank(ev)
                pe.wait_ge(x2_ready, i + 1)
                for k in range(KD):
                    ins = pe.transpose(dst[:, k * P:(k + 1) * P], x2f[:, i % 3, k * P:(k + 1) * P], ident[:])
                ins.then_inc(acc_full, 1)
            elif ev[0] == "L":
                i = ev[1]
                wait_used(pe, ("x2T", i))
                if i >= 2:
                    pe.wait_ge(l_ready, i - 1)
                for c in range(2):
                    for r, (s, m) in enumerate(PASSES):
                        for k in range(KD):
                            ins = pe.matmul(ps[:, 2 * (i % 2) + c, :], x2T[s][:, i % 2, k],
                                            seT[m][:, k, c * 512:(c + 1) * 512],
                                            start=(r == 0 and k == 0), stop=(r == 2 and k == KD - 1))
                ins.then_inc(l_full, 1)
        pe.wait_ge(l_ready, TILES)
        for ev in slots:
            if ev[0] == "CM":
                b = ev[1]
                pe.wait_ge(colmax_ready, TB * (b + 1))
                if b:
                    pe.wait_ge(cm_ready, b)
                for t in range(ST):
                    ins = pe.transpose(ps[:, 2 + t // 4, t % 4 * P:(t % 4 + 1) * P], colmax[:, b, t * P:(t + 1) * P],
                                       ident[:])
                ins.then_inc(cm_full, 1)
                pe.wait_ge(cm_diag, b + 1)
                for t in range(ST):
                    ins = pe.matmul(ps[:, t // 4, t % 4 * P:(t % 4 + 1) * P], ones[:], disp_f[:, 1, t],
                                    start=True, stop=True)
                ins.then_inc(cm_bcast, 1)
            elif ev[0] == "E":
                continue
            elif ev[0] == "D":
                n = ev[1]
                b = n // ST
                dst = bank(ev)
                pe.wait_ge(d_low, n + 1)
                if n == 0:
                    pe.wait_ge(x2_low, TILES)
                    pe.wait_ge(const_dve, 2)
                for r, (s, m) in enumerate(PASSES):
                    for i in range(TB):
                        ins = pe.matmul(dst[:, 0:DN], disp[s][:, n % 3, i], x2[m][:, b * TB + i],
                                        start=(r == 0 and i == 0), stop=(r == 2 and i == TB - 1))
                ins.then_inc(acc_full, 1)
            else:
                n = ev[1]
                dst = bank(ev)
                wait_used(pe, ("D", n))
                for k in range(KD):
                    ins = pe.transpose(dst[:, k * P:(k + 1) * P], slot_f[:, n % 2, k * P:(k + 1) * P], ident[:])
                ins.then_inc(acc_full, 1)
        pe.wait_ge(acc_free, SLOTS_END)
        for ev in experts:
            e = ev[1]
            if ev[0] == "GU":
                if e >= 2:
                    pe.wait_ge(hid_ready, e - 1)
                pe.wait_ge(b_low, 1)
                for w in range(2):
                    pe.wait_ge((gate_low, up_low)[w], e + 1)
                    dst = ps[:, 2 * (e % 2) + w, :]
                    pe.matmul(dst, b_pick[:, e], b_row[:, w * F:(w + 1) * F], start=True, stop=False)
                    for r, (s, m) in enumerate(PASSES):
                        for k in range(KD):
                            ins = pe.matmul(dst, sT[s][:, k, e].rearrange("p b s -> p (b s)"), w_gu[m][:, e % 2, w, k],
                                            start=False, stop=(r == 2 and k == KD - 1))
                ins.then_inc(gu_full, 1)
            elif ev[0] == "HT":
                dst = bank(ev)
                pe.wait_ge(hid_ready, e + 1)
                for f in range(FT):
                    ins = pe.transpose(dst[:, f * P:(f + 1) * P], hid[:, e % 2, f * P:(f + 1) * P], ident[:])
                ins.then_inc(acc_full, 1)
            else:
                dst = bank(ev)
                wait_used(pe, ("HT", e))
                pe.wait_ge(down_low, e + 1)
                pe.matmul(dst[:, 0:D], b_pick[:, e], b_row[:, 2 * F:BW], start=True, stop=False)
                for r, (s, m) in enumerate(PASSES):
                    for f in range(FT):
                        ins = pe.matmul(dst[:, 0:D], hT[s][:, e % 2, f], w_d[m][:, e % 2, f],
                                        start=False, stop=(r == 2 and f == FT - 1))
                ins.then_inc(acc_full, 1)
        for ev in combine:
            if ev[0] == "CT":
                _, i, c = ev
                k = 2 * i + c
                pe.wait_ge(c_ready, i + 1)
                if k >= 4:
                    pe.wait_ge(ct_low, k - 3)
                else:
                    pe.wait_ge(hid_ready, E)
                for t in range(4):
                    ins = pe.transpose(ps[:, k % 4, t * P:(t + 1) * P], comb[:, i % 2, (4 * c + t) * P:(4 * c + t + 1) * P],
                                       ident[:])
                ins.then_inc(ct_full, 1)
            elif ev[0] == "CO":
                i = ev[1]
                b = i // TB
                dst = bank(ev)
                pe.wait_ge(ct_low, 2 * i + 2)
                wait_used(pe, ("EO", E - 1))
                for r, (s, m) in enumerate(PASSES):
                    for t in range(ST):
                        ins = pe.matmul(dst[:, 0:D], combT[s][:, i % 2, t], eo[m][:, b, t],
                                        start=(r == 0 and t == 0), stop=(r == 2 and t == ST - 1))
                ins.then_inc(acc_full, 1)

    top.close()


_INS = ['x', 'ctx_1024', 'mask_1x1xSxS2_bk1', 'L0_xattn_Wq', 'L0_xattn_bq', 'L0_xattn_Wk', 'L0_xattn_bk',
        'L0_xattn_Wv', 'L0_xattn_bv', 'L0_xattn_Wo', 'L0_xattn_bo', 'L0_ffn_norm_g', 'L0_ffn_norm_b',
        'L0_ffn_slot_g', 'L0_ffn_slot_b', 'L0_ffn_scale', 'L0_ffn_slot_embeds', 'L0_ffn_Wg', 'L0_ffn_bg',
        'L0_ffn_Wu', 'L0_ffn_bu', 'L0_ffn_Wd', 'L0_ffn_bd']


def kernel(**inputs):
    import numpy as _np
    import concourse.bacc as _bacc
    from concourse import mybir as _mybir
    from concourse.bass_utils import run_bass_kernel_spmd as _run

    nc = _bacc.Bacc("TRN2", target_bir_lowering=False, num_devices=1)
    arrays, io = {}, {}
    for name in _INS:
        a = _np.ascontiguousarray(inputs[name])
        arrays[f"in_{name}_dram"] = a
        io[name] = nc.dram_tensor(f"in_{name}_dram", a.shape, _mybir.dt.from_np(a.dtype), kind="ExternalInput").ap()
    shape = inputs["x"].shape
    slots = inputs["L0_ffn_slot_embeds"].shape
    io["out"] = nc.dram_tensor("out_0_dram", shape, _mybir.dt.float32, kind="ExternalOutput").ap()
    io["logits"] = nc.dram_tensor("logits_dram", (shape[0] * shape[1], slots[0] * slots[1]),
                                  _mybir.dt.float32, kind="Internal").ap()
    program(nc, io)
    r = _run(nc, [arrays], core_ids=[0])
    return r.results[0]["out_0_dram"]
```

```python
from contextlib import ExitStack

import concourse.bass as bass
from concourse import mybir

P = 128
F32 = mybir.dt.float32
F32R = mybir.dt.float32r
BF16 = mybir.dt.bfloat16
U8 = mybir.dt.uint8
ALU = mybir.AluOpType
ACT = mybir.ActivationFunctionType
AX = mybir.AxisListType.X
EPS = 1e-5
MASKED = -1e30

NS, NT, NA = 3, 2, 3
WARM = 16
PROLOGUE = [
    ('K', 0), ('split', 1), ('zeros',), ('K', 2), ('K', 1), ('K', 3), ('K', 4), ('K', 5), ('LN', 0), ('XN', 0),
    ('K', 6), ('K', 7), ('split', 2), ('V', 0, 0, 0), ('xT', 0, 0), ('V', 0, 0, 1), ('xT', 0, 1), ('V', 0, 1, 1),
    ('V', 0, 1, 0), ('mask',), ('Q', 0, 0), ('Q', 0, 1), ('V', 1, 0, 0), ('V', 1, 0, 1), ('V', 1, 1, 1),
    ('V', 1, 1, 0), ('split', 3),
]
STEP = "R1 LN S00 S01 PV0 T0 Q0 R0 PV1 XN Q1 S10 T1 T2 Y0 Y1 S11 xT0 xT1"
LATER_DVE = {'R': 3.5, 'T': 0.5, 'SB': 2, 'SA': 2, 'PV': 1, 'XN': -1}
LATER_ACT = {'S': 3.5, 'Q': 0.5, 'seT': -1, 'T': 0.5}
N2_AT = 20
A_LATE = 2
SLOTS_HEAD = [('H', 0), ('MX', 1, 0), ('H', 1), ('D', 0), ('MX', 1, 1), ('MB', 1, 0)]
LATER_SLOTS_ACT = {('E', 0): 4, ('E', 1): 4, ('E', 2): 4}
LATER_SLOTS_DVE = {'L': 1, 'A': 4}
LATER_SLOTS_POOL = {'E': 1.5}
LATER_EXPERTS_ACT = {'C': 2}
LATER_EXPERTS_DVE = {'HT': -2, 'GU': -1}
STORE_LAG = 3

PASSES = ((0, 0), (1, 0), (0, 1))


def attention_schedule(groups, quads):
    steps = groups * quads
    order = []
    for n in range(steps + 2):
        g, q = divmod(n, quads)
        now, nxt, last, before = n < steps, n + 1 < steps, 1 <= n <= steps, n >= 2
        norm, result = q == 1 and g + 1 < groups, q == 1 and g >= 1
        parts = {"Q0": [("Q", n + 1, 0)] * nxt, "Q1": [("Q", n + 1, 1)] * nxt,
                 "S00": [("S", n, 0, 0)] * now, "S01": [("S", n, 0, 1)] * now,
                 "S10": [("S", n, 1, 0)] * now, "S11": [("S", n, 1, 1)] * now,
                 "R0": [("R", n, 0)] * now, "R1": [("R", n - 1, 1)] * last,
                 "T0": [("T", n - 1, 0)] * last, "T1": [("T", n - 1, 1)] * last, "T2": [("T", n - 1, 2)] * last,
                 "PV0": [("PV", n - 2, 0)] * before, "PV1": [("PV", n - 2, 1)] * before,
                 "LN": [("LN", g + 1)] * norm, "XN": [("XN", g + 1)] * norm,
                 "Y0": [("Y", g - 1, 0)] * result, "Y1": [("Y", g - 1, 1)] * result,
                 "xT0": [("xT", g + 1, 0)] * (q == quads - 2 and g + 1 < groups and now),
                 "xT1": [("xT", g + 1, 1)] * (q == quads - 2 and g + 1 < groups and now)}
        for part in STEP.split():
            order += parts[part]
    return order


def later(order, by):
    at = [i + by.get(ev, by.get(ev[0], 0)) for i, ev in enumerate(order)]
    return [order[i] for i in sorted(range(len(order)), key=lambda i: (at[i], i))]


def program(nc, io):
    x, ctx, mask = io["x"], io["ctx_1024"], io["mask_1x1xSxS2_bk1"]
    Wq, bq, Wk, bk = (io["L0_xattn_" + n] for n in ("Wq", "bq", "Wk", "bk"))
    Wv, bv, Wo, bo = (io["L0_xattn_" + n] for n in ("Wv", "bv", "Wo", "bo"))
    norm_g, norm_b, slot_g, slot_b = (io["L0_ffn_" + n] for n in ("norm_g", "norm_b", "slot_g", "slot_b"))
    scale, slot_embeds = io["L0_ffn_scale"], io["L0_ffn_slot_embeds"]
    Wg, bg, Wu, bu, Wd, bd = (io["L0_ffn_" + n] for n in ("Wg", "bg", "Wu", "bu", "Wd", "bd"))
    out, logits_dram = io["out"], io["logits"]

    B, N, D = x.shape
    SK = ctx.shape[1]
    DM = Wq.shape[1]
    DH = 64
    E, SLOTS, _ = slot_embeds.shape
    F = Wg.shape[2]
    KD = D // P
    TILES = B * N // P
    TB = N // P
    GROUPS = TILES // 2
    PAIRS = DM // P
    QUADS = PAIRS // 2
    TAIL = SK - P
    PK = 2 * SK
    T4 = 4 * TAIL
    ES = E * SLOTS
    ST = ES // P
    FT = F // P
    DN = D + 2
    assert D == 2 * P and DM == 1024 and ES == 1024 and F == 512 and B == 2 and T4 <= P

    prologue = [("cT", k) for k in range(KD)] + [("warm", WARM)] + PROLOGUE
    assert {ev for ev in PROLOGUE if ev[0] in "KV"} == {("K", p) for p in range(PAIRS)} | {
        ("V", b, c, t) for b in range(B) for c in range(2) for t in range(2)}
    attention = attention_schedule(GROUPS, QUADS)
    last_q, last_y = attention.index(("Q", GROUPS * QUADS - 1, 1)), attention.index(("Y", GROUPS - 1, 0))
    tail = attention[last_q + 1:last_y]
    for t in range(ST):
        at = (t + 1) * len(tail) // ST
        tail.insert(min(at + t, len(tail)), ("seT", t))
    head = attention[:last_q + 1]
    norms = [("SA",)] + [("SB", t) for t in range(ST)]
    for k, ev in enumerate(norms):
        head.insert(head.index(("S", GROUPS // B * QUADS + 1 + k, 0, 0)), ev)
    tail = tail[:N2_AT] + [("N2", 0), ("N2", 1), ("N2", 2)] + tail[N2_AT:] + [("x2T", 0)]
    attention = head + tail + attention[last_y:]
    attention_dve = later(attention, LATER_DVE)
    attention_act = later(attention, LATER_ACT)
    logits = []
    for i in range(TILES):
        logits += [("x2T", i + 1)] * (i + 1 < TILES) + [("N2", i + 3)] * (i + 3 < TILES) + [("L", i)]
        logits += [("A", i)] * (i < TILES - A_LATE)
        logits += {TB: [("MX", 0, 0)], TB + 2: [("MB", 0, 0), ("MX", 0, 1)], TB + 4: [("MB", 0, 1)],
                   TB + 5: [("E", 0)], TB + 6: [("E", 1)], TB + 7: [("E", 2)]}.get(i, [])
    slots = list(SLOTS_HEAD)
    for n in range(B * ST):
        slots += [("H", n + 2)] * (n + 2 < B * ST) + [("E", n + 3)] * (n + 3 < B * ST) + [("D", n + 1)] * (n + 1 < B * ST)
        slots += [("A", TILES - A_LATE + n)] * (n < A_LATE)
        slots += [("MB", 1, 1)] * (n == 0) + [("sT", n)]
    experts = [("GU", 0)]
    for e in range(E):
        experts += [("GU", e + 1)] * (e + 1 < E) + [("HT", e)] + [("EO", e - 1)] * (e >= 1)
    experts.remove(("EO", E - 2))
    experts.remove(("HT", E - 1))
    experts += [("C", 0), ("C", 1), ("HT", E - 1), ("EO", E - 2), ("CT", 0, 0), ("CT", 0, 1), ("EO", E - 1)]
    pieces = [(e, w) for e in range(2) for w in range(3)]
    for kind, e, *_ in experts:
        if e + 2 < E and kind == "GU":
            pieces += [(e + 2, 0), (e + 2, 1)]
        elif e + 2 < E and kind == "EO":
            pieces += [(e + 2, 2)]
    piece_no = {piece: i for i, piece in enumerate(pieces)}
    combine = []
    for i in range(TILES):
        combine += [("CT", i + 1, 0), ("CT", i + 1, 1)] * (i + 1 < TILES) + [("C", i + 2)] * (i + 2 < TILES)
        combine += [("CO", i)]

    acc_no, t_no, s_no, high_no, v_no, tail_no = {}, {}, {}, {}, {}, {}
    for ev in prologue + attention + logits + slots + experts + combine:
        if ev[0] in ("cT", "K", "V", "xT", "Q", "PV", "Y", "seT", "x2T", "MX", "MB", "D", "sT", "HT", "EO", "CO"):
            acc_no[ev] = len(acc_no)
        if ev[0] == "T":
            t_no[ev] = len(t_no)
        if ev[0] == "S":
            s_no[ev] = len(s_no)
        if ev[0] == "V":
            v_no[ev] = len(v_no)
            if ev[3] == 1:
                tail_no[ev] = len(tail_no)
        if ev[0] in ("cT", "K", "xT", "Q", "PV", "seT", "x2T", "sT", "HT"):
            high_no[ev] = len(high_no)

    top = ExitStack()
    top.enter_context(nc.allow_non_contiguous_dma(reason="three bias vectors, one value a partition"))

    def sb(stack, name, shape, dt=F32):
        return stack.enter_context(nc.sbuf_tensor(name, shape, dt))

    def halves(stack, name, shape):
        return [sb(stack, name + "_high", shape, F32R), sb(stack, name + "_low", shape, F32R)]

    def sem(name):
        return top.enter_context(nc.semaphore(name))

    ident = sb(top, "ident", [P, P])
    ident16 = sb(top, "ident16", [P, P], BF16)
    ones = sb(top, "ones", [P, P])
    x1 = sb(top, "x1", [P, TILES, D])
    gain = sb(top, "gain", [P, D])
    shift = sb(top, "shift", [P, D])
    eps = sb(top, "eps", [P, 2])
    mhalf = sb(top, "mhalf", [P, ST])
    mv2 = sb(top, "mv2", [P, TILES, 2])
    rstd2 = sb(top, "rstd2", [P, TILES])
    neg_amax = sb(top, "neg_amax", [P, TILES])
    csum = sb(top, "csum", [P, TILES])
    crec = sb(top, "crec", [P, TILES])

    wkq = halves(top, "wkq", [P, KD, DM])
    room = -(-nc.sbuf_base // 32) * 32
    att = ExitStack()
    kbd = sb(att, "kbd", [P, B, 2, PAIRS, PK], F32R)

    def small(name, half, at, shape, dt=F32):
        return nc.alloc_sbuf_tensor_at(name, shape, dt, offset=room + 4 * (half * PAIRS * PK + at))

    bo_b = sb(att, "bo_b", [P, D])
    bq_c = sb(att, "bq_c", [P, PAIRS])
    bk_c = sb(att, "bk_c", [P, PAIRS])
    bv_c = sb(att, "bv_c", [P, PAIRS])
    maskb = sb(att, "maskb", [P, TB, SK], BF16)
    wvo = halves(att, "wvo", [P, 2 * DM])
    wv = [w[:, :].rearrange("p (k n) -> p k n", k=KD) for w in wvo]
    wo = [w[:, :].rearrange("p (k n) -> p k n", k=PAIRS) for w in wvo]
    vm = halves(att, "vm", [P, B, PAIRS, 3 * DH])
    vt = halves(att, "vt", [T4, B, QUADS, 4 * DH])
    xn = sb(att, "xn", [P, 2, D])
    bst = sb(att, "bst", [P, 2, 6])
    bmv = sb(att, "bmv", [P, 2, 2])
    rstd = sb(att, "rstd", [P, 2, 2])
    bst2 = sb(att, "bst2", [P, 6])
    norm2 = sb(att, "norm2", [P, 6, 2])
    nmax = sb(att, "nmax", [P, NS, 2])
    psums = sb(att, "psums", [P, 2, 2, 2, 2])
    prec = sb(att, "prec", [P, 2, 2, 2, 2])
    xT = halves(att, "xT", [P, KD, 2 * P])
    qT = halves(att, "qT", [P, 2, 2, 2 * P])
    expo = sb(att, "expo", [P, 2, 2, 2, 2, SK])
    prob = sb(att, "prob", [P, 2, 2, 4, P])
    prob_t = sb(att, "prob_t", [P, 2, 2, 4, TAIL])
    pro = ExitStack()
    wraw = sb(pro, "wraw", [P, 2, 2 * DM])
    mask_u8 = sb(pro, "mask_u8", [P, TB, SK], U8)
    ctx_main = sb(pro, "ctx_main", [P, B, D])
    ctx_tail = sb(pro, "ctx_tail", [TAIL, B, D])
    cT = halves(pro, "cT", [P, KD, B, SK])
    cT4 = halves(pro, "cT4", [P, KD, B, 4, TAIL])
    v_f = sb(pro, "v_f", [T4, 2, 4 * DH])
    quad_mask = sb(pro, "quad_mask", [T4, 4, DH])
    pro.close()
    loop = ExitStack()
    pT = halves(loop, "pT", [P, 2, 5, 2 * P])
    oT = halves(loop, "oT", [P, PAIRS, 2 * P])
    loop.close()
    att.close()

    ffn = ExitStack()
    sb(ffn, "room", [P, 2 * PAIRS * PK])
    sT = halves(ffn, "sT", [P, KD, E, B, SLOTS])
    lg = ExitStack()
    lsb = sb(lg, "lsb", [P, TILES, ES])
    x2 = halves(lg, "x2", [P, TILES, DN])
    colmax = sb(lg, "colmax", [P, B, ES])
    den = sb(lg, "den", [P, 2])
    nb_b = sb(lg, "nb_b", [P, B, ES])
    nb = sb(lg, "nb", [P, ST])
    diag = sb(lg, "diag", [P, 4, P])
    slot_f = sb(lg, "slot_f", [P, 2, D])
    lg.close()
    seT = wkq
    se = small("se", 0, 0, [P, ST, D])
    sg_b = small("sg_b", 0, ST * D, [P, D])
    at = (ST + 1) * D
    sst = small("sst", 0, at, [P, ST, 6])
    smv = small("smv", 0, at + 6 * ST, [P, ST, 2])
    srs = small("srs", 0, at + 8 * ST, [P, 2, ST])
    sc_b = small("sc_b", 0, at + 10 * ST, [P, 1])
    sb_b = small("sb_b", 1, 0, [P, D])
    x2f = small("x2f", 1, D, [P, 3, D])
    x2T = [small("x2T_high", 1, 4 * D, [P, 2, KD, P], F32R), small("x2T_low", 1, 6 * D, [P, 2, KD, P], F32R)]
    disp_f = [small("disp_f0", 0, 0, [P, TB, P]), small("disp_f1", 0, TB * P, [P, TB, P]),
              colmax[:, 0].rearrange("p (t n) -> p t n", t=TB)]
    disp0 = [small("disp0_high", 1, 0, [P, TB, P], F32R), small("disp0_low", 1, TB * P, [P, TB, P], F32R)]
    disp = [[disp0[s][:]] + [wkq[s][:, k].rearrange("p (t n) -> p t n", t=TB) for k in range(2)] for s in range(2)]
    ex = ExitStack()
    RAW = 6
    w_raw = sb(ex, "w_raw", [P, RAW, 1024])
    BW = 2 * F + D
    b_raw = sb(ex, "b_raw", [E, BW])
    gate = sb(ex, "gate", [P, F])
    eo = halves(ex, "eo", [P, B, ST, D])
    w_gu = halves(ex, "w_gu", [P, 2, 2, KD, F])
    hT = halves(ex, "hT", [P, 2, FT, P])
    lraw = sb(ex, "lraw", [P, 3, ES])
    outb = sb(ex, "outb", [P, 2, D])
    ex.close()
    w_d = [w[:, :, :].rearrange("p r (f d) -> p r f d", f=FT) for w in wkq]
    b_pick = small("b_pick", 0, 0, [32 + E, E, P], F32R)
    b_row = small("b_row", 1, 0, [32 + E, BW], F32R)
    hid = small("hid", 1, BW, [P, 2, F])
    cb = ExitStack()
    combT = halves(cb, "combT", [P, 2, ST, P])
    cb.close()
    ffn.close()

    assert NS + NT + NA == 8 and NA <= 4
    ps = top.enter_context(nc.psum_tensor("ps", [P, 8, 512], F32))

    def acc(no):
        return ps[:, NS + NT + no % NA, :]

    d_ctx, d_bk, d_x, d_small, d_mask, d_gain, d_se = (sem(s) for s in (
        "d_ctx", "d_bk", "d_x", "d_small", "d_mask", "d_gain", "d_se"))
    d_w = [sem(f"d_w{i}") for i in range(4)]
    d_w0 = [sem("d_w0_first"), sem("d_w0_second")]
    d_raw = [sem(f"d_raw{i}") for i in range(RAW)]
    d_bias = sem("d_bias")
    d_lst = sem("d_lst")
    d_lld = [sem(f"d_lld{i}") for i in range(3)]
    d_out = [sem(f"d_out{i}") for i in range(2)]
    const_pool, const_dve, mask_ready = sem("const_pool"), sem("const_dve"), sem("mask_ready")
    zeros_ready, bk_ready = sem("zeros_ready"), sem("bk_ready")
    acc_full, acc_high, acc_free = sem("acc_full"), sem("acc_high"), sem("acc_free")
    split_high, split_low, late_low = sem("split_high"), sem("split_low"), sem("late_low")
    v_ready, v_high, v_low = sem("v_ready"), sem("v_high"), sem("v_low")
    cT4_ready = sem("cT4_ready")
    var_ready, rstd_ready, xn_ready, xbo_ready = sem("var_ready"), sem("rstd_ready"), sem("xn_ready"), sem("xbo_ready")
    s_full, s_max, s_exp = sem("s_full"), sem("s_max"), sem("s_exp")
    recip_ready, norm_ready = sem("recip_ready"), sem("norm_ready")
    t_full, t_high, t_free = sem("t_full"), sem("t_high"), sem("t_free")
    mv2_ready, rstd2_ready = sem("mv2_ready"), sem("rstd2_ready")
    dve_step, pool_step = sem("dve_step"), sem("pool_step")
    se_var, se_rstd, se_ready = sem("se_var"), sem("se_rstd"), sem("se_ready")
    x2_centered, x2_ready, x2_high, x2_low = sem("x2_centered"), sem("x2_ready"), sem("x2_high"), sem("x2_low")
    l_full, l_ready, amax_ready, colmax_ready = sem("l_full"), sem("l_ready"), sem("amax_ready"), sem("colmax_ready")
    diag_ready = sem("diag_ready")
    d_shift, d_exp, d_high, d_low = (sem(s) for s in ("d_shift", "d_exp", "d_high", "d_low"))
    w_high, first_low, gate_low, up_low, down_low, b_high, b_low = (sem(s) for s in (
        "w_high", "first_low", "gate_low", "up_low", "down_low", "b_high", "b_low"))
    gu_full, gate_ready, hid_ready = sem("gu_full"), sem("gate_ready"), sem("hid_ready")
    c_ready, ct_full, ct_high, ct_low, out_ready = (sem(s) for s in (
        "c_ready", "ct_full", "ct_high", "ct_low", "out_ready"))

    ATT_END = acc_no[("Y", GROUPS - 1, 1)] + 1
    SLOTS_END = acc_no[("sT", B * ST - 1)] + 1

    def wait_used(eng, ev):
        eng.wait_ge(acc_free, acc_no[ev] + 1)

    def wait_done(eng, ev):
        eng.wait_ge(acc_full, acc_no[ev] + 1)

    def low_made(e, w):
        if w == 0:
            return (first_low, e + 1) if e < 2 else (gate_low, e - 1)
        return (up_low if w == 1 else down_low), e + 1

    def weight_piece(e, w):
        return [(w_gu[s][:, e % 2, w] if w < 2 else w_d[s][:, e % 2]) for s in range(2)]

    def weight_half(i, c):
        parts = [w[:, :, :] if i % 2 == 0 else w[:, :].rearrange("p (k n) -> p k n", k=KD) for w in (wkq, wvo)[i % 2]]
        parts.append(wraw[:, i % 2].rearrange("p (k n) -> p k n", k=KD))
        return [w[:, :, c * 512:(c + 1) * 512] for w in parts]

    def key_blocks(p, src):
        keys = src[:, 0:B * SK].rearrange("p (b s) -> p b s", b=B)
        return [(slice(0, DH), slice(0, SK), keys[0:DH]), (slice(DH, P), slice(SK, PK), keys[DH:P])]

    def prologue_over(eng):
        eng.wait_ge(late_low, 6)
        eng.wait_ge(v_low, 2 * B)
        eng.wait_ge(mask_ready, 1)
        wait_done(eng, ("V", B - 1, 1, 1))

    block = top.enter_context(nc.Block())

    @block.sync
    def _(sp):
        sp.dma_start(ctx_main[:], ctx[:, 0:P].rearrange("b p d -> p b d")).then_inc(d_ctx, 16)
        sp.dma_start(ctx_tail[:], ctx[:, P:SK].rearrange("b p d -> p b d")).then_inc(d_ctx, 16)
        weights = [w.rearrange("(k p) n -> p k n", p=P) for w in (Wk, Wv, Wq, Wo)]

        def load_weights(i):
            if i >= 2:
                sp.wait_ge(split_high, 2 * (i - 1))
                sp.wait_ge(*((split_low, 2) if i == 2 else (late_low, 2)))
            k = weights[i].shape[1]
            if i == 0:
                for c in range(2):
                    sp.dma_start(weight_half(0, c)[2], weights[0][:, :, c * 512:(c + 1) * 512]).then_inc(d_w0[c], 16)
                return
            sp.dma_start(wraw[:, i % 2].rearrange("p (k n) -> p k n", k=k), weights[i]).then_inc(d_w[i], 16)

        load_weights(0)
        sp.dma_start(bk_c[:], bk.rearrange("(m p) -> p m", p=P)).then_inc(d_bk, 16)
        x_t = x.rearrange("b (t p) d -> p (b t) d", p=P)
        sp.dma_start(x1[:, 0:2], x_t[:, 0:2]).then_inc(d_x, 16)
        load_weights(1)
        load_weights(2)
        sp.dma_start(bq_c[:], bq.rearrange("(m p) -> p m", p=P)).then_inc(d_small, 16)
        sp.dma_start(bv_c[:], bv.rearrange("(m p) -> p m", p=P)).then_inc(d_small, 16)
        sp.dma_start(bo_b[:], bo.unsqueeze(0).to_broadcast([P, D])).then_inc(d_small, 16)
        sp.dma_start(mask_u8[:], mask.rearrange("a b (t p) k -> p (a b t) k", p=P)).then_inc(d_mask, 16)
        sp.dma_start(x1[:, 2:TILES], x_t[:, 2:TILES]).then_inc(d_x, 16)
        load_weights(3)
        sp.dma_start(gain[:], norm_g.unsqueeze(0).to_broadcast([P, D])).then_inc(d_gain, 16)
        sp.dma_start(shift[:], norm_b.unsqueeze(0).to_broadcast([P, D])).then_inc(d_gain, 16)
        sp.wait_ge(s_full, s_no[("S", GROUPS // B * QUADS - 1, 1, 1)] + 1)
        sp.dma_start(se[:], slot_embeds.rearrange("(t e) s d -> (e s) t d", e=P // SLOTS)).then_inc(d_se, 16)
        sp.dma_start(sg_b[:], slot_g.unsqueeze(0).to_broadcast([P, D])).then_inc(d_se, 16)
        sp.dma_start(sb_b[:], slot_b.unsqueeze(0).to_broadcast([P, D])).then_inc(d_se, 16)
        sp.dma_start(sc_b[:], scale.unsqueeze(0).to_broadcast([P, 1])).then_inc(d_se, 16)
        l_t = logits_dram.rearrange("(t p) s -> p t s", p=P)
        for i in range(TILES):
            sp.wait_ge(l_ready, i + 1)
            sp.dma_start(l_t[:, i], lsb[:, i]).then_inc(d_lst, 16)
        sp.wait_ge(d_shift, ST)
        sp.wait_ge(colmax_ready, TB)
        sp.wait_ge(amax_ready, TB)
        sp.wait_ge(d_lst, 16 * TILES)
        for bias, at in ((bg, 0), (bu, F), (bd, 2 * F)):
            sp.dma_start(b_raw[:, at:at + bias.shape[1]], bias).then_inc(d_bias, 16)
        for i, (e, w) in enumerate(pieces):
            if i >= RAW:
                sp.wait_ge(w_high, i - RAW + 1)
                e0, w0 = pieces[i - RAW]
                sp.wait_ge(*low_made(e0, w0))
            view = (Wg, Wu, Wd)[w][e].rearrange("(k p) n -> p k n", p=P)
            sp.dma_start(w_raw[:, i % RAW].rearrange("p (k n) -> p k n", k=view.shape[1]), view)\
                .then_inc(d_raw[i % RAW], 16)
        out_t = out.rearrange("b (t p) d -> p (b t) d", p=P)
        sp.wait_ge(acc_free, SLOTS_END)
        for i in range(TILES + STORE_LAG):
            if i < TILES:
                if i >= 3:
                    sp.wait_ge(ct_full, 2 * (i - 2))
                sp.dma_start(lraw[:, i % 3], l_t[:, i]).then_inc(d_lld[i % 3], 16)
            if i >= STORE_LAG:
                o = i - STORE_LAG
                sp.wait_ge(out_ready, o + 1)
                sp.dma_start(out_t[:, o], outb[:, o % 2]).then_inc(d_out[o % 2], 16)
        for s in d_out:
            sp.wait_ge(s, 16 * TILES // 2)

    @block.gpsimd
    def _(pool):
        steps = [0]

        def link(ins):
            steps[0] += 1
            ins.then_inc(pool_step, 1)
            pool.wait_ge(pool_step, steps[0])

        link(pool.memset(ident[:], 0.0))
        link(pool.affine_select(out=ident[:], in_=ident[:], compare_op=ALU.not_equal, fill=1.0, base=0,
                                pattern=[[-1, P]], channel_multiplier=1))
        pool.tensor_copy(ident16[:], ident[:]).then_inc(const_pool, 1)
        link(pool.memset(quad_mask[:], 1.0))
        link(pool.affine_select(out=quad_mask[:], in_=quad_mask[:], compare_op=ALU.is_ge, fill=0.0, base=0,
                                pattern=[[-TAIL, 4], [0, DH]], channel_multiplier=1))
        pool.affine_select(out=quad_mask[:], in_=quad_mask[:], compare_op=ALU.is_ge, fill=0.0, base=TAIL - 1,
                           pattern=[[TAIL, 4], [0, DH]], channel_multiplier=-1).then_inc(const_pool, 1)
        for s in range(2):
            link(pool.memset(vm[s][:].rearrange("p b q (a d) -> p (b q) a d", a=3)[:, :, 1].bitcast(F32), 0.0))
        link(pool.memset(kbd[0:DH, :, :, :, SK:PK].rearrange("p b s q k -> p (b s q) k").bitcast(F32), 0.0))
        pool.wait_ge(const_dve, 1)

        def step(ev):
            if ev[0] == "zeros":
                pool.wait_ge(late_low, 2)
                link(pool.memset(kbd[DH:P, :, :, :, 0:SK].rearrange("p b s q k -> p (b s q) k").bitcast(F32), 0.0))
                pool.engine_nop().then_inc(zeros_ready, 1)
            elif ev[0] == "split":
                for c in range(2):
                    high, low, raw = weight_half(ev[1], c)
                    pool.wait_ge(split_high, 2 * ev[1] + c + 1)
                    pool.tensor_tensor(low, raw, high, ALU.subtract).then_inc(late_low, 1)
            elif ev[0] == "LN":
                g = ev[1]
                pool.wait_ge(var_ready, g + 1)
                link(pool.tensor_tensor(rstd[:, 0], bmv[:, :, 1], eps[:], ALU.add))
                pool.tensor_tensor(rstd[:, 1], rstd[:, 0], mhalf[:, 0:2], ALU.pow).then_inc(rstd_ready, 1)
            elif ev[0] == "XN":
                g = ev[1]
                if g == 0:
                    pool.wait_ge(d_small, 48)
                pool.wait_ge(xn_ready, g + 1)
                pool.tensor_tensor(x1[:, 2 * g:2 * g + 2], x1[:, 2 * g:2 * g + 2],
                                   bo_b[:].unsqueeze(1).to_broadcast([P, 2, D]), ALU.add).then_inc(xbo_ready, 1)
            elif ev[0] == "R":
                _, n, pp = ev
                pool.wait_ge(recip_ready, 2 * n + pp + 1)
                if n >= 2:
                    pool.wait_ge(t_full, 3 * (n - 2) + 3)
                heads = slice(2 * pp, 2 * pp + 2)
                pool.tensor_tensor(prob[:, n % 2, :, heads, :], expo[:, n % 2, pp, :, :, 0:P],
                                   prec[:, n % 2, pp].unsqueeze(3).to_broadcast([P, 2, 2, P]), ALU.mult)
                pool.tensor_tensor(prob_t[:, n % 2, :, heads, :], expo[:, n % 2, pp, :, :, P:SK],
                                   prec[:, n % 2, pp].unsqueeze(3).to_broadcast([P, 2, 2, TAIL]), ALU.mult)\
                    .then_inc(norm_ready, 1)
            elif ev[0] == "Y" and ev[2] == 1:
                g = ev[1]
                pool.wait_ge(mv2_ready, 2 * g + 2)
                v = mv2[:, 2 * g:2 * g + 2, 1]
                link(pool.tensor_tensor(norm2[:, 0], v, eps[:], ALU.add))
                link(pool.tensor_tensor(norm2[:, 1], norm2[:, 0], mhalf[:, 0:2], ALU.pow))
                link(pool.tensor_tensor(norm2[:, 2], v, norm2[:, 1], ALU.mult))
                link(pool.tensor_tensor(norm2[:, 3], norm2[:, 2], norm2[:, 1], ALU.mult))
                link(pool.tensor_tensor(norm2[:, 4], norm2[:, 3], eps[:], ALU.add))
                link(pool.tensor_tensor(norm2[:, 5], norm2[:, 4], mhalf[:, 0:2], ALU.pow))
                pool.tensor_tensor(rstd2[:, 2 * g:2 * g + 2], norm2[:, 5], norm2[:, 1], ALU.mult)\
                    .then_inc(rstd2_ready, 1)
            elif ev[0] == "SA":
                pool.wait_ge(se_var, 1)
                link(pool.tensor_tensor(srs[:, 0], smv[:, :, 1], eps[:, 0:1].to_broadcast([P, ST]), ALU.add))
                pool.tensor_tensor(srs[:, 1], srs[:, 0], mhalf[:], ALU.pow).then_inc(se_rstd, 1)
            elif ev[0] == "N2":
                i = ev[1]
                pool.wait_ge(x2_centered, i + 1)
                if i == 0:
                    pool.wait_ge(d_gain, 32)
                link(pool.tensor_tensor(x2f[:, i % 3], x2f[:, i % 3], gain[:], ALU.mult))
                pool.tensor_tensor(x2f[:, i % 3], x2f[:, i % 3], shift[:], ALU.add).then_inc(x2_ready, 1)
            elif ev[0] == "x2T":
                i = ev[1]
                pool.wait_ge(x2_high, i + 1)
                pool.tensor_tensor(x2[1][:, i, 0:D], x2f[:, i % 3], x2[0][:, i, 0:D], ALU.subtract).then_inc(x2_low, 1)
            elif ev[0] == "E":
                n = ev[1]
                b, t = divmod(n, ST)
                wait_used(pool, ("MB", b, 1))
                if n < 3:
                    wait_done(pool, ("MX", 0, 1))
                    wait_used(pool, ("seT", ST - 1))
                else:
                    pool.wait_ge(d_low, n - 2)
                pool.tensor_tensor(disp_f[n % 3][:], lsb[:, b * TB:(b + 1) * TB, t * P:(t + 1) * P],
                                   nb_b[:, b, t * P:(t + 1) * P].unsqueeze(1).to_broadcast([P, TB, P]), ALU.add)\
                    .then_inc(d_shift, 1)

        for ev in prologue + attention + later(logits + slots, LATER_SLOTS_POOL):
            step(ev)
        wait_used(pool, ("D", B * ST - 1))
        for e, w in pieces:
            if w == 1 or (w == 0 and e < 2):
                continue
            i = piece_no[e, w]
            pool.wait_ge(w_high, i + 1)
            high, low = weight_piece(e, w)
            pool.tensor_tensor(low, w_raw[:, i % RAW].rearrange("p (k n) -> p k n", k=KD if w == 0 else FT), high,
                               ALU.subtract).then_inc(gate_low if w == 0 else down_low, 1)

    @block.scalar
    def _(act):
        def high_half(ev, dst, src, bias=0.0):
            wait_done(act, ev)
            act.activation(dst, src, ACT.Identity, bias=bias).then_inc(acc_high, 1)

        def split_weights(i):
            if i:
                act.wait_ge(d_w[i], 16)
            if i >= 2:
                wait_done(act, ("K", PAIRS - 1) if i == 2 else ("V", B - 1, 1, 1))
            for c in range(2):
                high, _, raw = weight_half(i, c)
                if i == 0:
                    act.wait_ge(d_w0[c], 16)
                act.activation(high, raw, ACT.Identity, scale=DH ** -0.5 if i == 0 else 1.0).then_inc(split_high, 1)

        def weights_high(e, w):
            i = piece_no[e, w]
            act.wait_ge(d_raw[i % RAW], 16 * (i // RAW + 1))
            if e >= 2:
                act.wait_ge(gu_full, e - 1) if w < 2 else wait_done(act, ("EO", e - 2))
            act.copy(weight_piece(e, w)[0],
                     w_raw[:, i % RAW].rearrange("p (k n) -> p k n", k=KD if w < 2 else FT)).then_inc(w_high, 1)

        split_weights(0)
        act.wait_ge(bk_ready, 1)

        def step(ev):
            no = acc_no.get(ev)
            if ev[0] == "cT":
                high_half(ev, cT[0][:, ev[1]], acc(no)[:, 0:B * SK].rearrange("p (b s) -> p b s", b=B))
            elif ev[0] == "split":
                split_weights(ev[1])
            elif ev[0] == "K":
                p = ev[1]
                wait_done(act, ev)
                for at, cols, src in key_blocks(p, acc(no)):
                    ins = act.activation(kbd[at, :, 0, p, cols], src, ACT.Identity, bias=bk_c[at, p:p + 1])
                ins.then_inc(acc_high, 1)
            elif ev[0] == "V":
                _, b, c, t = ev
                if t == 0:
                    wait_done(act, ev)
                    act.copy(vm[0][:, b, 4 * c:4 * c + 4, :].rearrange("p q (a d) -> p q a d", a=3)[:, :, 0:3:2],
                             acc(no).rearrange("p (q a d) -> p q a d", q=4, a=2)).then_inc(v_high, 1)
                else:
                    act.wait_ge(v_ready, tail_no[ev] + 1)
                    act.copy(vt[0][:, b, 2 * c:2 * c + 2, :], v_f[:]).then_inc(v_high, 1)
            elif ev[0] == "xT":
                high_half(ev, xT[0][:, ev[2]], acc(no)[:, 0:2 * P])
            elif ev[0] == "Q":
                _, n, pp = ev
                p = 2 * (n % QUADS) + pp
                if n == 0:
                    act.wait_ge(d_small, 48)
                high_half(ev, qT[0][:, n % 2, pp], acc(no)[:, 0:2 * P], bq_c[:, p:p + 1])
            elif ev[0] == "S":
                _, n, pp, j = ev
                s = s_no[ev]
                act.wait_ge(s_max, s + 1)
                if n >= 2:
                    act.wait_ge(norm_ready, 2 * (n - 2) + pp + 1)
                for h in range(2):
                    ins = act.activation(expo[:, n % 2, pp, j, h, :], ps[:, s % NS, h * SK:(h + 1) * SK], ACT.Exp,
                                         bias=nmax[:, s % NS, h:h + 1],
                                         accum_out=psums[:, n % 2, pp, j, h:h + 1])
                ins.then_inc(s_exp, 1)
            elif ev[0] == "T":
                _, n, t = ev
                k = t_no[ev]
                act.wait_ge(t_full, k + 1)
                if n == 0:
                    prologue_over(act)
                if n >= 2:
                    wait_done(act, ("PV", n - 2, 1))
                rows, tiles = (P, 2) if t < 2 else (T4, 1)
                act.copy(pT[0][0:rows, n % 2, 2 * t:2 * t + tiles],
                         ps[0:rows, NS + k % NT, 0:tiles * 2 * P].rearrange("p (t n) -> p t n", t=tiles))\
                    .then_inc(t_high, 1)
            elif ev[0] == "PV":
                _, n, pp = ev
                p = 2 * (n % QUADS) + pp
                high_half(ev, oT[0][:, p], acc(no)[:, 0:2 * P], bv_c[:, p:p + 1])
            elif ev[0] == "seT":
                t = ev[1]
                high_half(ev, seT[0][:, :, t * P:(t + 1) * P], acc(no)[:, 0:2 * P].rearrange("p (k s) -> p k s", k=KD))
            elif ev[0] == "x2T":
                i = ev[1]
                high_half(ev, x2T[0][:, i % 2], acc(no)[:, 0:2 * P].rearrange("p (k s) -> p k s", k=KD))
                if i == 0:
                    act.wait_ge(acc_free, ATT_END)
                act.copy(x2[0][:, i, 0:D], x2f[:, i % 3]).then_inc(x2_high, 1)
            elif ev[0] == "L":
                i = ev[1]
                act.wait_ge(l_full, i + 1)
                act.copy(lsb[:, i].rearrange("p (c n) -> p c n", c=2), ps[:, 2 * (i % 2):2 * (i % 2) + 2, :])\
                    .then_inc(l_ready, 1)
            elif ev[0] == "E":
                n = ev[1]
                act.wait_ge(d_shift, n + 1)
                act.activation(disp_f[n % 3][:], disp_f[n % 3][:], ACT.Exp).then_inc(d_exp, 1)
            elif ev[0] == "H":
                n = ev[1]
                if n >= 3:
                    wait_done(act, ("D", n - 3))
                elif n == 0:
                    act.wait_ge(x2_low, TILES)
                else:
                    act.wait_ge(l_full, TILES)
                act.wait_ge(d_exp, n + 1)
                act.copy(disp[0][n % 3], disp_f[n % 3][:]).then_inc(d_high, 1)
            elif ev[0] == "sT":
                b, t = divmod(ev[1], ST)
                wait_done(act, ev)
                for k in range(KD):
                    ins = act.copy(sT[0][:, k, 2 * t:2 * t + 2, b, :],
                                   acc(no)[:, k * P:(k + 1) * P].rearrange("p (e s) -> p e s", e=2))
                ins.then_inc(acc_high, 1)
            elif ev[0] == "GU":
                e = ev[1]
                act.wait_ge(gu_full, e + 1)
                if e >= 1:
                    act.wait_ge(hid_ready, e)
                act.activation(gate[:], ps[:, 2 * (e % 2), :], ACT.Gelu).then_inc(gate_ready, 1)
                if e + 2 < E:
                    weights_high(e + 2, 0)
                    weights_high(e + 2, 1)
            elif ev[0] == "HT":
                e = ev[1]
                high_half(ev, hT[0][:, e % 2].rearrange("p f s -> p (f s)"), acc(no))
            elif ev[0] == "EO" and ev[1] + 2 < E:
                weights_high(ev[1] + 2, 2)
            elif ev[0] == "C":
                i = ev[1]
                act.wait_ge(d_lld[i % 3], 16 * (i // 3 + 1))
                act.activation(lraw[:, i % 3], lraw[:, i % 3], ACT.Exp, bias=neg_amax[:, i:i + 1],
                               accum_out=csum[:, i:i + 1]).then_inc(c_ready, 1)
            elif ev[0] == "CT":
                _, i, c = ev
                k = 2 * i + c
                act.wait_ge(ct_full, k + 1)
                if k == 0:
                    for w in range(3):
                        act.wait_ge(*low_made(E - 1, w))
                    act.wait_ge(w_high, 3 * E)
                if i >= 2:
                    wait_done(act, ("CO", i - 2))
                act.copy(combT[0][:, i % 2, 4 * c:4 * c + 4].rearrange("p t n -> p (t n)"), ps[:, k % 4, :])\
                    .then_inc(ct_high, 1)

        for ev in prologue + attention_act + later(logits + slots, LATER_SLOTS_ACT):
            step(ev)
        wait_done(act, ("D", B * ST - 1))
        act.wait_ge(d_lst, 16 * TILES)
        weights_high(0, 0)
        weights_high(0, 1)
        act.wait_ge(d_bias, 48)
        act.wait_ge(const_dve, 3)
        act.copy(b_row[0:E], b_raw[:]).then_inc(b_high, 1)
        for e, w in pieces[2:6]:
            weights_high(e, w)
        for ev in later(experts, LATER_EXPERTS_ACT) + combine:
            step(ev)

    @block.vector
    def _(dve):
        steps = [0]

        def link(ins):
            steps[0] += 1
            ins.then_inc(dve_step, 1)
            dve.wait_ge(dve_step, steps[0])

        def low_half(ev, dst, src, high, bias=None):
            dve.wait_ge(acc_high, high_no[ev] + 1)
            if bias is None:
                dve.tensor_tensor(dst, src, high, ALU.subtract).then_inc(acc_free, 1)
            else:
                dve.scalar_tensor_tensor(out=dst, in0=src, scalar=bias, in1=high, op0=ALU.add, op1=ALU.subtract)\
                    .then_inc(acc_free, 1)

        dve.memset(eps[:], EPS)
        dve.memset(mhalf[:], -0.5)
        dve.memset(ones[:], 1.0).then_inc(const_dve, 1)

        def weights_low(e):
            for w in ((0, 1) if e < 2 else (1,)):
                i = piece_no[e, w]
                high, low = weight_piece(e, w)
                dve.wait_ge(w_high, i + 1)
                dve.tensor_tensor(low, w_raw[:, i % RAW].rearrange("p (k n) -> p k n", k=KD), high, ALU.subtract)\
                    .then_inc(up_low if w else first_low, 1)

        dve.wait_ge(d_bk, 16)
        dve.tensor_scalar(bk_c[:], bk_c[:], DH ** -0.5, None, ALU.mult).then_inc(bk_ready, 1)
        for c in range(2):
            high, low, raw = weight_half(0, c)
            dve.wait_ge(split_high, c + 1)
            dve.scalar_tensor_tensor(out=low, in0=raw, scalar=DH ** -0.5, in1=high, op0=ALU.mult,
                                     op1=ALU.subtract).then_inc(split_low, 1)
        dve.wait_ge(bk_ready, 1)
        dve.wait_ge(const_pool, 2)

        def step(ev):
            no = acc_no.get(ev)
            if ev[0] == "cT":
                k = ev[1]
                low_half(ev, cT[1][:, k], acc(no)[:, 0:B * SK].rearrange("p (b s) -> p b s", b=B), cT[0][:, k])
                if k == KD - 1:
                    wait_used(dve, ev)
                    for s in range(2):
                        for kk in range(KD):
                            ins = dve.tensor_copy(cT4[s][:, kk],
                                                  cT[s][:, kk, :, P:SK].unsqueeze(2).to_broadcast([P, B, 4, TAIL]))
                    ins.then_inc(cT4_ready, 1)
            elif ev[0] == "mask":
                dve.wait_ge(d_mask, 16)
                dve.tensor_scalar(maskb[:], mask_u8[:], MASKED, None, ALU.mult).then_inc(mask_ready, 1)
            elif ev[0] == "K":
                p = ev[1]
                dve.wait_ge(acc_high, high_no[ev] + 1)
                for at, cols, src in key_blocks(p, acc(no)):
                    ins = dve.scalar_tensor_tensor(out=kbd[at, :, 1, p, cols], in0=src, scalar=bk_c[at, p:p + 1],
                                                   in1=kbd[at, :, 0, p, cols], op0=ALU.add, op1=ALU.subtract)
                ins.then_inc(acc_free, 1)
            elif ev[0] == "V":
                _, b, c, t = ev
                if t == 0:
                    src = acc(no).rearrange("p (q a d) -> p q a d", q=4, a=2)
                    view = [v[:, b, 4 * c:4 * c + 4, :].rearrange("p q (a d) -> p q a d", a=3)[:, :, 0:3:2] for v in vm]
                    dve.wait_ge(v_high, v_no[ev] + 1)
                    dve.tensor_tensor(view[1], src, view[0], ALU.subtract).then_inc(acc_free, 1)
                else:
                    wait_done(dve, ev)
                    if tail_no[ev]:
                        dve.wait_ge(v_low, tail_no[ev])
                    dve.tensor_tensor(v_f[:], acc(no)[0:T4, :].rearrange("p (q n) -> p q n", q=2),
                                      quad_mask[:].rearrange("p a d -> p (a d)").unsqueeze(1).to_broadcast([T4, 2, 4 * DH]),
                                      ALU.mult).then_inc(v_ready, 1)
                    dve.wait_ge(v_high, v_no[ev] + 1)
                    dve.tensor_tensor(vt[1][:, b, 2 * c:2 * c + 2, :], v_f[:], vt[0][:, b, 2 * c:2 * c + 2, :],
                                      ALU.subtract).then_inc(v_low, 1)
                    dve.wait_ge(v_low, tail_no[ev] + 1)
                    dve.engine_nop().then_inc(acc_free, 1)
            elif ev[0] == "LN":
                g = ev[1]
                dve.wait_ge(d_x, 16 if g == 0 else 32)
                for j in range(2):
                    ins = dve.bn_stats(bst[:, j], x1[:, 2 * g + j])
                link(ins)
                for j in range(2):
                    ins = dve.bn_aggr(bmv[:, j], bst[:, j])
                ins.then_inc(var_ready, 1)
            elif ev[0] == "XN":
                g = ev[1]
                dve.wait_ge(rstd_ready, g + 1)
                dve.wait_ge(var_ready, g + 1)
                if g:
                    wait_done(dve, ("xT", g - 1, 1))
                for j in range(2):
                    ins = dve.tensor_scalar(xn[:, j], x1[:, 2 * g + j], bmv[:, j, 0:1], rstd[:, 1, j:j + 1],
                                            ALU.subtract, ALU.mult)
                ins.then_inc(xn_ready, 1)
            elif ev[0] == "xT":
                low_half(ev, xT[1][:, ev[2]], acc(no)[:, 0:2 * P], xT[0][:, ev[2]])
            elif ev[0] == "Q":
                _, n, pp = ev
                p = 2 * (n % QUADS) + pp
                if n == 0:
                    dve.wait_ge(d_small, 48)
                low_half(ev, qT[1][:, n % 2, pp], acc(no)[:, 0:2 * P], qT[0][:, n % 2, pp], bq_c[:, p:p + 1])
            elif ev[0] == "S":
                s = s_no[ev]
                dve.wait_ge(s_full, s + 1)
                dve.tensor_reduce(nmax[:, s % NS], ps[:, s % NS, 0:PK].rearrange("p (h k) -> p h k", h=2), AX, ALU.max,
                                  negate=True).then_inc(s_max, 1)
            elif ev[0] == "R":
                _, n, pp = ev
                dve.wait_ge(s_exp, s_no[("S", n, pp, 1)] + 1)
                if n >= 2:
                    dve.wait_ge(norm_ready, 2 * (n - 2) + pp + 1)
                dve.reciprocal(prec[:, n % 2, pp], psums[:, n % 2, pp]).then_inc(recip_ready, 1)
            elif ev[0] == "T":
                _, n, t = ev
                k = t_no[ev]
                dve.wait_ge(t_high, k + 1)
                if n == 0:
                    prologue_over(dve)
                rows, tiles = (P, 2) if t < 2 else (T4, 1)
                dve.tensor_tensor(pT[1][0:rows, n % 2, 2 * t:2 * t + tiles],
                                  ps[0:rows, NS + k % NT, 0:tiles * 2 * P].rearrange("p (t n) -> p t n", t=tiles),
                                  pT[0][0:rows, n % 2, 2 * t:2 * t + tiles], ALU.subtract).then_inc(t_free, 1)
            elif ev[0] == "PV":
                _, n, pp = ev
                p = 2 * (n % QUADS) + pp
                low_half(ev, oT[1][:, p], acc(no)[:, 0:2 * P], oT[0][:, p], bv_c[:, p:p + 1])
            elif ev[0] == "Y":
                _, g, j = ev
                i = 2 * g + j
                wait_done(dve, ev)
                dve.wait_ge(xbo_ready, g + 1)
                dve.tensor_tensor(x1[:, i], acc(no)[:, 0:D], x1[:, i], ALU.add).then_inc(acc_free, 1)
                wait_used(dve, ev)
                link(dve.bn_stats(bst2[:], x1[:, i]))
                dve.bn_aggr(mv2[:, i], bst2[:]).then_inc(mv2_ready, 1)
            elif ev[0] == "SA":
                dve.wait_ge(d_se, 64)
                for t in range(ST):
                    dve.bn_stats(sst[:, t], se[:, t])
                dve.tensor_scalar(sg_b[:], sg_b[:], sc_b[:], None, ALU.mult)
                link(dve.tensor_scalar(sb_b[:], sb_b[:], sc_b[:], None, ALU.mult))
                for t in range(ST):
                    ins = dve.bn_aggr(smv[:, t], sst[:, t])
                ins.then_inc(se_var, 1)
            elif ev[0] == "SB":
                t = ev[1]
                dve.wait_ge(se_var, 1)
                dve.wait_ge(se_rstd, 1)
                link(dve.scalar_tensor_tensor(out=se[:, t], in0=se[:, t], scalar=smv[:, t, 0:1], in1=sg_b[:],
                                              op0=ALU.subtract, op1=ALU.mult))
                dve.scalar_tensor_tensor(out=se[:, t], in0=se[:, t], scalar=srs[:, 1, t:t + 1], in1=sb_b[:],
                                         op0=ALU.mult, op1=ALU.add).then_inc(se_ready, 1)
            elif ev[0] == "seT":
                t = ev[1]
                cols = slice(t * P, (t + 1) * P)
                low_half(ev, seT[1][:, :, cols], acc(no)[:, 0:2 * P].rearrange("p (k s) -> p k s", k=KD),
                         seT[0][:, :, cols])
            elif ev[0] == "N2":
                i = ev[1]
                dve.wait_ge(rstd2_ready, i // 2 + 1)
                if i >= 3:
                    wait_done(dve, ("x2T", i - 3))
                    dve.wait_ge(x2_high, i - 2)
                    dve.wait_ge(x2_low, i - 2)
                dve.tensor_scalar(x2f[:, i % 3], x1[:, i], mv2[:, i, 0:1], rstd2[:, i:i + 1],
                                  ALU.subtract, ALU.mult).then_inc(x2_centered, 1)
            elif ev[0] == "x2T":
                i = ev[1]
                if i == 1:
                    dve.wait_ge(acc_free, ATT_END)
                    dve.memset(x2[0][:, :, D:D + 1].bitcast(F32), 1.0)
                    dve.memset(x2[0][:, :, D + 1:DN].bitcast(F32), 0.0)
                    dve.memset(x2[1][:, :, D:DN].bitcast(F32), 0.0).then_inc(const_dve, 1)
                low_half(ev, x2T[1][:, i % 2], acc(no)[:, 0:2 * P].rearrange("p (k s) -> p k s", k=KD), x2T[0][:, i % 2])
            elif ev[0] == "L":
                i = ev[1]
                dve.wait_ge(l_ready, i + 1)
                b = i // TB
                if i % TB:
                    dve.wait_ge(colmax_ready, i)
                first = lsb[:, i] if i % TB == 0 else colmax[:, b]
                dve.tensor_tensor(colmax[:, b], first, lsb[:, i], ALU.max).then_inc(colmax_ready, 1)
            elif ev[0] == "A":
                i = ev[1]
                dve.tensor_reduce(neg_amax[:, i:i + 1], lsb[:, i], AX, ALU.max, negate=True).then_inc(amax_ready, 1)
            elif ev[0] == "MX":
                _, b, c = ev
                wait_done(dve, ev)
                if (b, c) != (0, 0):
                    wait_done(dve, ("MB", (2 * b + c - 1) // 2, (c + 1) % 2))
                part_nb = nb[:, 4 * c:4 * c + 4]
                dve.tensor_reduce(part_nb, acc(no).rearrange("p (t n) -> p t n", t=4), AX, ALU.max, negate=True)\
                    .then_inc(acc_free, 1)
                wait_used(dve, ev)
                dve.tensor_tensor(diag[:], ident[:].unsqueeze(1).to_broadcast([P, 4, P]),
                                  part_nb.unsqueeze(2).to_broadcast([P, 4, P]), ALU.mult).then_inc(diag_ready, 1)
            elif ev[0] == "MB":
                _, b, c = ev
                wait_done(dve, ev)
                dve.tensor_copy(nb_b[:, b, c * 512:(c + 1) * 512], acc(no)).then_inc(acc_free, 1)
            elif ev[0] == "H":
                n = ev[1]
                dve.wait_ge(d_high, n + 1)
                if n == 0:
                    dve.wait_ge(l_full, TILES)
                dve.tensor_tensor(disp[1][n % 3], disp_f[n % 3][:], disp[0][n % 3], ALU.subtract).then_inc(d_low, 1)
            elif ev[0] == "D":
                n = ev[1]
                wait_done(dve, ev)
                if n >= 2:
                    wait_done(dve, ("sT", n - 2))
                link(dve.reciprocal(den[:, n % 2:n % 2 + 1], acc(no)[:, D:D + 1]))
                dve.tensor_scalar(slot_f[:, n % 2], acc(no)[:, 0:D], den[:, n % 2:n % 2 + 1], None, ALU.mult)\
                    .then_inc(acc_free, 1)
            elif ev[0] == "sT":
                b, t = divmod(ev[1], ST)
                dve.wait_ge(acc_high, high_no[ev] + 1)
                for k in range(KD):
                    at = (slice(None), k, slice(2 * t, 2 * t + 2), b)
                    ins = dve.tensor_tensor(sT[1][at], acc(no)[:, k * P:(k + 1) * P].rearrange("p (e s) -> p e s", e=2),
                                            sT[0][at], ALU.subtract)
                ins.then_inc(acc_free, 1)
            elif ev[0] == "GU":
                e = ev[1]
                dve.wait_ge(gate_ready, e + 1)
                if e >= 2:
                    wait_done(dve, ("HT", e - 2))
                dve.tensor_tensor(hid[:, e % 2], ps[:, 2 * (e % 2) + 1, :], gate[:], ALU.mult)\
                    .then_inc(hid_ready, 1)
                if e + 2 < E:
                    weights_low(e + 2)
            elif ev[0] == "HT":
                e = ev[1]
                low_half(ev, hT[1][:, e % 2].rearrange("p f s -> p (f s)"), acc(no),
                         hT[0][:, e % 2].rearrange("p f s -> p (f s)"))
            elif ev[0] == "EO":
                e = ev[1]
                wait_done(dve, ev)
                places = [(slice(64 * (e % 2), 64 * (e % 2) + 64), b, e // 2) for b in range(B)]
                for b, at in enumerate(places):
                    ins = dve.tensor_copy(eo[0][at], acc(no)[64 * b:64 * b + 64, 0:D])
                link(ins)
                for b, at in enumerate(places):
                    ins = dve.tensor_tensor(eo[1][at], acc(no)[64 * b:64 * b + 64, 0:D], eo[0][at], ALU.subtract)
                ins.then_inc(acc_free, 1)
            elif ev[0] == "C":
                i = ev[1]
                dve.wait_ge(c_ready, i + 1)
                dve.reciprocal(crec[:, i:i + 1], csum[:, i:i + 1]).then_inc(dve_step, 1)
                steps[0] += 1
            elif ev[0] == "CT":
                _, i, c = ev
                k = 2 * i + c
                dve.wait_ge(ct_high, k + 1)
                at = (slice(None), i % 2, slice(4 * c, 4 * c + 4))
                dve.tensor_tensor(combT[1][at].rearrange("p t n -> p (t n)"), ps[:, k % 4, :],
                                  combT[0][at].rearrange("p t n -> p (t n)"), ALU.subtract).then_inc(ct_low, 1)
            elif ev[0] == "CO":
                i = ev[1]
                no = acc_no[ev]
                wait_done(dve, ev)
                if i >= 2:
                    dve.wait_ge(d_out[i % 2], 16 * (i // 2))
                dve.wait_ge(dve_step, steps[0])
                dve.scalar_tensor_tensor(out=outb[:, i % 2], in0=acc(no)[:, 0:D], scalar=crec[:, i:i + 1],
                                         in1=x1[:, i], op0=ALU.mult, op1=ALU.add).then_inc(out_ready, 1)
                dve.wait_ge(out_ready, i + 1)
                dve.engine_nop().then_inc(acc_free, 1)

        for ev in prologue + attention_dve + later(logits + slots, LATER_SLOTS_DVE):
            step(ev)
        dve.wait_ge(d_lst, 16 * TILES)
        dve.memset(b_row[:].bitcast(F32), 0.0)
        rows = slice(0, 32 + E)
        dve.tensor_tensor(b_pick[:], ident[rows, 0:E].unsqueeze(2).to_broadcast([32 + E, E, P]),
                          ident[rows, 32:32 + E].unsqueeze(2).to_broadcast([32 + E, E, P]), ALU.add)\
            .then_inc(const_dve, 1)
        weights_low(0)
        dve.wait_ge(const_dve, 3)
        dve.wait_ge(b_high, 1)
        dve.tensor_tensor(b_row[32:32 + E], b_raw[:], b_row[0:E], ALU.subtract).then_inc(b_low, 1)
        weights_low(1)
        for ev in later(experts, LATER_EXPERTS_DVE) + combine:
            step(ev)

    @block.tensor
    def _(pe):
        def bank(ev):
            no = acc_no[ev]
            if no >= NA:
                pe.wait_ge(acc_free, no - NA + 1)
            return acc(no)

        pe.wait_ge(const_pool, 1)
        pe.wait_ge(d_ctx, 32)

        def step(ev):
            if ev[0] == "warm":
                for _ in range(ev[1]):
                    pe.matmul(ps[:, 0, :], ident16[:], ident16[:].unsqueeze(1).to_broadcast([P, 4, P]),
                              start=True, stop=True)
            elif ev[0] == "cT":
                dst = bank(ev)
                k = ev[1]
                for b in range(B):
                    pe.transpose(dst[:, b * SK:b * SK + P], ctx_main[:, b, k * P:(k + 1) * P], ident[:])
                    ins = pe.transpose(dst[:, b * SK + P:(b + 1) * SK], ctx_tail[:, b, k * P:(k + 1) * P],
                                       ident[0:TAIL, 0:TAIL])
                ins.then_inc(acc_full, 1)
            elif ev[0] == "K":
                p = ev[1]
                dst = bank(ev)
                if p == 0:
                    wait_used(pe, ("cT", KD - 1))
                pe.wait_ge(split_low, 1 + p // 4)
                for n, (s, m) in enumerate(PASSES):
                    for k in range(KD):
                        ins = pe.matmul(dst[:, 0:B * SK], wkq[s][:, k, p * P:(p + 1) * P],
                                        cT[m][:, k].rearrange("p b s -> p (b s)"),
                                        start=(n == 0 and k == 0), stop=(n == 2 and k == KD - 1))
                ins.then_inc(acc_full, 1)
            elif ev[0] == "V":
                _, b, c, t = ev
                dst = bank(ev)
                pe.wait_ge(split_high, 3 + c)
                if (b, c, t) == (0, 0, 0):
                    pe.wait_ge(cT4_ready, 1)
                rows = P if t == 0 else T4
                for n, (s, m) in enumerate(PASSES):
                    if m == 1:
                        pe.wait_ge(late_low, 1 + c)
                    for k in range(KD):
                        lhs = cT[s][:, k, b, 0:P] if t == 0 else cT4[s][:, k, b].rearrange("p a t -> p (a t)")
                        ins = pe.matmul(dst[0:rows, :], lhs, wv[m][:, k, c * F:(c + 1) * F],
                                        start=(n == 0 and k == 0), stop=(n == 2 and k == KD - 1))
                ins.then_inc(acc_full, 1)
            elif ev[0] == "xT":
                _, g, k = ev
                dst = bank(ev)
                pe.wait_ge(xn_ready, g + 1)
                for j in range(2):
                    ins = pe.transpose(dst[:, j * P:(j + 1) * P], xn[:, j, k * P:(k + 1) * P], ident[:])
                ins.then_inc(acc_full, 1)
            elif ev[0] == "Q":
                _, n, pp = ev
                g, q = divmod(n, QUADS)
                p = 2 * q + pp
                dst = bank(ev)
                wait_used(pe, ("xT", g, 1))
                if n <= QUADS:
                    pe.wait_ge(late_low, 3 + p // 4)
                for r, (s, m) in enumerate(PASSES):
                    for k in range(KD):
                        ins = pe.matmul(dst[:, 0:2 * P], wkq[s][:, k, p * P:(p + 1) * P], xT[m][:, k],
                                        start=(r == 0 and k == 0), stop=(r == 2 and k == KD - 1))
                ins.then_inc(acc_full, 1)
            elif ev[0] == "S":
                _, n, pp, j = ev
                g, q = divmod(n, QUADS)
                s_i, tile = s_no[ev], 2 * g + j
                b, p = tile // TB, 2 * q + pp
                if s_i == 0:
                    pe.wait_ge(mask_ready, 1)
                    wait_used(pe, ("K", PAIRS - 1))
                    pe.wait_ge(zeros_ready, 1)
                if s_i >= NS:
                    pe.wait_ge(s_exp, s_i - NS + 1)
                wait_used(pe, ("Q", n, pp))
                dst = ps[:, s_i % NS, 0:PK]
                pe.matmul(dst.rearrange("p (h k) -> p h k", h=2), ident16[:],
                          maskb[:, tile % TB].unsqueeze(1).to_broadcast([P, 2, SK]), start=True, stop=False)
                for r, (s, m) in enumerate(PASSES):
                    ins = pe.matmul(dst, qT[s][:, n % 2, pp, j * P:(j + 1) * P], kbd[:, b, m, p, :],
                                    start=False, stop=(r == 2))
                ins.then_inc(s_full, 1)
            elif ev[0] == "T":
                _, n, t = ev
                k = t_no[ev]
                if k >= NT:
                    pe.wait_ge(t_free, k - NT + 1)
                pe.wait_ge(norm_ready, 2 * n + 1 + (t > 0))
                for j in range(2):
                    if t < 2:
                        for h in range(2):
                            ins = pe.transpose(ps[:, NS + k % NT, (2 * h + j) * P:(2 * h + j + 1) * P],
                                               prob[:, n % 2, j, 2 * t + h, 0:P], ident[:])
                    else:
                        ins = pe.transpose(ps[0:T4, NS + k % NT, j * P:(j + 1) * P],
                                           prob_t[:, n % 2, j].rearrange("p h k -> p (h k)"), ident[:])
                ins.then_inc(t_full, 1)
            elif ev[0] == "PV":
                _, n, pp = ev
                g, q = divmod(n, QUADS)
                b, p = 2 * g // TB, 2 * q + pp
                dst = bank(ev)
                pe.wait_ge(t_free, t_no[("T", n, 2)] + 1)
                if n == 0:
                    pe.wait_ge(v_low, 2 * B)
                for r, (s, m) in enumerate(PASSES):
                    for h in range(2):
                        pe.matmul(dst[:, 0:2 * P], vm[s][:, b, p, h * DH:h * DH + P], pT[m][:, n % 2, 2 * pp + h],
                                  start=(r == 0 and h == 0), stop=False)
                    ins = pe.matmul(dst[:, 0:2 * P], vt[s][:, b, q, pp * P:(pp + 1) * P], pT[m][0:T4, n % 2, 4],
                                    start=False, stop=(r == 2))
                ins.then_inc(acc_full, 1)
            elif ev[0] == "Y":
                _, g, j = ev
                dst = bank(ev)
                for p in range(PAIRS):
                    if p >= PAIRS - 2:
                        wait_used(pe, ("PV", QUADS * g + QUADS - 1, p - PAIRS + 2))
                    if g == 0 and p == 0:
                        pe.wait_ge(late_low, 6)
                    for r, (s, m) in enumerate(PASSES):
                        ins = pe.matmul(dst[:, 0:D], oT[s][:, p, j * P:(j + 1) * P], wo[m][:, p],
                                        start=(p == 0 and r == 0), stop=(p == PAIRS - 1 and r == 2))
                ins.then_inc(acc_full, 1)

            elif ev[0] == "seT":
                t = ev[1]
                dst = bank(ev)
                pe.wait_ge(se_ready, t + 1)
                for k in range(KD):
                    ins = pe.transpose(dst[:, k * P:(k + 1) * P], se[:, t, k * P:(k + 1) * P], ident[:])
                ins.then_inc(acc_full, 1)
            elif ev[0] == "x2T":
                i = ev[1]
                dst = bank(ev)
                pe.wait_ge(x2_ready, i + 1)
                for k in range(KD):
                    ins = pe.transpose(dst[:, k * P:(k + 1) * P], x2f[:, i % 3, k * P:(k + 1) * P], ident[:])
                ins.then_inc(acc_full, 1)
            elif ev[0] == "L":
                i = ev[1]
                wait_used(pe, ("x2T", i))
                if i >= 2:
                    pe.wait_ge(l_ready, i - 1)
                elif i == 0:
                    pe.wait_ge(s_exp, len(s_no))
                    pe.wait_ge(t_free, len(t_no))
                    wait_used(pe, ("seT", ST - 1))
                for c in range(2):
                    for r, (s, m) in enumerate(PASSES):
                        for k in range(KD):
                            ins = pe.matmul(ps[:, 2 * (i % 2) + c, :], x2T[s][:, i % 2, k],
                                            seT[m][:, k, c * 512:(c + 1) * 512],
                                            start=(r == 0 and k == 0), stop=(r == 2 and k == KD - 1))
                ins.then_inc(l_full, 1)
            elif ev[0] == "MX":
                _, b, c = ev
                dst = bank(ev)
                pe.wait_ge(colmax_ready, TB * (b + 1))
                for t in range(4):
                    ins = pe.transpose(dst[:, t * P:(t + 1) * P], colmax[:, b, (4 * c + t) * P:(4 * c + t + 1) * P],
                                       ident[:])
                ins.then_inc(acc_full, 1)
            elif ev[0] == "MB":
                _, b, c = ev
                dst = bank(ev)
                pe.wait_ge(diag_ready, 2 * b + c + 1)
                pe.matmul(dst, ones[:], diag[:].rearrange("p t n -> p (t n)"), start=True, stop=True)\
                    .then_inc(acc_full, 1)
            elif ev[0] == "D":
                n = ev[1]
                b = n // ST
                dst = bank(ev)
                pe.wait_ge(d_low, n + 1)
                if n == 0:
                    pe.wait_ge(x2_low, TILES)
                    pe.wait_ge(const_dve, 2)
                for r, (s, m) in enumerate(PASSES):
                    for i in range(TB):
                        ins = pe.matmul(dst[:, 0:DN], disp[s][n % 3][:, i], x2[m][:, b * TB + i],
                                        start=(r == 0 and i == 0), stop=(r == 2 and i == TB - 1))
                ins.then_inc(acc_full, 1)
            elif ev[0] == "sT":
                n = ev[1]
                dst = bank(ev)
                wait_used(pe, ("D", n))
                for k in range(KD):
                    ins = pe.transpose(dst[:, k * P:(k + 1) * P], slot_f[:, n % 2, k * P:(k + 1) * P], ident[:])
                ins.then_inc(acc_full, 1)
            elif ev[0] == "GU":
                e = ev[1]
                if e >= 2:
                    pe.wait_ge(hid_ready, e - 1)
                if e == 0:
                    pe.wait_ge(acc_free, SLOTS_END)
                    pe.wait_ge(l_ready, TILES)
                banks = [ps[:, 2 * (e % 2) + w, :] for w in range(2)]
                for w, dst in enumerate(banks):
                    pe.wait_ge(w_high, piece_no[e, w] + 1)
                    for r, (s, m) in enumerate(PASSES):
                        if m == 1:
                            pe.wait_ge(*low_made(e, w))
                        for k in range(KD):
                            pe.matmul(dst, sT[s][:, k, e].rearrange("p b s -> p (b s)"), w_gu[m][:, e % 2, w, k],
                                      start=(r == 0 and k == 0), stop=False)
                if e == 0:
                    pe.wait_ge(b_low, 1)
                for w, dst in enumerate(banks):
                    ins = pe.matmul(dst, b_pick[:, e], b_row[:, w * F:(w + 1) * F], start=False, stop=True)
                ins.then_inc(gu_full, 1)
            elif ev[0] == "HT":
                e = ev[1]
                dst = bank(ev)
                pe.wait_ge(hid_ready, e + 1)
                for f in range(FT):
                    ins = pe.transpose(dst[:, f * P:(f + 1) * P], hid[:, e % 2, f * P:(f + 1) * P], ident[:])
                ins.then_inc(acc_full, 1)
            elif ev[0] == "EO":
                e = ev[1]
                dst = bank(ev)
                wait_used(pe, ("HT", e))
                pe.wait_ge(down_low, e + 1)
                pe.matmul(dst[:, 0:D], b_pick[:, e], b_row[:, 2 * F:BW], start=True, stop=False)
                for r, (s, m) in enumerate(PASSES):
                    for f in range(FT):
                        ins = pe.matmul(dst[:, 0:D], hT[s][:, e % 2, f], w_d[m][:, e % 2, f],
                                        start=False, stop=(r == 2 and f == FT - 1))
                ins.then_inc(acc_full, 1)
            elif ev[0] == "CT":
                _, i, c = ev
                k = 2 * i + c
                pe.wait_ge(c_ready, i + 1)
                if k >= 4:
                    pe.wait_ge(ct_low, k - 3)
                else:
                    pe.wait_ge(hid_ready, E)
                for t in range(4):
                    ins = pe.transpose(ps[:, k % 4, t * P:(t + 1) * P], lraw[:, i % 3, (4 * c + t) * P:(4 * c + t + 1) * P],
                                       ident[:])
                ins.then_inc(ct_full, 1)
            elif ev[0] == "CO":
                i = ev[1]
                b = i // TB
                dst = bank(ev)
                pe.wait_ge(ct_low, 2 * i + 2)
                wait_used(pe, ("EO", E - 1))
                for r, (s, m) in enumerate(PASSES):
                    for t in range(ST):
                        ins = pe.matmul(dst[:, 0:D], combT[s][:, i % 2, t], eo[m][:, b, t],
                                        start=(r == 0 and t == 0), stop=(r == 2 and t == ST - 1))
                ins.then_inc(acc_full, 1)

        for ev in prologue + attention + logits + slots + experts + combine:
            step(ev)

    top.close()


_INS = ['x', 'ctx_1024', 'mask_1x1xSxS2_bk1', 'L0_xattn_Wq', 'L0_xattn_bq', 'L0_xattn_Wk', 'L0_xattn_bk',
        'L0_xattn_Wv', 'L0_xattn_bv', 'L0_xattn_Wo', 'L0_xattn_bo', 'L0_ffn_norm_g', 'L0_ffn_norm_b',
        'L0_ffn_slot_g', 'L0_ffn_slot_b', 'L0_ffn_scale', 'L0_ffn_slot_embeds', 'L0_ffn_Wg', 'L0_ffn_bg',
        'L0_ffn_Wu', 'L0_ffn_bu', 'L0_ffn_Wd', 'L0_ffn_bd']


def kernel(**inputs):
    import numpy as _np
    import concourse.bacc as _bacc
    from concourse import mybir as _mybir
    from concourse.bass_utils import run_bass_kernel_spmd as _run

    nc = _bacc.Bacc("TRN2", target_bir_lowering=False, num_devices=1)
    arrays, io = {}, {}
    for name in _INS:
        a = _np.ascontiguousarray(inputs[name])
        arrays[f"in_{name}_dram"] = a
        io[name] = nc.dram_tensor(f"in_{name}_dram", a.shape, _mybir.dt.from_np(a.dtype), kind="ExternalInput").ap()
    shape = inputs["x"].shape
    slots = inputs["L0_ffn_slot_embeds"].shape
    io["out"] = nc.dram_tensor("out_0_dram", shape, _mybir.dt.float32, kind="ExternalOutput").ap()
    io["logits"] = nc.dram_tensor("logits_dram", (shape[0] * shape[1], slots[0] * slots[1]),
                                  _mybir.dt.float32, kind="Internal").ap()
    program(nc, io)
    r = _run(nc, [arrays], core_ids=[0])
    return r.results[0]["out_0_dram"]
```
